# Optimizing a Trainium2 kernel written in Bass

```python
import numpy as np
import jax
import jax.numpy as jnp

def _softmax(x, axis=-1):
    return jax.nn.softmax(x, axis=axis)

def _gelu(x):
    return jax.nn.gelu(x, approximate=True)

def _silu(x):
    return jax.nn.silu(x)

def _sigmoid(x):
    return jax.nn.sigmoid(x)

def _layernorm(x, axis=-1, eps=1e-05):
    m = jnp.mean(x, axis=axis, keepdims=True)
    v = jnp.var(x, axis=axis, keepdims=True)
    return (x - m) / jnp.sqrt(v + eps)

def _scatter_add(tgt, idx, src, axis=0):
    return tgt.at[idx].add(src)

def _segment_sum(src, seg, n):
    return jax.ops.segment_sum(src, seg, n)
kernel_name = 'mk_vit_tower_d2_tok_img512_r4_921aa7'

def setup_inputs(seed: int=0):
    np.random.seed(seed)
    _w = jnp.asarray

    def _rec_inputs():
        import jax
        import jax.numpy as jnp
        _rk = jax.random.key(seed)
        x = -0.000147625 + 0.999875 * jax.random.normal(jax.random.fold_in(_rk, 1), (64, 3, 224, 224), jnp.float32)
        return x
    x = _rec_inputs()

    def _L0_tok_setup():
        import jax, jax.numpy as jnp
        import numpy as np
        N_PATCHES = 8
        PATCH = 28
        C = 3
        IN_D = C * PATCH * PATCH
        HID = 128
        SEQ = N_PATCHES * N_PATCHES + 1

        def _positional_embedding(seq_len, dim):
            i = np.arange(seq_len)[:, None].astype(np.float32)
            j = np.arange(dim)[None, :].astype(np.float32)
            ang = i / np.power(100000.0, j / dim)
            pe = np.where(j % 2 == 0, np.sin(ang), np.cos(ang))
            return jnp.asarray(pe, dtype=jnp.float32)
        key = jax.random.key(seed)
        k1, k2, k3, k4 = jax.random.split(key, 4)
        B = 64
        X = jax.random.normal(k1, (B, C, 224, 224), dtype=jnp.float32)
        bound = 1.0 / np.sqrt(IN_D)
        W = jax.random.uniform(k2, (HID, IN_D), minval=-bound, maxval=bound, dtype=jnp.float32)
        b = jax.random.uniform(k3, (HID,), minval=-bound, maxval=bound, dtype=jnp.float32)
        class_token = jax.random.uniform(k4, (1, HID), dtype=jnp.float32)
        pos_embed = _positional_embedding(SEQ, HID)
        return {'X': X, 'W': W, 'b': b, 'class_token': class_token, 'pos_embed': pos_embed}
    _L0_tok_all = _L0_tok_setup()
    _L0_tok_in = {k: v for k, v in _L0_tok_all.items() if k in ('W', 'b', 'class_token', 'pos_embed')}
    del _L0_tok_all

    def _L0_attn_setup():
        import jax, jax.numpy as jnp
        import numpy as np
        T, BATCH, DIM = (512, 32, 128)

        def _layernorm(y, gamma, beta, eps=1e-05):
            mu = jnp.mean(y, axis=-1, keepdims=True)
            var = jnp.mean(jnp.square(y - mu), axis=-1, keepdims=True)
            return (y - mu) * jax.lax.rsqrt(var + eps) * gamma + beta
        key = jax.random.key(seed)
        ks = jax.random.split(key, 9)
        s = 1.0 / np.sqrt(DIM)
        return {'x': jax.random.normal(ks[0], (T, BATCH, DIM), dtype=jnp.float32), 'W_in': jax.random.uniform(ks[1], (2 * DIM, DIM), jnp.float32, -s, s), 'b_in': jax.random.uniform(ks[2], (2 * DIM,), jnp.float32, -s, s), 'W_out': jax.random.uniform(ks[3], (DIM, DIM), jnp.float32, -s, s), 'b_out': jax.random.uniform(ks[4], (DIM,), jnp.float32, -s, s), 'A': jax.random.normal(ks[5], (DIM,), dtype=jnp.float32) * 0.1, 'B': jax.random.normal(ks[6], (DIM,), dtype=jnp.float32) * 0.1, 'gamma': jnp.ones((DIM,), dtype=jnp.float32), 'beta': jnp.zeros((DIM,), dtype=jnp.float32)}
    _L0_attn_all = _L0_attn_setup()
    _L0_attn_in = {k: v for k, v in _L0_attn_all.items() if k in ('W_in', 'b_in', 'W_out', 'b_out', 'A', 'B', 'gamma', 'beta')}
    del _L0_attn_all

    def _L0_ffn_setup():
        import jax, jax.numpy as jnp
        import numpy as np
        TOP_K = 2
        key = jax.random.key(seed)
        ks = jax.random.split(key, 4)
        b, t, d, e, h = (2, 512, 128, 8, 256)
        scale = 0.02
        return {'x': jax.random.normal(ks[0], (b, t, d), dtype=jnp.float32), 'router_w': jax.random.normal(ks[1], (e, d), dtype=jnp.float32) * scale, 'router_b': jnp.zeros((e,), dtype=jnp.float32), 'fc1_w': jax.random.normal(ks[2], (e, 2 * h, d), dtype=jnp.float32) * scale, 'fc1_b': jnp.zeros((e, 2 * h), dtype=jnp.float32), 'fc2_w': jax.random.normal(ks[3], (e, d, h), dtype=jnp.float32) * scale, 'fc2_b': jnp.zeros((e, d), dtype=jnp.float32)}
    _L0_ffn_all = _L0_ffn_setup()
    _L0_ffn_in = {k: v for k, v in _L0_ffn_all.items() if k in ('router_w', 'router_b', 'fc1_w', 'fc1_b', 'fc2_w', 'fc2_b')}
    del _L0_ffn_all

    def _L1_attn_setup():
        import jax, jax.numpy as jnp
        import numpy as np
        N_HEADS = 8

        def log_sparse_plus_neighbors_mask(seq_len: int, k: int) -> jnp.ndarray:
            i = np.arange(seq_len)[:, None]
            j = np.arange(seq_len)[None, :]
            d = i - j
            pow2 = (d > 0) & (d & d - 1 == 0)
            m = (d == 0) | (d >= 1) & (d <= k) | pow2
            return jnp.asarray(m)
        key = jax.random.key(seed)
        ks = jax.random.split(key, 9)
        bs, S, D = (4, 512, 128)
        s = 0.02
        return {'x': jax.random.normal(ks[0], (bs, S, D), jnp.float32), 'W_Q': jax.random.normal(ks[1], (D, D), jnp.float32) * s, 'b_Q': jnp.zeros((D,), jnp.float32), 'W_K': jax.random.normal(ks[2], (D, D), jnp.float32) * s, 'b_K': jnp.zeros((D,), jnp.float32), 'W_V': jax.random.normal(ks[3], (D, D), jnp.float32) * s, 'b_V': jnp.zeros((D,), jnp.float32), 'W_O': jax.random.normal(ks[4], (D, D), jnp.float32) * s, 'b_O': jnp.zeros((D,), jnp.float32)}
    _L1_attn_all = _L1_attn_setup()
    _L1_attn_in = {k: v for k, v in _L1_attn_all.items() if k in ('W_Q', 'b_Q', 'W_K', 'b_K', 'W_V', 'b_V', 'W_O', 'b_O')}
    del _L1_attn_all

    def _L1_ffn_setup():
        import jax, jax.numpy as jnp
        import numpy as np
        B, S, D, H, E = (4, 512, 128, 8, 8)
        FF = 4 * D
        HD = D // H
        EPS = 1e-05

        def _layernorm(x, g, b):
            mu = jnp.mean(x, axis=-1, keepdims=True)
            var = jnp.mean((x - mu) ** 2, axis=-1, keepdims=True)
            return (x - mu) * jax.lax.rsqrt(var + EPS) * g + b
        key = jax.random.key(seed)
        ks = jax.random.split(key, 16)
        s = 0.02
        return {'x': jax.random.normal(ks[0], (B, S, D), dtype=jnp.float32), 'ln1_g': jnp.ones((D,), jnp.float32), 'ln1_b': jnp.zeros((D,), jnp.float32), 'Wq': jax.random.normal(ks[1], (D, D), jnp.float32) * s, 'bq': jnp.zeros((D,), jnp.float32), 'Wk': jax.random.normal(ks[2], (D, D), jnp.float32) * s, 'bk': jnp.zeros((D,), jnp.float32), 'Wv': jax.random.normal(ks[3], (D, D), jnp.float32) * s, 'bv': jnp.zeros((D,), jnp.float32), 'Wo': jax.random.normal(ks[4], (D, D), jnp.float32) * s, 'bo': jnp.zeros((D,), jnp.float32), 'gate_W': jax.random.normal(ks[5], (D, E), jnp.float32) * s, 'gate_b': jnp.zeros((E,), jnp.float32), 'W1': jax.random.normal(ks[6], (E, D, FF), jnp.float32) * s, 'b1': jnp.zeros((E, FF), jnp.float32), 'W2': jax.random.normal(ks[7], (E, FF, D), jnp.float32) * s, 'b2': jnp.zeros((E, D), jnp.float32)}
    _L1_ffn_all = _L1_ffn_setup()
    _L1_ffn_in = {k: v for k, v in _L1_ffn_all.items() if k in ('ln1_g', 'ln1_b', 'Wq', 'bq', 'Wk', 'bk', 'Wv', 'bv', 'Wo', 'bo', 'gate_W', 'gate_b', 'W1', 'b1', 'W2', 'b2')}
    del _L1_ffn_all
    return {'x': x, 'L0_tok_W': _L0_tok_in['W'], 'L0_tok_b': _L0_tok_in['b'], 'L0_tok_class_token': _L0_tok_in['class_token'], 'L0_tok_pos_embed': _L0_tok_in['pos_embed'], 'L0_attn_W_in': _L0_attn_in['W_in'], 'L0_attn_b_in': _L0_attn_in['b_in'], 'L0_attn_W_out': _L0_attn_in['W_out'], 'L0_attn_b_out': _L0_attn_in['b_out'], 'L0_attn_A': _L0_attn_in['A'], 'L0_attn_B': _L0_attn_in['B'], 'L0_attn_gamma': _L0_attn_in['gamma'], 'L0_attn_beta': _L0_attn_in['beta'], 'L0_ffn_router_w': _L0_ffn_in['router_w'], 'L0_ffn_router_b': _L0_ffn_in['router_b'], 'L0_ffn_fc1_w': _L0_ffn_in['fc1_w'], 'L0_ffn_fc1_b': _L0_ffn_in['fc1_b'], 'L0_ffn_fc2_w': _L0_ffn_in['fc2_w'], 'L0_ffn_fc2_b': _L0_ffn_in['fc2_b'], 'L1_attn_W_Q': _L1_attn_in['W_Q'], 'L1_attn_b_Q': _L1_attn_in['b_Q'], 'L1_attn_W_K': _L1_attn_in['W_K'], 'L1_attn_b_K': _L1_attn_in['b_K'], 'L1_attn_W_V': _L1_attn_in['W_V'], 'L1_attn_b_V': _L1_attn_in['b_V'], 'L1_attn_W_O': _L1_attn_in['W_O'], 'L1_attn_b_O': _L1_attn_in['b_O'], 'L1_ffn_ln1_g': _L1_ffn_in['ln1_g'], 'L1_ffn_ln1_b': _L1_ffn_in['ln1_b'], 'L1_ffn_Wq': _L1_ffn_in['Wq'], 'L1_ffn_bq': _L1_ffn_in['bq'], 'L1_ffn_Wk': _L1_ffn_in['Wk'], 'L1_ffn_bk': _L1_ffn_in['bk'], 'L1_ffn_Wv': _L1_ffn_in['Wv'], 'L1_ffn_bv': _L1_ffn_in['bv'], 'L1_ffn_Wo': _L1_ffn_in['Wo'], 'L1_ffn_bo': _L1_ffn_in['bo'], 'L1_ffn_gate_W': _L1_ffn_in['gate_W'], 'L1_ffn_gate_b': _L1_ffn_in['gate_b'], 'L1_ffn_W1': _L1_ffn_in['W1'], 'L1_ffn_b1': _L1_ffn_in['b1'], 'L1_ffn_W2': _L1_ffn_in['W2'], 'L1_ffn_b2': _L1_ffn_in['b2']}

def reference(x, L0_tok_W, L0_tok_b, L0_tok_class_token, L0_tok_pos_embed, L0_attn_W_in, L0_attn_b_in, L0_attn_W_out, L0_attn_b_out, L0_attn_A, L0_attn_B, L0_attn_gamma, L0_attn_beta, L0_ffn_router_w, L0_ffn_router_b, L0_ffn_fc1_w, L0_ffn_fc1_b, L0_ffn_fc2_w, L0_ffn_fc2_b, L1_attn_W_Q, L1_attn_b_Q, L1_attn_W_K, L1_attn_b_K, L1_attn_W_V, L1_attn_b_V, L1_attn_W_O, L1_attn_b_O, L1_ffn_ln1_g, L1_ffn_ln1_b, L1_ffn_Wq, L1_ffn_bq, L1_ffn_Wk, L1_ffn_bk, L1_ffn_Wv, L1_ffn_bv, L1_ffn_Wo, L1_ffn_bo, L1_ffn_gate_W, L1_ffn_gate_b, L1_ffn_W1, L1_ffn_b1, L1_ffn_W2, L1_ffn_b2):
    import jax
    import jax.numpy as jnp

    def _L0_tok_ref(X, W, b, class_token, pos_embed):
        import jax, jax.numpy as jnp
        import numpy as np
        N_PATCHES = 8
        PATCH = 28
        C = 3
        IN_D = C * PATCH * PATCH
        HID = 128
        SEQ = N_PATCHES * N_PATCHES + 1

        def _positional_embedding(seq_len, dim):
            i = np.arange(seq_len)[:, None].astype(np.float32)
            j = np.arange(dim)[None, :].astype(np.float32)
            ang = i / np.power(100000.0, j / dim)
            pe = np.where(j % 2 == 0, np.sin(ang), np.cos(ang))
            return jnp.asarray(pe, dtype=jnp.float32)
        B = X.shape[0]
        patches = X.reshape(B, C, N_PATCHES, PATCH, N_PATCHES, PATCH)
        patches = patches.transpose(0, 2, 4, 1, 3, 5).reshape(B, N_PATCHES * N_PATCHES, IN_D)
        tokens = jnp.einsum('bpi,hi->bph', patches, W) + b
        cls = jnp.broadcast_to(class_token[None, :, :], (B, 1, HID))
        tokens = jnp.concatenate([cls, tokens], axis=1)
        return tokens * pos_embed[None, :, :]

    def _L0_attn_ref(x, W_in, b_in, W_out, b_out, A, B, gamma, beta):
        import jax, jax.numpy as jnp
        import numpy as np
        T, BATCH, DIM = (512, 32, 128)

        def _layernorm(y, gamma, beta, eps=1e-05):
            mu = jnp.mean(y, axis=-1, keepdims=True)
            var = jnp.mean(jnp.square(y - mu), axis=-1, keepdims=True)
            return (y - mu) * jax.lax.rsqrt(var + eps) * gamma + beta
        zg = jnp.einsum('tbd,ed->tbe', x, W_in) + b_in
        z, g = jnp.split(zg, 2, axis=-1)
        g = jax.nn.sigmoid(g)
        Bz = B * z
        gA = g * A

        def step(prev, inp):
            ga_t, bz_t = inp
            curr = ga_t * prev + bz_t
            return (curr, curr)
        h0 = jnp.zeros((x.shape[1], x.shape[2]), dtype=x.dtype)
        _, h = jax.lax.scan(step, h0, (gA, Bz))
        out = jnp.einsum('tbd,ed->tbe', h, W_out) + b_out
        return _layernorm(x + out, gamma, beta)

    def _L0_ffn_ref(x, router_w, router_b, fc1_w, fc1_b, fc2_w, fc2_b):
        import jax, jax.numpy as jnp
        import numpy as np
        TOP_K = 2
        n_experts = router_w.shape[0]
        temp = 1.0
        logits = (jnp.einsum('btd,ed->bte', x, router_w) + router_b) / temp
        topk_val, topk_idx = jax.lax.top_k(logits, TOP_K)
        weights = jax.nn.softmax(topk_val, axis=-1)
        onehot = jax.nn.one_hot(topk_idx, n_experts, dtype=x.dtype)
        cw = jnp.einsum('btk,btke->bte', weights, onehot)
        h = jnp.einsum('btd,efd->btef', x, fc1_w) + fc1_b
        h1, h2 = jnp.split(h, 2, axis=-1)
        a = jax.nn.silu(h1) * h2
        y = jnp.einsum('bteh,edh->bted', a, fc2_w) + fc2_b
        out = jnp.einsum('bted,bte->btd', y, cw)
        return out

    def _L1_attn_ref(x, W_Q, b_Q, W_K, b_K, W_V, b_V, W_O, b_O):
        import jax, jax.numpy as jnp
        import numpy as np
        N_HEADS = 8

        def log_sparse_plus_neighbors_mask(seq_len: int, k: int) -> jnp.ndarray:
            i = np.arange(seq_len)[:, None]
            j = np.arange(seq_len)[None, :]
            d = i - j
            pow2 = (d > 0) & (d & d - 1 == 0)
            m = (d == 0) | (d >= 1) & (d <= k) | pow2
            return jnp.asarray(m)
        bs, S, D = x.shape
        h = N_HEADS
        dk = D // h
        q = (x @ W_Q + b_Q).reshape(bs, S, h, dk).transpose(0, 2, 1, 3)
        k = (x @ W_K + b_K).reshape(bs, S, h, dk).transpose(0, 2, 1, 3)
        v = (x @ W_V + b_V).reshape(bs, S, h, dk).transpose(0, 2, 1, 3)
        mask = log_sparse_plus_neighbors_mask(S, S // 2)
        scores = jnp.einsum('bhqd,bhkd->bhqk', q, k) / jnp.sqrt(jnp.asarray(dk, x.dtype))
        scores = jnp.where(mask, scores, -jnp.inf)
        p_attn = jax.nn.softmax(scores, axis=-1)
        out = jnp.einsum('bhqk,bhkd->bhqd', p_attn, v)
        out = out.transpose(0, 2, 1, 3).reshape(bs, S, D)
        return out @ W_O + b_O

    def _L1_ffn_ref(x, ln1_g, ln1_b, Wq, bq, Wk, bk, Wv, bv, Wo, bo, gate_W, gate_b, W1, b1, W2, b2):
        import jax, jax.numpy as jnp
        import numpy as np
        B, S, D, H, E = (4, 512, 128, 8, 8)
        FF = 4 * D
        HD = D // H
        EPS = 1e-05

        def _layernorm(x, g, b):
            mu = jnp.mean(x, axis=-1, keepdims=True)
            var = jnp.mean((x - mu) ** 2, axis=-1, keepdims=True)
            return (x - mu) * jax.lax.rsqrt(var + EPS) * g + b
        b, s, d = x.shape
        q = (x @ Wq + bq).reshape(b, s, H, HD)
        k = (x @ Wk + bk).reshape(b, s, H, HD)
        v = (x @ Wv + bv).reshape(b, s, H, HD)
        scores = jnp.einsum('bqhd,bkhd->bhqk', q, k) / jnp.sqrt(jnp.float32(HD))
        attn = jax.nn.softmax(scores, axis=-1)
        o = jnp.einsum('bhqk,bkhd->bqhd', attn, v).reshape(b, s, d) @ Wo + bo
        h = _layernorm(x + o, ln1_g, ln1_b)
        t = h.reshape(b * s, d)
        probs = jax.nn.softmax(t @ gate_W + gate_b, axis=-1)
        idx = jnp.argmax(probs, axis=-1)
        gw = jnp.max(probs, axis=-1)
        hid = jax.nn.gelu(jnp.einsum('nd,edf->enf', t, W1) + b1[:, None, :])
        out_all = jnp.einsum('enf,efd->end', hid, W2) + b2[:, None, :]
        onehot = jax.nn.one_hot(idx, E, dtype=t.dtype)
        out = jnp.einsum('ne,end->nd', onehot, out_all)
        out = out * gw[:, None]
        return out.reshape(b, s, d)
    h = _L0_tok_ref(x, L0_tok_W, L0_tok_b, L0_tok_class_token, L0_tok_pos_embed)
    h = h + _L0_attn_ref(_layernorm(h, axis=-1), L0_attn_W_in, L0_attn_b_in, L0_attn_W_out, L0_attn_b_out, L0_attn_A, L0_attn_B, L0_attn_gamma, L0_attn_beta)
    h = h + _L0_ffn_ref(_layernorm(h, axis=-1), L0_ffn_router_w, L0_ffn_router_b, L0_ffn_fc1_w, L0_ffn_fc1_b, L0_ffn_fc2_w, L0_ffn_fc2_b)
    h = h + _L1_attn_ref(_layernorm(h, axis=-1), L1_attn_W_Q, L1_attn_b_Q, L1_attn_W_K, L1_attn_b_K, L1_attn_W_V, L1_attn_b_V, L1_attn_W_O, L1_attn_b_O)
    h = h + _L1_ffn_ref(_layernorm(h, axis=-1), L1_ffn_ln1_g, L1_ffn_ln1_b, L1_ffn_Wq, L1_ffn_bq, L1_ffn_Wk, L1_ffn_bk, L1_ffn_Wv, L1_ffn_bv, L1_ffn_Wo, L1_ffn_bo, L1_ffn_gate_W, L1_ffn_gate_b, L1_ffn_W1, L1_ffn_b1, L1_ffn_W2, L1_ffn_b2)
    return h

_drawn_inputs = setup_inputs


def setup_inputs(seed=0):
    import zlib

    import numpy as np

    out = dict(_drawn_inputs(seed))
    spreads = {'L0_attn_gamma': (1.0, 0.2),
     'L0_attn_beta': (0.0, 0.1),
     'L0_ffn_router_b': (0.0, 0.344),
     'L0_ffn_fc1_b': (0.0, 0.8),
     'L0_ffn_fc2_b': (0.0, 0.1),
     'L1_attn_b_Q': (0.0, 0.8),
     'L1_attn_b_K': (0.0, 0.8),
     'L1_attn_b_V': (0.0, 0.57),
     'L1_attn_b_O': (0.0, 0.1),
     'L1_ffn_ln1_g': (1.0, 0.6),
     'L1_ffn_ln1_b': (0.0, 0.8),
     'L1_ffn_bq': (0.0, 0.8),
     'L1_ffn_bk': (0.0, 0.8),
     'L1_ffn_bv': (0.0, 0.8),
     'L1_ffn_bo': (0.0, 0.8),
     'L1_ffn_gate_b': (0.0, 0.8),
     'L1_ffn_b1': (0.0, 0.8),
     'L1_ffn_b2': (0.0, 0.66)}
    factors = {'L0_attn_b_in': 8.0,
     'L0_attn_A': 8.0,
     'L0_ffn_fc1_w': 8.0,
     'L0_ffn_fc2_w': 8.0,
     'L1_attn_W_Q': 8.0,
     'L1_attn_W_K': 8.0,
     'L1_attn_W_V': 5.859,
     'L1_attn_W_O': 3.299,
     'L1_ffn_Wq': 8.0,
     'L1_ffn_Wk': 8.0,
     'L1_ffn_Wv': 8.0,
     'L1_ffn_Wo': 8.0,
     'L1_ffn_gate_W': 4.379,
     'L1_ffn_W1': 8.0,
     'L1_ffn_W2': 7.947}
    for name, (base, spread) in spreads.items():
        noise = np.random.default_rng([zlib.crc32(name.encode()), seed]).standard_normal(out[name].shape)
        drawn = base * np.exp(spread * noise) if base else spread * noise
        out[name] = jnp.asarray(drawn.astype(out[name].dtype))
    for name, factor in factors.items():
        out[name] = (out[name] * factor).astype(out[name].dtype)
    return out
```

```python
from contextlib import ExitStack

import concourse.bass as bass
from concourse import mybir

F32 = mybir.dt.float32
BF16 = mybir.dt.bfloat16
ALU = mybir.AluOpType
ACT = mybir.ActivationFunctionType
AX = mybir.AxisListType

D = 128
B = 64
S = 65
NP = S - 1
GI = 8
G = B // GI
GT = GI * S
TP = 104
T = GT // TP
NT = G * T
KF = 18
KR = 48
H = 8
DK = D // H
HA = DK + 1
E = 8
NB = 10
BT = 4
BN = BT * TP
HALF = GI // 2 * S
EPS = 1e-5
SHRINK = 7
SPLIT = ((0, 3 * TP), (3 * TP, 2 * TP))
PARTS = ((0, 6), (6, 12), (12, 18))

C_TOKB, C_CLS, C_BZ, C_BG, C_B, C_A = range(6)
C_ATT = 6
C_HEAD = 12
NCOL = C_HEAD + H
R_BOUT, R_GAMMA, R_BETA, R_BO0, R_BO1, R_G1, R_B1 = range(7)
NROW = 7
M_Z, M_G, M_OUT, M_ATT = 0, 1, 2, 3
NMAT = 11


def after(eng, sem, value):
    if isinstance(value, int) and value <= 0:
        return
    eng.wait_ge(sem, value)


def build_program(nc, d):
    ctx = ExitStack()
    with ctx:
        def sb(name, shape, dt=F32):
            return ctx.enter_context(nc.sbuf_tensor(name, shape, dt))

        def sem(name):
            return ctx.enter_context(nc.semaphore(name))

        ps = ctx.enter_context(nc.psum_tensor("ps", [128, 8, 512], F32))

        h_tok = sb("h_tok", [TP, NT, D])
        xfT = sb("xfT", [D, NT, TP])
        mats = sb("mats", [D, NMAT, D])
        cols = sb("cols", [D, NCOL])
        rows = sb("rows", [TP, NROW, D])
        route_w = sb("route_w", [D, 2, E])
        route_b = sb("route_b", [TP, 2, E])
        bias2 = sb("bias2", [E, 2, D])
        ident = sb("ident", [128, 128])
        identb = sb("identb", [128, 128], BF16)
        halves = sb("halves", [TP, T])
        posT = sb("posT", [D, S])
        maskf = sb("maskf", [S, HALF])
        maskb = sb("maskb", [S, HALF], BF16)
        ids = sb("ids", [TP, E])
        logits = sb("logits", [TP, NT, E])
        cw = sb("cw", [TP, NT, E])
        arena = sb("arena", [128, 2 * (KF + 1) * 512])
        xs = arena[:, :].rearrange("p (b c n) -> p b c n", b=2, c=KF + 1)
        wp = sb("wp", [128, KF + 1, D])

        def carve(start, parts, shape):
            n = 1
            for x in shape:
                n *= x
            ap = arena[0:parts, start:start + n]
            names = "abcd"[:len(shape)]
            if len(shape) > 1:
                ap = ap.rearrange(f"p ({' '.join(names)}) -> p {' '.join(names)}",
                                  **dict(zip(names, shape)))
            return ap, start + n

        at = 0
        keysM, at = carve(at, D, (2, GI, H, S))
        qT, at = carve(at, D, (2, GT))
        vals, at = carve(at, S, (2, GI, H, HA))
        outT, at = carve(at, D, (2, GT))
        keysT, at = carve(at, D, (GT,))
        diff, at = carve(at, S, (2, H, S))
        prob, at = carve(at, S, (2, H, S))
        probT, at = carve(at, S, (2, H, S))
        at = 0
        w1, at = carve(at, 128, (2, 4 * D))
        w2, at = carve(at, 128, (2, 4, D))
        b1, at = carve(at, 128, (2, 4))
        act_a, at = carve(at, 128, (4, BN))
        act_b, at = carve(at, 128, (2, BN))
        at = 0
        rt = []
        for _ in range(6):
            r, at = carve(at, TP, (NT, E))
            rt.append(r)
        rv = []
        for _ in range(8):
            r, at = carve(at, TP, (NT,))
            rv.append(r)

        tokT = sb("tokT", [D, GI, S])
        xn = sb("xn", [TP, 2, T, D])
        xT = sb("xT", [D, GT])
        norm_tiles = [(sb(f"stats{k}", [TP, T, 6]), sb(f"mv{k}", [TP, T, 2]), sb(f"spread{k}", [TP, T]),
                       sb(f"rstd{k}", [TP, T])) for k in range(2)]
        gate = sb("gate", [D, GT])
        ga = sb("ga", [D, GT])
        bz = sb("bz", [D, GT])
        carried = sb("carried", [D, S])
        state = sb("state", [D, GI, S])
        xb = sb("xb", [TP, T, D])
        hb = sb("hb", [TP, T, D])
        y = sb("y", [TP, T, D])
        xf = sb("xf", [TP, T, D])
        tT = sb("tT", [D, GT])
        peak = sb("peak", [S, 2, H])
        rden = sb("rden", [S, H])
        o_tok = sb("o_tok", [S, 2, D])
        largest, shrunk, limit, limit2, eps_shrunk, eps_shrunk2, in_range, kept = (
            sb(n, [TP, T]) for n in ("largest", "shrunk", "limit", "limit2", "eps_shrunk", "eps_shrunk2",
                                     "in_range", "kept"))
        cws = sb("cws", [TP, T, E])
        cwT = sb("cwT", [E, GT])

        def tok_psum(bank, n=T):
            return ps[0:TP, bank:bank + 2, :].rearrange("p a n -> p (a n)")[:, 0:n * D]\
                .rearrange("p (t d) -> p t d", d=D)

        def tok_tile(bank, t):
            return ps[0:TP, bank + t // 4, t % 4 * D:(t % 4 + 1) * D]

        def feat_tile(bank, t):
            k = t // 3
            return ps[:, bank + k, (t - 3 * k) * TP:(t - 3 * k + 1) * TP]

        s_in = sem("constants_loaded")
        s_const = sem("class_token_ready")
        s_made = sem("identity_made")
        s_stood = sem("stood")
        phase_done = sem("phase_done")
        loads = []

        def load(dst, src):
            loads.append((dst, src))

        load(wp[:, 0:KF, :], d["wp"])
        load(wp[0:KR, KF, :], d["wpr"])
        load(cols[:, :], d["cols"])
        load(posT[:, :], d["posT"])
        load(mats[:, :, :], d["mats"])
        load(rows[:, :, :], d["rows"])
        load(route_w[:, :, :], d["route_w"])
        load(route_b[:, :, :], d["route_b"])
        load(bias2[:, :, :], d["bias2"])
        load(maskf[:, :], d["mask"])
        load(ids[:, :], d["ids"])

        x_in = [[sem(f"x_in{p}{k}") for k in range(len(PARTS))] for p in range(2)]
        names = ("patch_mm patch_read tok_turned h_saved norm_ready norm_turned normT_ready zg_mm gate_ready "
                 "bz_ready carry_ready state_ready out_mm xb_ready hb_ready out_read y_ready scaled_ready h_ready "
                 "xf_ready xf_turned xfT_ready xfT_kept logit_mm logit_ready stats_ready mean_ready "
                 "spread_ready rstd_ready shrink_step").split()
        p1 = {n: sem("p1_" + n) for n in names}
        p1["tiles"] = norm_tiles[0]

        def stand(eng, sem_, value):
            eng.wait_ge(sem_, value)
            eng.sem_inc(s_stood, 1)

        def norm_stats(dve, q, src, count):
            stats, mv = q["tiles"][0:2]
            for t in range(T):
                last = dve.bn_stats(stats[:, t, :], src[:, t, :])
            last.then_inc(q["stats_ready"], 1)
            stand(dve, q["stats_ready"], count)
            for t in range(T):
                last = dve.bn_aggr(mv[:, t, :], stats[:, t, :])
            last.then_inc(q["mean_ready"], 1)

        def norm_spread(pool, q, count, eps=None):
            _, mv, spread, rstd = q["tiles"]
            stand(pool, q["mean_ready"], count)
            if eps is None:
                ins = pool.tensor_scalar(spread[:, :], mv[:, :, 1], EPS, None, ALU.add)
            else:
                ins = pool.tensor_tensor(spread[:, :], mv[:, :, 1], eps[:, :], ALU.add)
            ins.then_inc(q["spread_ready"], 1)
            pool.wait_ge(q["spread_ready"], count)
            pool.tensor_tensor(rstd[:, :], spread[:, :], halves[:, :], ALU.pow).then_inc(q["rstd_ready"], 1)

        def norm_apply(dve, q, dst, src, count, r=None):
            _, mv, _, rstd = q["tiles"]
            if r is None:
                dve.wait_ge(q["rstd_ready"], count)
            else:
                rstd = r
            for t in range(T):
                last = dve.tensor_scalar(dst[:, t, :], src[:, t, :], mv[:, t, 0:1], rstd[:, t:t + 1],
                                         ALU.subtract, ALU.mult)
            return last

        def steps(eng, emit, first, inner, last):
            for i in range(first[0], first[1]):
                emit(i, i % 2)
            a = first[1]
            with eng.Fori(0, inner // 2) as k:
                for j in range(2):
                    emit(2 * k + (a + j), (a + j) % 2)
            for i in range(a + inner, last):
                emit(i, i % 2)

        def has(i, lo, hi):
            return not isinstance(i, int) or lo <= i < hi

        P1_FIRST, P1_INNER, P1_LAST = (0, 4), 4, 10

        def p1_sync(sp):
            def emit(g):
                par = g % 2
                if g >= 2:
                    sp.wait_ge(p1["patch_mm"], g - 1)
                for k, (a, b) in enumerate(PARTS):
                    sp.dma_start(xs[:, par, a:b, :], d["xa"][g, :, a:b, :]).then_inc(x_in[par][k], 16)
                sp.dma_start(xs[0:KR, par, KF, :], d["xr"][g]).then_inc(x_in[par][2], 16)
            emit(0)
            emit(1)
            with sp.Fori(0, 3) as k:
                for par in range(2):
                    g = 2 * k + (2 + par)
                    sp.wait_ge(p1["patch_mm"], g - 1)
                    for n, (a, b) in enumerate(PARTS):
                        sp.dma_start(xs[:, par, a:b, :], d["xa"][g, :, a:b, :]).then_inc(x_in[par][n], 16)
                    sp.dma_start(xs[0:KR, par, KF, :], d["xr"][g]).then_inc(x_in[par][2], 16)

        def p1_tensor(pe):
            q = p1

            def turn_tokens(g):
                pe.wait_ge(q["patch_read"], g + 1)
                after(pe, q["out_read"], g)
                for t in range(T):
                    last = pe.transpose(tok_tile(2, t), tokT[:, :, :].rearrange("p a s -> p (a s)")[:, t * TP:(t + 1) * TP],
                                        ident[:, :])
                last.then_inc(q["tok_turned"], 1)

            def turn_norm(g):
                pe.wait_ge(q["norm_ready"], g + 1)
                after(pe, q["xfT_kept"], g)
                for t in range(T):
                    last = pe.transpose(feat_tile(4, t), xn[:, 0, t, :], ident[0:TP, 0:TP])
                last.then_inc(q["norm_turned"], 1)

            def project(g):
                pe.wait_ge(q["normT_ready"], g + 1)
                pe.wait_ge(q["h_saved"], g + 1)
                for m, bank in ((M_Z, 2), (M_G, 4)):
                    for k, (o, n) in enumerate(SPLIT):
                        last = pe.matmul(ps[:, bank + k, 0:n], mats[:, m, :], xT[:, o:o + n], start=True, stop=True)
                last.then_inc(q["zg_mm"], 1)

            def project_out(g):
                pe.wait_ge(q["state_ready"], GI * g + GI)
                for t in range(T):
                    last = pe.matmul(tok_tile(2, t), state[:, :, :].rearrange("p a s -> p (a s)")[:, t * TP:(t + 1) * TP],
                                     mats[:, M_OUT, :], start=True, stop=True)
                last.then_inc(q["out_mm"], 1)

            def turn_router(g):
                pe.wait_ge(q["xf_ready"], g + 1)
                pe.wait_ge(q["gate_ready"], g + 1)
                for t in range(T):
                    last = pe.transpose(feat_tile(4, t), xf[:, t, :], ident[0:TP, 0:TP])
                last.then_inc(q["xf_turned"], 1)

            def router(g):
                pe.wait_ge(q["xfT_ready"], g + 1)
                after(pe, q["logit_ready"], g)
                for t in range(T):
                    last = pe.matmul(ps[0:TP, 6, t * E:(t + 1) * E], tT[:, t * TP:(t + 1) * TP], route_w[:, 0, :],
                                     start=True, stop=True)
                last.then_inc(q["logit_mm"], 1)

            def emit(i, par):
                use = i // 2 + 1 if isinstance(i, int) else None
                full = has(i, 0, G)

                def chunks(a, b):
                    for c in range(a, b):
                        rows_n = 128 if c < KF else KR
                        last = pe.matmul(ps[:, par, :], wp[0:rows_n, c, :], xs[0:rows_n, par, c, :],
                                         start=(c == 0), stop=(c == KF))
                    return last

                def loaded(k):
                    per = 32 if k == 2 else 16
                    if use is not None:
                        pe.wait_ge(x_in[par][k], per * use)
                    else:
                        pe.wait_ge(x_in[par][k], (i - par) * (per // 2) + per)

                if full:
                    after(pe, q["patch_read"], i - 1)
                    loaded(0)
                    chunks(0, 1)
                if has(i, 1, G + 1):
                    turn_tokens(i - 1)
                if has(i, 2, G + 2):
                    turn_router(i - 2)
                if full:
                    chunks(1, 4)
                if has(i, 2, G + 2):
                    router(i - 2)
                if full:
                    chunks(4, 6)
                    loaded(1)
                    chunks(6, 7)
                if has(i, 1, G + 1):
                    turn_norm(i - 1)
                if full:
                    chunks(7, 9)
                if has(i, 1, G + 1):
                    project(i - 1)
                if full:
                    chunks(9, 12)
                    loaded(2)
                    chunks(12, 17)
                if has(i, 1, G + 1):
                    project_out(i - 1)
                if full:
                    chunks(17, 19).then_inc(q["patch_mm"], 1)

            steps(pe, emit, P1_FIRST, P1_INNER, P1_LAST)

        def p1_scalar(act):
            q = p1

            def emit(i, par):
                if has(i, 1, G + 1):
                    g = i - 1
                    act.wait_ge(q["tok_turned"], g + 1)
                    act.activation(h_tok[:, bass.ts(g, T), :], tok_psum(2), ACT.Copy).then_inc(q["h_saved"], 1)
                if has(i, 2, G + 2):
                    g = i - 2
                    act.wait_ge(q["xf_turned"], g + 1)
                    after(act, q["logit_mm"], g)
                    for k, (o, n) in enumerate(SPLIT):
                        last = act.activation(tT[:, o:o + n], ps[:, 4 + k, 0:n], ACT.Copy)
                    last.then_inc(q["xfT_ready"], 1)
                    keep = xfT[:, bass.ts(g, T), :]
                    for k, (o, n) in enumerate(SPLIT):
                        last = act.activation(keep[:, o // TP:(o + n) // TP, :],
                                              ps[:, 4 + k, 0:n].rearrange("p (t n) -> p t n", n=TP), ACT.Copy)
                    last.then_inc(q["xfT_kept"], 1)
                if has(i, 1, G + 1):
                    g = i - 1
                    act.wait_ge(q["norm_turned"], g + 1)
                    after(act, q["zg_mm"], g)
                    for k, (o, n) in enumerate(SPLIT):
                        last = act.activation(xT[:, o:o + n], ps[:, 4 + k, 0:n], ACT.Copy)
                    last.then_inc(q["normT_ready"], 1)
                    act.wait_ge(q["zg_mm"], g + 1)
                    after(act, q["bz_ready"], g)
                    for k, (o, n) in enumerate(SPLIT):
                        last = act.activation(gate[:, o:o + n], ps[:, 4 + k, 0:n], ACT.Sigmoid,
                                              bias=cols[:, C_BG:C_BG + 1])
                    last.then_inc(q["gate_ready"], 1)

            steps(act, emit, P1_FIRST, P1_INNER, P1_LAST)

        def shrink(dve, g):
            q = p1
            n = SHRINK * g

            def then(ins, k):
                ins.then_inc(q["shrink_step"], 1)
                dve.wait_ge(q["shrink_step"], n + k)

            then(dve.tensor_reduce(largest[:, :], y[:, :, :], AX.X, ALU.max, apply_absolute_value=True), 1)
            then(dve.tensor_scalar(largest[:, :], largest[:, :], 1.0, None, ALU.max), 2)
            then(dve.reciprocal(shrunk[:, :], largest[:, :]), 3)
            dve.tensor_tensor(y[:, :, :], y[:, :, :], shrunk[:, :].unsqueeze(2).broadcast_to([TP, T, D]), ALU.mult)
            dve.tensor_scalar(limit[:, :], shrunk[:, :], 2.0 ** 64, 1e12, ALU.mult, ALU.min)
            then(dve.scalar_tensor_tensor(out=eps_shrunk[:, :], in0=shrunk[:, :], scalar=EPS, in1=shrunk[:, :],
                                          op0=ALU.mult, op1=ALU.mult), 4)
            dve.tensor_tensor(limit2[:, :], limit[:, :], limit[:, :], ALU.mult)
            then(dve.tensor_scalar(eps_shrunk2[:, :], eps_shrunk[:, :], 1e-30, None, ALU.max), 5)

        def judge(dve, g):
            q = p1
            mv, rstd = norm_tiles[0][1], norm_tiles[0][3]
            n = SHRINK * g
            dve.wait_ge(q["rstd_ready"], 3 * g + 2)
            dve.scalar_tensor_tensor(out=in_range[:, :], in0=mv[:, :, 1], scalar=float(D), in1=limit2[:, :],
                                     op0=ALU.mult, op1=ALU.is_lt).then_inc(q["shrink_step"], 1)
            dve.wait_ge(q["shrink_step"], n + 6)
            dve.tensor_tensor(kept[:, :], rstd[:, :], in_range[:, :], ALU.mult).then_inc(q["shrink_step"], 1)
            dve.wait_ge(q["shrink_step"], n + SHRINK)

        def p1_vector(dve):
            q = p1

            def emit(i, par):
                if has(i, 1, G + 1):
                    g = i - 1
                    ht = h_tok[:, bass.ts(g, T), :]
                    stand(dve, q["h_saved"], g + 1)
                    norm_stats(dve, q, ht, 3 * g + 1)
                    after(dve, q["norm_turned"], g)
                    after(dve, q["xb_ready"], g)
                    norm_apply(dve, q, xn[:, 0], ht, 3 * g + 1).then_inc(q["norm_ready"], 1)
                if has(i, 2, G + 2):
                    g = i - 2
                    dve.wait_ge(q["logit_mm"], g + 1)
                    dve.tensor_tensor(logits[:, bass.ts(g, T), :],
                                      ps[0:TP, 6, 0:T * E].rearrange("p (t e) -> p t e", e=E),
                                      route_b[:, 0:1, :].broadcast_to([TP, T, E]), ALU.add)\
                       .then_inc(q["logit_ready"], 1)
                if has(i, 1, G + 1):
                    g = i - 1
                    dve.wait_ge(q["zg_mm"], g + 1)
                    for k, (o, n) in enumerate(SPLIT):
                        dve.tensor_scalar(bz[:, o:o + n], ps[:, 2 + k, 0:n], cols[:, C_BZ:C_BZ + 1],
                                          cols[:, C_B:C_B + 1], ALU.add, ALU.mult)
                    dve.wait_ge(q["gate_ready"], g + 1)
                    dve.tensor_scalar(ga[:, :], gate[:, :], cols[:, C_A:C_A + 1], None, ALU.mult)\
                       .then_inc(q["bz_ready"], 1)
                    dve.wait_ge(q["bz_ready"], g + 1)
                    after(dve, q["out_mm"], g)
                    for b in range(GI):
                        prev = state[:, (b - 1) % GI, :]
                        if b:
                            dve.wait_ge(q["state_ready"], GI * g + b)
                        dve.tensor_tensor(carried[:, :], ga[:, b * S:(b + 1) * S], prev, ALU.mult)\
                           .then_inc(q["carry_ready"], 1)
                        dve.wait_ge(q["carry_ready"], GI * g + b + 1)
                        dve.tensor_tensor(state[:, b, :], carried[:, :], bz[:, b * S:(b + 1) * S], ALU.add)\
                           .then_inc(q["state_ready"], 1)
                    dve.wait_ge(q["out_mm"], g + 1)
                    dve.wait_ge(q["xb_ready"], g + 1)
                    dve.tensor_tensor(y[:, :, :], tok_psum(2), xb[:, :, :], ALU.add).then_inc(q["out_read"], 1)
                    dve.wait_ge(q["out_read"], g + 1)
                    shrink(dve, g)
                    norm_stats(dve, q, y, 3 * g + 2)
                    judge(dve, g)
                    after(dve, q["xf_turned"], g)
                    norm_apply(dve, q, xf, y, 3 * g + 2, r=kept).then_inc(q["y_ready"], 1)
                    dve.wait_ge(q["y_ready"], g + 1)
                    dve.tensor_tensor(y[:, :, :], xf[:, :, :],
                                      rows[:, R_GAMMA:R_GAMMA + 1, :].broadcast_to([TP, T, D]), ALU.mult)\
                       .then_inc(q["scaled_ready"], 1)
                    dve.wait_ge(q["scaled_ready"], g + 1)
                    dve.wait_ge(q["hb_ready"], g + 1)
                    ht = h_tok[:, bass.ts(g, T), :]
                    dve.tensor_tensor(ht, y[:, :, :], hb[:, :, :], ALU.add).then_inc(q["h_ready"], 1)
                    stand(dve, q["h_ready"], g + 1)
                    norm_stats(dve, q, ht, 3 * g + 3)
                    norm_apply(dve, q, xf, ht, 3 * g + 3).then_inc(q["xf_ready"], 1)
                if has(i, 0, G):
                    g = i
                    dve.wait_ge(q["patch_mm"], g + 1)
                    after(dve, q["tok_turned"], g)
                    dve.scalar_tensor_tensor(out=tokT[:, :, 1:S],
                                             in0=ps[:, par, :].rearrange("p (a s) -> p a s", s=NP),
                                             scalar=cols[:, C_TOKB:C_TOKB + 1],
                                             in1=posT[:, 1:S].unsqueeze(1).broadcast_to([D, GI, NP]),
                                             op0=ALU.add, op1=ALU.mult).then_inc(q["patch_read"], 1)

            dve.wait_ge(s_in, 16 * len(loads))
            dve.memset(state[:, :, :], 0.0)
            dve.tensor_copy(maskb[:, :], maskf[:, :])
            dve.tensor_tensor(tokT[:, 0, 0:1], cols[:, C_CLS:C_CLS + 1], posT[:, 0:1], ALU.mult).then_inc(s_const, 1)
            dve.wait_ge(s_const, 1)
            dve.tensor_copy(tokT[:, 1:GI, 0:1], tokT[:, 0:1, 0:1].broadcast_to([D, GI - 1, 1])).then_inc(s_const, 1)
            dve.wait_ge(s_const, 2)
            steps(dve, emit, P1_FIRST, P1_INNER, P1_LAST)

        def p1_gpsimd(pool):
            q = p1

            def emit(i, par):
                if has(i, 1, G + 1):
                    g = i - 1
                    norm_spread(pool, q, 3 * g + 1)
                    pool.wait_ge(q["norm_ready"], g + 1)
                    after(pool, q["out_read"], g)
                    pool.tensor_tensor(xb[:, :, :], xn[:, 0], rows[:, R_BOUT:R_BOUT + 1, :].broadcast_to([TP, T, D]),
                                       ALU.add).then_inc(q["xb_ready"], 1)
                    after(pool, q["h_ready"], g)
                    pool.tensor_tensor(hb[:, :, :], h_tok[:, bass.ts(g, T), :],
                                       rows[:, R_BETA:R_BETA + 1, :].broadcast_to([TP, T, D]),
                                       ALU.add).then_inc(q["hb_ready"], 1)
                    norm_spread(pool, q, 3 * g + 2, eps_shrunk2)
                    norm_spread(pool, q, 3 * g + 3)

            steps(pool, emit, P1_FIRST, P1_INNER, P1_LAST)

        rs = [{n: sem(f"route{k}_{n}") for n in ("step", "gap", "exp", "weights")} for k in range(2)]

        def route_vector(dve, layer):
            q = rs[layer]
            count = [0]

            def then(ins):
                count[0] += 1
                ins.then_inc(q["step"], 1)
                dve.wait_ge(q["step"], count[0])

            def wide(v):
                return v[:, :].unsqueeze(2).broadcast_to([TP, NT, E])

            idw = ids[:, :].unsqueeze(1).broadcast_to([TP, NT, E])
            BIG = 64.0

            def pick(of, top, out, first):
                then(dve.tensor_reduce(top[:, :], of[:, :, :], AX.X, ALU.max))
                then(dve.tensor_tensor(rt[0], of[:, :, :], wide(top), ALU.is_equal))
                then(dve.scalar_tensor_tensor(out=rt[1], in0=rt[0], scalar=-BIG, in1=idw, op0=ALU.mult, op1=ALU.add))
                then(dve.tensor_reduce(first[:, :], rt[1], AX.X, ALU.min))
                then(dve.tensor_tensor(out, rt[1], wide(first), ALU.is_equal))

            pick(logits, rv[0], rt[2], rv[1])
            if layer == 0:
                then(dve.scalar_tensor_tensor(out=rt[3], in0=rt[2], scalar=-3e38, in1=logits[:, :, :],
                                              op0=ALU.mult, op1=ALU.add))
                pick(rt[3], rv[2], rt[4], rv[3])
                dve.tensor_tensor(rv[4], rv[2], rv[0], ALU.subtract).then_inc(q["gap"], 1)
                dve.wait_ge(q["exp"], 1)
                then(dve.tensor_scalar(rv[6], rv[5], 1.0, None, ALU.add))
                then(dve.reciprocal(rv[7], rv[6]))
                then(dve.tensor_tensor(rv[4], rv[5], rv[7], ALU.mult))
                then(dve.tensor_tensor(rt[0], rt[2], wide(rv[7]), ALU.mult))
                then(dve.tensor_tensor(rt[1], rt[4], wide(rv[4]), ALU.mult))
                dve.tensor_tensor(cw[:, :, :], rt[0], rt[1], ALU.add).then_inc(q["weights"], 1)
            else:
                dve.tensor_tensor(rt[3], logits[:, :, :], wide(rv[0]), ALU.subtract).then_inc(q["gap"], 1)
                dve.wait_ge(q["exp"], 1)
                then(dve.tensor_reduce(rv[6], rt[4], AX.X, ALU.add))
                then(dve.reciprocal(rv[7], rv[6]))
                dve.tensor_tensor(cw[:, :, :], rt[2], wide(rv[7]), ALU.mult).then_inc(q["weights"], 1)

        def route_scalar(act, layer):
            q = rs[layer]
            act.wait_ge(q["gap"], 1)
            if layer == 0:
                act.activation(rv[5], rv[4], ACT.Exp).then_inc(q["exp"], 1)
            else:
                act.activation(rt[4], rt[3], ACT.Exp).then_inc(q["exp"], 1)

        ex = [{n: sem(f"ex{k}_{n}") for n in
               ("w_in0", "w_in1", "up_mm", "act_ready", "hid_ready", "down_mm", "added", "staged", "cw_turned",
                "cwT_ready", "bias_mm", "bias_added")} for k in range(2)]
        UNITS = (2, 4)

        def bias_tensor(pe, layer):
            q = ex[layer]
            with pe.Fori(0, G) as g:
                pe.wait_ge(q["staged"], g + 1)
                for t in range(T):
                    last = pe.transpose(feat_tile(4, t)[0:E, :], cws[:, t, :], ident[0:TP, 0:TP])
                last.then_inc(q["cw_turned"], 1)
                pe.wait_ge(q["cwT_ready"], g + 1)
                for t in range(T):
                    last = pe.matmul(tok_tile(2, t), cwT[:, t * TP:(t + 1) * TP], bias2[:, layer, :],
                                     start=True, stop=True)
                last.then_inc(q["bias_mm"], 1)

        def bias_scalar(act, layer):
            q = ex[layer]
            with act.Fori(0, G) as g:
                act.wait_ge(q["cw_turned"], g + 1)
                for k, (o, n) in enumerate(SPLIT):
                    last = act.activation(cwT[:, o:o + n], ps[0:E, 4 + k, 0:n], ACT.Copy)
                last.then_inc(q["cwT_ready"], 1)

        def bias_vector(dve, layer):
            q = ex[layer]
            dve.wait_ge(rs[layer]["weights"], 1)
            with dve.Fori(0, G) as g:
                dve.tensor_copy(cws[:, :, :], cw[:, bass.ts(g, T), :]).then_inc(q["staged"], 1)
                dve.wait_ge(q["bias_mm"], g + 1)
                ht = h_tok[:, bass.ts(g, T), :]
                dve.tensor_tensor(ht, tok_psum(2), ht, ALU.add).then_inc(q["bias_added"], 1)
            dve.wait_ge(q["bias_added"], G)

        def experts_sync(sp, layer):
            q = ex[layer]
            up, down, bias = d[f"up{layer}"], d[f"down{layer}"], d[f"b1_{layer}"]

            def fetch(e, par):
                sp.dma_start(w1[:, par, :], up[e]).then_inc(q[f"w_in{par}"], 16)
                sp.dma_start(w2[:, par, 0:UNITS[layer], :], down[e]).then_inc(q[f"w_in{par}"], 16)
                sp.dma_start(b1[:, par, :], bias[e]).then_inc(q[f"w_in{par}"], 16)

            fetch(0, 0)
            fetch(1, 1)
            with sp.Fori(0, E // 2 - 1) as k:
                for par in range(2):
                    sp.wait_ge(q["down_mm"], (2 * k + (par + 1)) * NB)
                    fetch(2 * k + (par + 2), par)

        def experts_tensor(pe, layer):
            q = ex[layer]
            U = UNITS[layer]

            def expert(e, k, par):
                def up(blk, c, n):
                    pe.wait_ge(q["hid_ready"], n + 1)
                    for j in range(2 if layer == 0 else 1):
                        f = c + j * U
                        last = pe.matmul(ps[:, 2 * (c % 2) + j, 0:BN], w1[:, par, f * D:(f + 1) * D],
                                         xfT[:, bass.ts(blk, BT), :], start=True, stop=True)
                    last.then_inc(q["up_mm"], 1)

                def down(c, n, bb, block):
                    pe.wait_ge(q["hid_ready"], n + 3)
                    if c == 0:
                        pe.wait_ge(q["added"], block + 1)
                    for t in range(BT):
                        last = pe.matmul(ps[0:TP, 4 + bb, t * D:(t + 1) * D], act_a[:, c, t * TP:(t + 1) * TP],
                                         w2[:, par, c, :], start=(c == 0 and t == 0), stop=(c == U - 1),
                                         skip_group_check=True)
                    if c == U - 1:
                        last.then_inc(q["down_mm"], 1)

                base = e * (NB * U)
                pe.wait_ge(q[f"w_in{par}"], 48 * k + 48)
                up(0, 0, base)

                def pair(j, is_last):
                    for bb in range(2):
                        blk = 2 * j + bb
                        n = base + blk * U
                        for c in range(U):
                            if c + 1 < U:
                                up(blk, c + 1, n + (c + 1))
                            elif not (is_last and bb == 1):
                                up(blk + 1, 0, n + U)
                            down(c, n + c, bb, e * NB + blk)

                with pe.Fori(0, NB // 2 - 1) as j:
                    pair(j, False)
                pair(NB // 2 - 1, True)

            with pe.Fori(0, E // 2) as k:
                for par in range(2):
                    expert(2 * k + par, k, par)

        def experts_scalar(act, layer):
            q = ex[layer]
            U = UNITS[layer]
            if layer == 1:
                act.sem_inc(q["hid_ready"], 2)
            with act.Fori(0, E // 2) as k:
                for par in range(2):
                    act.wait_ge(q[f"w_in{par}"], 48 * k + 48)
                    with act.Fori(0, NB) as blk:
                        for c in range(U):
                            n = (2 * k + par) * (NB * U) + blk * U + c
                            act.wait_ge(q["up_mm"], n + 1)
                            if layer == 0:
                                act.activation(act_b[:, c, :], ps[:, 2 * c, 0:BN], ACT.Silu,
                                               bias=b1[:, par, c:c + 1]).then_inc(q["act_ready"], 1)
                            else:
                                act.activation(act_a[:, c, :], ps[:, 2 * (c % 2), 0:BN], ACT.Gelu_apprx_tanh,
                                               bias=b1[:, par, c:c + 1]).then_inc(q["hid_ready"], 1)

        def experts_vector(dve, layer):
            q = ex[layer]
            U = UNITS[layer]
            if layer == 0:
                dve.sem_inc(q["hid_ready"], 2)
            dve.sem_inc(q["added"], 2)
            with dve.Fori(0, E // 2) as k:
                for par in range(2):
                    e = 2 * k + par
                    if layer == 0:
                        stand(dve, q[f"w_in{par}"], 48 * k + 48)
                    with dve.Fori(0, NB // 2) as j:
                        for bb in range(2):
                            blk = 2 * j + bb
                            if layer == 0:
                                for c in range(U):
                                    n = e * (NB * U) + blk * U + c
                                    dve.wait_ge(q["act_ready"], n + 1)
                                    dve.scalar_tensor_tensor(out=act_a[:, c, :], in0=ps[:, 2 * c + 1, 0:BN],
                                                             scalar=b1[:, par, U + c:U + c + 1],
                                                             in1=act_b[:, c, :], op0=ALU.add, op1=ALU.mult)\
                                       .then_inc(q["hid_ready"], 1)
                            block = e * NB + blk
                            dve.wait_ge(q["down_mm"], block + 1)
                            dve.wait_ge(q["added"], block + 2)
                            for t in range(BT):
                                tile = blk * BT + t
                                ht = h_tok[:, bass.ts(tile, 1), :].squeeze(1)
                                last = dve.scalar_tensor_tensor(
                                    out=ht, in0=ps[0:TP, 4 + bb, t * D:(t + 1) * D],
                                    scalar=cw[:, bass.ts(tile, 1), bass.ts(e, 1)].rearrange("p a b -> p (a b)"),
                                    in1=ht, op0=ALU.mult, op1=ALU.add)
                            last.then_inc(q["added"], 1)

        JOBS = ("f0", "f1", "t0", "t1", "k0", "k1", "q0", "q1", "v0", "v1", "g0", "g1", "g2")
        JOB_SLOT = {"f0": 2, "f1": 2, "t0": 3, "t1": 3, "k0": 4, "k1": 4, "q0": 5, "q1": 5, "v0": 6, "v1": 6,
                    "g0": 7, "g1": 7, "g2": 7}
        at_ = {n: sem("at_" + n) for n in
               ("stats_ready mean_ready spread_ready rstd_ready norm_ready keysM_ready scores_mm peak_ready "
                "diff_ready prob_ready turn_mm probT_ready av_mm rden_ready o_ready o_turned outT_ready "
                "pool_ready y_ready y2_ready ones_ready t_ready t_kept").split()}
        at_["full"] = {j: sem(f"full_{j}") for j in JOBS}
        at_["empty"] = {j: sem(f"empty_{j}") for j in JOBS}
        at_["tiles"] = norm_tiles[0]
        fin = {n: sem("fin_" + n) for n in ("stats_ready", "mean_ready", "spread_ready", "rstd_ready")}
        fin["tiles"] = norm_tiles[1]

        def job_group(i, j):
            return i + 1 if j[0] in "tkqv" else i - 1

        def job_list(i, layer):
            return [j for j in JOBS if (layer or j[0] != "g") and has(job_group(i, j), 0, G)]

        def job_before(i, j, layer):
            here = job_list(i, layer)
            at = here.index(j)
            if at:
                return here[at - 1], job_group(i, here[at - 1])
            if isinstance(i, int):
                if i < 0:
                    return None
                prev = job_list(i - 1, layer)
            else:
                prev = job_list(i, layer)
            return (prev[-1], job_group(i - 1, prev[-1])) if prev else None

        AT_FIRST, AT_INNER, AT_LAST = (-1, 3), 4, G + 1

        def img(i, m, r):
            n = GI * i + (m + r)
            return (not isinstance(i, int) or 0 <= n < B), n

        def attention_tensor(pe, layer):
            q = at_
            L, N0 = G * layer, B * layer
            M = M_ATT + 4 * layer

            def take(i, j):
                before = job_before(i, j, layer)
                if before:
                    pe.wait_ge(q["empty"][before[0]], before[1] + (1 + (L if before[0][0] != "g" else 0)))

            def job(i, j, par):
                g = job_group(i, j)
                gp = 1 - par
                take(i, j)
                h = int(j[1])
                half = slice(h * HALF, (h + 1) * HALF)
                tiles = range(4) if h == 0 else range(4, 5)
                if j[0] == "f":
                    if h == 0:
                        pe.wait_ge(q["outT_ready"], GI * (g + (L + 1)))
                    for t in tiles:
                        last = pe.matmul(ps[0:TP, 7, t % 4 * D:(t % 4 + 1) * D], outT[:, gp, t * TP:(t + 1) * TP],
                                         mats[:, M + 3, :], start=True, stop=True)
                elif j[0] in "tg" and j != "g2":
                    if h == 0:
                        pe.wait_ge(*((q["norm_ready"], g + (L + 1)) if j[0] == "t" else (q["t_ready"], g + 1)))
                    src = xn[:, gp] if j[0] == "t" else xf[:, :, :]
                    for t in tiles:
                        last = pe.transpose(ps[:, 7, t % 4 * TP:(t % 4 + 1) * TP], src[:, t, :], ident[0:TP, 0:TP])
                elif j[0] in "kq":
                    last = pe.matmul(ps[:, 7, 0:HALF], mats[:, M + (j[0] == "k"), :], xT[:, half], start=True, stop=True)
                elif j[0] == "v":
                    for a in range(GI // 2):
                        b = h * (GI // 2) + a
                        last = pe.matmul(ps[0:S, 7, a * D:(a + 1) * D], xT[:, b * S:(b + 1) * S], mats[:, M + 2, :],
                                         start=True, stop=True)
                else:
                    for t in range(T):
                        last = pe.matmul(ps[0:TP, 7, t * E:(t + 1) * E], tT[:, t * TP:(t + 1) * TP],
                                         route_w[:, 1, :], start=True, stop=True)
                last.then_inc(q["full"][j], 1)

            def emit(i, par):
                for m in range(GI):
                    ok, n = img(i, m, 1)
                    if ok:
                        p, b = (m + 1) % 2, (m + 1) % GI
                        gp = par if m + 1 < GI else 1 - par
                        g = i if m + 1 < GI else i + 1
                        if b in (0, GI // 2):
                            pe.wait_ge(q["keysM_ready"], 2 * g + (2 * L + (1 if b == 0 else 2)))
                            pe.wait_ge(q["empty"]["q1"], g + (L + 1))
                        after(pe, q["diff_ready"], n + (N0 - 1))
                        for k in range(2):
                            bank = ps[0:S, 2 * p + k, 0:HALF]
                            if layer == 0:
                                pe.matmul(bank, identb[0:S, 0:S], maskb[:, :], start=True, stop=False)
                            last = pe.matmul(bank, qT[:, gp, b * S:(b + 1) * S],
                                             keysM[:, gp, b, 4 * k:4 * k + 4, :].rearrange("p h s -> p (h s)"),
                                             start=(layer == 1), stop=True)
                        last.then_inc(q["scores_mm"], 1)
                    ok, n = img(i, m, -2)
                    if ok:
                        pe.wait_ge(q["o_ready"], n + (N0 + 1))
                        pe.transpose(ps[:, 6, 256:256 + S], o_tok[:, m % 2, :], ident[0:S, 0:S]).then_inc(q["o_turned"], 1)
                    ok, n = img(i, m, 0)
                    if ok:
                        pe.wait_ge(q["prob_ready"], n + (N0 + 1))
                        after(pe, q["probT_ready"], n + N0)
                        for h in range(H):
                            last = pe.transpose(ps[0:S, 4 + h // 4, h % 4 * S:(h % 4 + 1) * S], prob[:, m % 2, h, :],
                                                ident[0:S, 0:S])
                        last.then_inc(q["turn_mm"], 1)
                    ok, n = img(i, m, -1)
                    if ok:
                        p, b = (m - 1) % 2, (m - 1) % GI
                        gp = par if m else 1 - par
                        pe.wait_ge(q["probT_ready"], n + (N0 + 1))
                        after(pe, q["outT_ready"], n + N0)
                        for h in range(H):
                            last = pe.matmul(ps[0:S, 6, h * HA:(h + 1) * HA], probT[:, p, h, :], vals[:, gp, b, h, :],
                                             start=True, stop=True)
                        last.then_inc(q["av_mm"], 1)
                    for j in job_list(i, layer):
                        if JOB_SLOT[j] == m:
                            job(i, j, par)

            steps(pe, emit, AT_FIRST, AT_INNER, AT_LAST)

        def attention_scalar(act, layer):
            q = at_
            L, N0 = G * layer, B * layer
            C = C_ATT + 3 * layer

            def job(i, j, par):
                g = job_group(i, j)
                gp = 1 - par
                h = int(j[1])
                half = slice(h * HALF, (h + 1) * HALF)
                tok = slice(0, 4 * TP) if h == 0 else slice(4 * TP, GT)
                nt = 4 if h == 0 else 1
                act.wait_ge(q["full"][j], g + (1 if j[0] == "g" else L + 1))
                if j[0] == "t":
                    last = act.activation(xT[:, tok], ps[:, 7, 0:nt * TP], ACT.Copy)
                elif j[0] == "k":
                    after(act, q["keysM_ready"], 2 * g + 2 * L)
                    last = act.activation(keysT[:, half], ps[:, 7, 0:HALF], ACT.Identity, bias=cols[:, C + 1:C + 2])
                elif j[0] == "q":
                    last = act.activation(qT[:, gp, half], ps[:, 7, 0:HALF], ACT.Identity, bias=cols[:, C:C + 1])
                elif j[0] == "v":
                    last = act.activation(vals[:, gp, 4 * h:4 * h + 4, :, 0:DK],
                                          ps[0:S, 7, :].rearrange("p (a h k) -> p a h k", a=4, h=H), ACT.Copy)
                else:
                    act.activation(tT[:, tok], ps[:, 7, 0:nt * TP], ACT.Copy).then_inc(q["t_kept"], 1)
                    last = act.activation(xfT[:, bass.ds(g * T + 4 * h, nt), :],
                                          ps[:, 7, 0:nt * TP].rearrange("p (t n) -> p t n", n=TP), ACT.Copy)
                last.then_inc(q["empty"][j], 1)

            def emit(i, par):
                for m in range(GI):
                    ok, n = img(i, m, -2)
                    if ok:
                        gp = par if m > 1 else 1 - par
                        b = (m - 2) % GI
                        act.wait_ge(q["o_turned"], n + (N0 + 1))
                        act.activation(outT[:, gp, b * S:(b + 1) * S], ps[:, 6, 256:256 + S], ACT.Identity,
                                       bias=cols[:, C + 2:C + 3]).then_inc(q["outT_ready"], 1)
                    ok, n = img(i, m, 0)
                    if ok:
                        act.wait_ge(q["turn_mm"], n + (N0 + 1))
                        for k in range(2):
                            last = act.activation(probT[:, m % 2, 4 * k:4 * k + 4, :].rearrange("p h s -> p (h s)"),
                                                  ps[0:S, 4 + k, 0:HALF], ACT.Copy)
                        last.then_inc(q["probT_ready"], 1)
                    ok, n = img(i, m, 1)
                    if ok:
                        p = (m + 1) % 2
                        act.wait_ge(q["diff_ready"], n + (N0 + 1))
                        act.activation(prob[:, p, :, :], diff[:, p, :, :], ACT.Exp, scale=DK ** -0.5)\
                           .then_inc(q["prob_ready"], 1)
                    for j in job_list(i, layer):
                        if JOB_SLOT[j] == m and j[0] in "tkqvg" and j != "g2":
                            job(i, j, par)

            steps(act, emit, AT_FIRST, AT_INNER, AT_LAST)

        def attention_vector(dve, layer):
            q = at_
            L, N0 = G * layer, B * layer

            def emit(i, par):
                nxt, prv = has(i + 1, 0, G), has(i - 1, 0, G)
                gp = 1 - par
                for m in range(GI):
                    ok, n = img(i, m, 1)
                    if ok:
                        p = (m + 1) % 2
                        banks = ps[0:S, 2 * p:2 * p + 2, 0:HALF].rearrange("p a (h s) -> p a h s", s=S)
                        dve.wait_ge(q["scores_mm"], n + (N0 + 1))
                        dve.tensor_reduce(peak[:, p, :].rearrange("p (a h) -> p a h", a=2), banks, AX.X, ALU.max)\
                           .then_inc(q["peak_ready"], 1)
                        dve.wait_ge(q["peak_ready"], n + (N0 + 1))
                        after(dve, q["prob_ready"], n + (N0 - 1))
                        dve.tensor_tensor(diff[:, p, :, :].rearrange("p (a h) s -> p a h s", a=2), banks,
                                          peak[:, p, :].rearrange("p (a h) -> p a h", a=2).unsqueeze(3)
                                          .broadcast_to([S, 2, 4, S]), ALU.subtract).then_inc(q["diff_ready"], 1)
                    ok, n = img(i, m, -1)
                    if ok:
                        av = ps[0:S, 6, 0:H * HA].rearrange("p (h a) -> p h a", a=HA)
                        dve.wait_ge(q["av_mm"], n + (N0 + 1))
                        dve.reciprocal(rden[:, :], av[:, :, DK]).then_inc(q["rden_ready"], 1)
                        dve.wait_ge(q["rden_ready"], n + (N0 + 1))
                        after(dve, q["o_turned"], n + (N0 - 1))
                        dve.tensor_tensor(o_tok[:, (m - 1) % 2, :].rearrange("p (h k) -> p h k", h=H), av[:, :, 0:DK],
                                          rden[:, :].unsqueeze(2).broadcast_to([S, H, DK]), ALU.mult)\
                           .then_inc(q["o_ready"], 1)
                    if m == 1 and nxt:
                        norm_stats(dve, q, h_tok[:, bass.ts(i + 1, T), :], i + (L + 2))
                    if m == 2 and nxt:
                        g = i + 1
                        if layer == 1:
                            after(dve, q["pool_ready"], g + (L - 1))
                        after(dve, q["full"]["t1"], g + (L - 1))
                        norm_apply(dve, q, xn[:, gp], h_tok[:, bass.ts(g, T), :], g + (L + 1)).then_inc(q["norm_ready"], 1)
                    if m == 2 and prv:
                        g = i - 1
                        dve.wait_ge(q["pool_ready"], g + (L + 1))
                        for h, (a, b) in enumerate(((0, 4), (4, 5))):
                            dve.wait_ge(q["full"][f"f{h}"], g + (L + 1))
                            dst = h_tok[:, bass.ds(g * T + a, b - a), :] if layer == 0 else y[:, a:b, :]
                            dve.tensor_tensor(dst, ps[0:TP, 7, 0:(b - a) * D].rearrange("p (t d) -> p t d", d=D),
                                              hb[:, a:b, :], ALU.add).then_inc(q["empty"][f"f{h}"], 1)
                    if m == 3 and prv and layer == 1:
                        g = i - 1
                        dve.wait_ge(q["empty"]["f1"], g + (L + 1))
                        norm_stats(dve, fin, y, g + 1)
                    if m == 5 and prv and layer == 1:
                        g = i - 1
                        after(dve, q["full"]["g1"], g)
                        norm_apply(dve, fin, xf, y, g + 1).then_inc(q["y_ready"], 1)
                        dve.wait_ge(q["y_ready"], g + 1)
                        dve.tensor_tensor(y[:, :, :], xf[:, :, :],
                                          rows[:, R_G1:R_G1 + 1, :].broadcast_to([TP, T, D]), ALU.mult)\
                           .then_inc(q["y2_ready"], 1)
                    if m == 6 and prv and layer == 1:
                        g = i - 1
                        dve.wait_ge(q["y2_ready"], g + 1)
                        dve.tensor_tensor(xf[:, :, :], y[:, :, :],
                                          rows[:, R_B1:R_B1 + 1, :].broadcast_to([TP, T, D]), ALU.add)\
                           .then_inc(q["t_ready"], 1)
                    if m in (5, 6) and nxt:
                        g = i + 1
                        h = m - 5
                        dve.wait_ge(q["empty"][f"k{h}"], g + (L + 1))
                        after(dve, q["scores_mm"], GI * (g + (L - 1)))
                        for hd in range(H):
                            last = dve.tensor_scalar(keysM[:, gp, 4 * h:4 * h + 4, hd, :],
                                                     keysT[:, h * HALF:(h + 1) * HALF].rearrange("p (a s) -> p a s", s=S),
                                                     cols[:, C_HEAD + hd:C_HEAD + hd + 1], None, ALU.mult)
                        last.then_inc(q["keysM_ready"], 1)
                    if m == 7 and prv and layer == 1:
                        g = i - 1
                        dve.wait_ge(q["full"]["g2"], g + 1)
                        dve.tensor_tensor(logits[:, bass.ts(g, T), :],
                                          ps[0:TP, 7, 0:T * E].rearrange("p (t e) -> p t e", e=E),
                                          route_b[:, 1:2, :].broadcast_to([TP, T, E]), ALU.add)\
                           .then_inc(q["empty"]["g2"], 1)

            dve.memset(vals[:, :, :, :, DK:HA].rearrange("p a b h k -> p (a b h) k"), 1.0).then_inc(q["ones_ready"], 1)
            dve.wait_ge(q["ones_ready"], layer + 1)
            steps(dve, emit, AT_FIRST, AT_INNER, AT_LAST)

        def attention_gpsimd(pool, layer):
            q = at_
            L, N0 = G * layer, B * layer

            def emit(i, par):
                if has(i - 1, 0, G):
                    g = i - 1
                    gp = 1 - par
                    after(pool, q["empty"]["f1"], g + L)
                    src = h_tok[:, bass.ts(g, T), :] if layer == 0 else xn[:, gp]
                    row = R_BO0 + layer
                    pool.tensor_tensor(hb[:, :, :], src, rows[:, row:row + 1, :].broadcast_to([TP, T, D]),
                                       ALU.add).then_inc(q["pool_ready"], 1)
                if has(i + 1, 0, G):
                    norm_spread(pool, q, i + (L + 2))
                if has(i - 1, 0, G) and layer == 1:
                    norm_spread(pool, fin, i)

            steps(pool, emit, AT_FIRST, AT_INNER, AT_LAST)

        phases = [0]

        def barrier(eng, number):
            eng.drain().then_inc(phase_done, 1)
            eng.wait_ge(phase_done, 5 * number)

        s_out = sem("stored")
        block = ctx.enter_context(nc.Block())

        @block.sync
        def _(sp):
            p1_sync(sp)
            barrier(sp, 1)
            barrier(sp, 2)
            experts_sync(sp, 0)
            for n in (3, 4, 5, 6):
                barrier(sp, n)
            experts_sync(sp, 1)
            barrier(sp, 7)
            sp.dma_start(d["out"], h_tok[:, :, :]).then_inc(s_out, 16)
            sp.wait_ge(s_out, 16)

        @block.tensor
        def _(pe):
            pe.wait_ge(s_in, 16 * len(loads))
            pe.wait_ge(s_made, 4)
            p1_tensor(pe)
            barrier(pe, 1)
            bias_tensor(pe, 0)
            barrier(pe, 2)
            experts_tensor(pe, 0)
            barrier(pe, 3)
            attention_tensor(pe, 0)
            barrier(pe, 4)
            attention_tensor(pe, 1)
            barrier(pe, 5)
            bias_tensor(pe, 1)
            barrier(pe, 6)
            experts_tensor(pe, 1)
            barrier(pe, 7)

        @block.scalar
        def _(act):
            for dst, src in loads:
                act.dma_start(dst, src).then_inc(s_in, 16)
            act.wait_ge(s_in, 16 * len(loads))
            p1_scalar(act)
            barrier(act, 1)
            route_scalar(act, 0)
            bias_scalar(act, 0)
            barrier(act, 2)
            experts_scalar(act, 0)
            barrier(act, 3)
            attention_scalar(act, 0)
            barrier(act, 4)
            attention_scalar(act, 1)
            barrier(act, 5)
            route_scalar(act, 1)
            bias_scalar(act, 1)
            barrier(act, 6)
            experts_scalar(act, 1)
            barrier(act, 7)

        @block.vector
        def _(dve):
            p1_vector(dve)
            barrier(dve, 1)
            route_vector(dve, 0)
            bias_vector(dve, 0)
            barrier(dve, 2)
            experts_vector(dve, 0)
            barrier(dve, 3)
            attention_vector(dve, 0)
            barrier(dve, 4)
            attention_vector(dve, 1)
            barrier(dve, 5)
            route_vector(dve, 1)
            bias_vector(dve, 1)
            barrier(dve, 6)
            experts_vector(dve, 1)
            barrier(dve, 7)

        @block.gpsimd
        def _(pool):
            pool.memset(ident[:, :], 0.0).then_inc(s_made, 1)
            pool.memset(halves[:, :], -0.5).then_inc(s_made, 1)
            pool.wait_ge(s_made, 2)
            pool.affine_select(out=ident[:, :], in_=ident[:, :], compare_op=ALU.not_equal, fill=1.0, base=0,
                               pattern=[[-1, 128]], channel_multiplier=1).then_inc(s_made, 1)
            pool.wait_ge(s_made, 3)
            pool.tensor_copy(identb[:, :], ident[:, :]).then_inc(s_made, 1)
            pool.wait_ge(s_in, 16 * len(loads))
            p1_gpsimd(pool)
            barrier(pool, 1)
            barrier(pool, 2)
            barrier(pool, 3)
            attention_gpsimd(pool, 0)
            barrier(pool, 4)
            attention_gpsimd(pool, 1)
            for n in (5, 6, 7):
                barrier(pool, n)


def kernel(**inputs):
    import numpy as np
    import concourse.bacc as bacc
    from concourse.bass_utils import run_bass_kernel_spmd

    f = {k: np.asarray(v) for k, v in inputs.items()}
    P = f["x"].shape[2] // 8
    x = f["x"].reshape(G, GI, 3, 8, P, 8, P).transpose(0, 2, 4, 6, 1, 3, 5).reshape(G, KF * 128 + KR, GI * NP)
    w = f["L0_tok_W"].T

    def parts(a, n):
        return a.reshape(*a.shape[:-2], n, 128, a.shape[-1]).swapaxes(-3, -2)

    heads = np.zeros((D, H), np.float32)
    for h in range(H):
        heads[h * DK:(h + 1) * DK, h] = 1.0
    cols = np.concatenate([np.stack([
        f["L0_tok_b"], f["L0_tok_class_token"][0], f["L0_attn_b_in"][:D], f["L0_attn_b_in"][D:], f["L0_attn_B"],
        f["L0_attn_A"], f["L1_attn_b_Q"], f["L1_attn_b_K"], f["L1_attn_b_V"], f["L1_ffn_bq"], f["L1_ffn_bk"],
        f["L1_ffn_bv"]], 1), heads], 1)
    rows = np.stack([f["L0_attn_b_out"], f["L0_attn_gamma"], f["L0_attn_beta"], f["L1_attn_b_O"], f["L1_ffn_bo"],
                     f["L1_ffn_ln1_g"], f["L1_ffn_ln1_b"]])
    win = f["L0_attn_W_in"].T
    mats = np.stack([win[:, :D], win[:, D:], f["L0_attn_W_out"].T]
                    + [f["L1_attn_W_" + n] for n in "QKVO"] + [f["L1_ffn_W" + n] for n in "qkvo"], 1)
    i, j = np.arange(S)[:, None], np.arange(S)[None, :]
    gap = i - j
    seen = (gap == 0) | (gap >= 1) & (gap <= S // 2) | (gap > 0) & (gap & gap - 1 == 0)
    mask = np.tile(np.where(seen, 0.0, -1e30).astype(np.float32), (1, 4))
    arrays = {
        "xa": parts(x[:, :KF * 128], KF),
        "xr": x[:, KF * 128:],
        "wp": parts(w[:KF * 128], KF),
        "wpr": w[KF * 128:],
        "cols": cols,
        "posT": f["L0_tok_pos_embed"].T,
        "mats": mats,
        "rows": np.broadcast_to(rows, (TP, NROW, D)),
        "route_w": np.stack([f["L0_ffn_router_w"].T, f["L1_ffn_gate_W"]], 1),
        "route_b": np.broadcast_to(np.stack([f["L0_ffn_router_b"], f["L1_ffn_gate_b"]]), (TP, 2, E)),
        "bias2": np.stack([f["L0_ffn_fc2_b"], f["L1_ffn_b2"]], 1),
        "mask": mask,
        "ids": np.broadcast_to(np.arange(E, dtype=np.float32), (TP, E)),
        "up0": f["L0_ffn_fc1_w"].transpose(0, 2, 1),
        "down0": parts(f["L0_ffn_fc2_w"].transpose(0, 2, 1), 2),
        "b1_0": f["L0_ffn_fc1_b"].reshape(E, 4, 128).transpose(0, 2, 1),
        "up1": f["L1_ffn_W1"],
        "down1": parts(f["L1_ffn_W2"], 4),
        "b1_1": f["L1_ffn_b1"].reshape(E, 4, 128).transpose(0, 2, 1),
    }
    nc = bacc.Bacc("TRN2", target_bir_lowering=False, num_devices=1)
    d = {}
    for name, a in arrays.items():
        arrays[name] = a = np.ascontiguousarray(a)
        d[name] = nc.dram_tensor("in_" + name, a.shape, mybir.dt.from_np(a.dtype), kind="ExternalInput").ap()
    d["out"] = nc.dram_tensor("stored_out", (B * S, D), F32, kind="ExternalOutput").ap().rearrange("(t p) d -> p t d", p=TP)
    build_program(nc, d)
    got = run_bass_kernel_spmd(nc, [{"in_" + k: a for k, a in arrays.items()}], core_ids=[0]).results[0]["stored_out"]
    return got.reshape(B, S, D)
```

```python
from contextlib import ExitStack

import concourse.bass as bass
from concourse import mybir

F32 = mybir.dt.float32
I32 = mybir.dt.int32
BF16 = mybir.dt.bfloat16
ALU = mybir.AluOpType
ACT = mybir.ActivationFunctionType
AX = mybir.AxisListType

D = 128
B = 64
S = 65
NP = S - 1
GI = 8
G = B // GI
GT = GI * S
TP = 104
T = GT // TP
NT = G * T
KF = 18
KR = 48
H = 8
DK = D // H
HA = DK + 1
E = 8
TOP = (2, 1)
ET = 128
NE = tuple(-(-((k * B * S + E * (ET - 1)) // ET) // 8) * 8 for k in TOP)
UNITS = (2, 4)
PACK = 2
RING = 4 * PACK
HALF = GI // 2 * S
EPS = 1e-5
SHRINK = 7
SPLIT = ((0, 3 * TP), (3 * TP, 2 * TP))
PARTS = ((0, 6), (6, 12), (12, 18))

C_TOKB, C_CLS, C_BZ, C_BG, C_B, C_A = range(6)
C_ATT = 6
C_HEAD = 12
NCOL = C_HEAD + H
R_BOUT, R_GAMMA, R_BETA, R_BO0, R_BO1, R_G1, R_B1 = range(7)
NROW = 7
M_Z, M_G, M_OUT, M_ATT = 0, 1, 2, 3
NMAT = 11


def after(eng, sem, value):
    if isinstance(value, int) and value <= 0:
        return
    eng.wait_ge(sem, value)


def build_program(nc, d):
    ctx = ExitStack()
    with ctx:
        def sb(name, shape, dt=F32):
            return ctx.enter_context(nc.sbuf_tensor(name, shape, dt))

        def sem(name):
            return ctx.enter_context(nc.semaphore(name))

        ps = ctx.enter_context(nc.psum_tensor("ps", [128, 8, 512], F32))

        h_tok = sb("h_tok", [TP, NT, D])
        xf_all = sb("xf_all", [TP, NT, D])
        mats = sb("mats", [D, NMAT, D])
        cols = sb("cols", [D, NCOL])
        rows = sb("rows", [TP, NROW, D])
        route_w = sb("route_w", [D, 2, E])
        route_b = sb("route_b", [TP, 2, E])
        bias2 = sb("bias2", [128, E, D])
        down_w = sb("down_w", [128, E, 4, D])
        ident = sb("ident", [128, 128])
        identb = sb("identb", [128, 128], BF16)
        halves = sb("halves", [TP, T])
        posT = sb("posT", [D, S])
        later = sb("later", [TP, TP])
        ones = sb("ones", [TP, TP])
        tile_no = sb("tile_no", [1, max(NE)])
        tile_expert = sb("tile_expert", [1, max(NE)], I32)
        weight = sb("weight", [TP, 2, NT])
        slot = sb("slot", [TP, 2, NT], I32)
        slot_now = sb("slot_now", [TP, 2, 2, T], I32)
        zeros = sb("zeros", [128, 4 * D])
        maskf = sb("maskf", [S, HALF])
        maskb = sb("maskb", [S, HALF], BF16)
        ids = sb("ids", [TP, E])
        logits = sb("logits", [TP, NT, E])
        arena = sb("arena", [128, 2 * (KF + 1) * 512])
        xs = arena[:, :].rearrange("p (b c n) -> p b c n", b=2, c=KF + 1)
        wp = sb("wp", [128, KF + 1, D])

        def carve(start, parts, shape):
            n = 1
            for x in shape:
                n *= x
            ap = arena[0:parts, start:start + n]
            names = "abcd"[:len(shape)]
            if len(shape) > 1:
                ap = ap.rearrange(f"p ({' '.join(names)}) -> p {' '.join(names)}",
                                  **dict(zip(names, shape)))
            return ap, start + n

        at = 0
        keysM, at = carve(at, D, (2, GI, H, S))
        qT, at = carve(at, D, (2, GT))
        vals, at = carve(at, S, (2, GI, H, HA))
        outT, at = carve(at, D, (2, GT))
        keysT, at = carve(at, D, (GT,))
        diff, at = carve(at, S, (2, H, S))
        prob, at = carve(at, S, (2, H, S))
        probT, at = carve(at, S, (2, H, S))
        got, at = carve(at, TP, (2, 2, T, D))
        assert at <= 2 * (KF + 1) * 512
        at = 0
        up_w, at = carve(at, 128, (RING, 4 * D + 4))
        rows_in, at = carve(at, ET, (RING, D))
        rowsT, at = carve(at, D, (2, ET))
        silu_h, at = carve(at, 128, (2, 2 * ET))
        hid, at = carve(at, 128, (2, 4, ET))
        rows_out, at = carve(at, ET, (RING, D))
        got_all, at = carve(at, TP, (NT, D))
        at = 0
        rt = []
        for _ in range(9):
            r, at = carve(at, TP, (NT, E))
            rt.append(r)
        rv = []
        for _ in range(8):
            r, at = carve(at, TP, (NT,))
            rv.append(r)
        re = []
        for _ in range(5):
            r, at = carve(at, TP, (E,))
            re.append(r)
        et = []
        for _ in range(3):
            r, at = carve(at, TP, (E, NT))
            et.append(r)
        counted_i = sb("counted_i", [TP, 2, E], I32)
        past, at = carve(at, 1, (max(NE), E))
        past_n, at = carve(at, 1, (max(NE),))

        tokT = sb("tokT", [D, GI, S])
        xn = sb("xn", [TP, 2, T, D])
        xT = sb("xT", [D, GT])
        norm_tiles = [(sb(f"stats{k}", [TP, T, 6]), sb(f"mv{k}", [TP, T, 2]), sb(f"spread{k}", [TP, T]),
                       sb(f"rstd{k}", [TP, T])) for k in range(2)]
        gate = sb("gate", [D, GT])
        ga = sb("ga", [D, GT])
        bz = sb("bz", [D, GT])
        carried = sb("carried", [D, S])
        state = sb("state", [D, GI, S])
        xb = sb("xb", [TP, T, D])
        hb = sb("hb", [TP, T, D])
        y = sb("y", [TP, T, D])
        xf = sb("xf", [TP, T, D])
        tT = sb("tT", [D, GT])
        peak = sb("peak", [S, 2, H])
        rden = sb("rden", [S, H])
        o_tok = sb("o_tok", [S, 2, D])
        warm = sb("warm", [1, 1])
        largest, shrunk, limit, limit2, eps_shrunk, eps_shrunk2, in_range, kept = (
            sb(n, [TP, T]) for n in ("largest", "shrunk", "limit", "limit2", "eps_shrunk", "eps_shrunk2",
                                     "in_range", "kept"))

        def tok_psum(bank, n=T):
            return ps[0:TP, bank:bank + 2, :].rearrange("p a n -> p (a n)")[:, 0:n * D]\
                .rearrange("p (t d) -> p t d", d=D)

        def tok_tile(bank, t):
            return ps[0:TP, bank + t // 4, t % 4 * D:(t % 4 + 1) * D]

        def feat_tile(bank, t):
            k = t // 3
            return ps[:, bank + k, (t - 3 * k) * TP:(t - 3 * k + 1) * TP]

        s_patch_w = sem("patch_weights_loaded")
        s_in = sem("constants_loaded")
        s_const = sem("class_token_ready")
        s_made = sem("identity_made")
        s_stood = sem("stood")
        s_zero = sem("zeros_ready")
        s_clear = sem("slots_cleared")
        s_scattered = sem("rows_scattered")
        s_experts = sem("expert_constants_loaded")
        s_last = sem("sum_ready")
        s_out = sem("stored")
        phase_done = sem("phase_done")
        loads = []

        def load(dst, src):
            loads.append((dst, src))

        load(cols[:, :], d["cols"])
        load(posT[:, :], d["posT"])
        load(mats[:, :, :], d["mats"])
        load(rows[:, :, :], d["rows"])
        load(route_w[:, :, :], d["route_w"])
        load(route_b[:, :, :], d["route_b"])
        load(tile_no[:, :], d["tile_no"])
        load(maskf[:, :], d["mask"])
        load(ids[:, :], d["ids"])

        x_in = [[sem(f"x_in{p}{k}") for k in range(len(PARTS))] for p in range(2)]
        names = ("patch_mm patch_read tok_turned h_saved norm_ready norm_turned normT_ready zg_mm gate_ready "
                 "bz_ready carry_ready state_ready out_mm xb_ready hb_ready out_read y_ready scaled_ready h_ready "
                 "xf_ready xf_turned xfT_ready xfT_kept logit_mm logit_ready shrink_step").split()
        p1 = {n: sem("p1_" + n) for n in names}
        norm_names = ("stats_ready", "mean_ready", "spread_ready", "rstd_ready")
        n_in = {n: sem("norm_in_" + n) for n in norm_names}
        n_in["tiles"] = norm_tiles[0]
        n_out = {n: sem("norm_out_" + n) for n in norm_names}
        n_out["tiles"] = norm_tiles[1]

        def stand(eng, sem_, value):
            eng.wait_ge(sem_, value)
            eng.sem_inc(s_stood, 1)

        def norm_sums(dve, q, src):
            stats = q["tiles"][0]
            for t in range(T):
                last = dve.bn_stats(stats[:, t, :], src[:, t, :])
            last.then_inc(q["stats_ready"], 1)

        def norm_means(dve, q, count):
            stats, mv = q["tiles"][0:2]
            stand(dve, q["stats_ready"], count)
            for t in range(T):
                last = dve.bn_aggr(mv[:, t, :], stats[:, t, :])
            last.then_inc(q["mean_ready"], 1)

        def norm_stats(dve, q, src, count):
            norm_sums(dve, q, src)
            norm_means(dve, q, count)

        def norm_spread(pool, q, count, eps=None):
            _, mv, spread, rstd = q["tiles"]
            stand(pool, q["mean_ready"], count)
            if eps is None:
                ins = pool.tensor_scalar(spread[:, :], mv[:, :, 1], EPS, None, ALU.add)
            else:
                ins = pool.tensor_tensor(spread[:, :], mv[:, :, 1], eps[:, :], ALU.add)
            ins.then_inc(q["spread_ready"], 1)
            pool.wait_ge(q["spread_ready"], count)
            pool.tensor_tensor(rstd[:, :], spread[:, :], halves[:, :], ALU.pow).then_inc(q["rstd_ready"], 1)

        def norm_apply(dve, q, dst, src, count, r=None):
            _, mv, _, rstd = q["tiles"]
            if r is None:
                dve.wait_ge(q["rstd_ready"], count)
            else:
                rstd = r
            for t in range(T):
                last = dve.tensor_scalar(dst[:, t, :], src[:, t, :], mv[:, t, 0:1], rstd[:, t:t + 1],
                                         ALU.subtract, ALU.mult)
            return last

        def steps(eng, emit, first, inner, last):
            for i in range(first[0], first[1]):
                emit(i, i % 2)
            a = first[1]
            with eng.Fori(0, inner // 2) as k:
                for j in range(2):
                    emit(2 * k + (a + j), (a + j) % 2)
            for i in range(a + inner, last):
                emit(i, i % 2)

        def has(i, lo, hi):
            return not isinstance(i, int) or lo <= i < hi

        P1_FIRST, P1_INNER, P1_LAST = (0, 4), 4, G + 3

        def p1_sync(sp):
            def emit(g):
                par = g % 2
                if g >= 2:
                    sp.wait_ge(p1["patch_mm"], g - 1)
                for k, (a, b) in enumerate(PARTS):
                    sp.dma_start(xs[:, par, a:b, :], d["xa"][g, :, a:b, :]).then_inc(x_in[par][k], 16)
                sp.dma_start(xs[0:KR, par, KF, :], d["xr"][g]).then_inc(x_in[par][2], 16)
            emit(0)
            emit(1)
            with sp.Fori(0, 3) as k:
                for par in range(2):
                    g = 2 * k + (2 + par)
                    sp.wait_ge(p1["patch_mm"], g - 1)
                    for n, (a, b) in enumerate(PARTS):
                        sp.dma_start(xs[:, par, a:b, :], d["xa"][g, :, a:b, :]).then_inc(x_in[par][n], 16)
                    sp.dma_start(xs[0:KR, par, KF, :], d["xr"][g]).then_inc(x_in[par][2], 16)

        def up_to(g):
            return min(g, G) if isinstance(g, int) else g

        def out_tiles(a, b):
            bank, first = (7, 0) if a < 4 else (6, 4)
            return ps[0:TP, bank, (a - first) * D:(b - first) * D].rearrange("p (t d) -> p t d", d=D)

        def p1_tensor(pe):
            q = p1

            def turn_tokens(g):
                pe.wait_ge(q["patch_read"], g + 1)
                after(pe, q["bz_ready"], g)
                for t in range(T):
                    last = pe.transpose(tok_tile(2, t), tokT[:, :, :].rearrange("p a s -> p (a s)")[:, t * TP:(t + 1) * TP],
                                        ident[:, :])
                last.then_inc(q["tok_turned"], 1)

            def turn_norm(g):
                pe.wait_ge(q["norm_ready"], g + 1)
                after(pe, q["xfT_ready"], g - 1)
                for t in range(T):
                    last = pe.transpose(feat_tile(4, t), xn[:, 0, t, :], ident[0:TP, 0:TP])
                last.then_inc(q["norm_turned"], 1)

            def project(g):
                pe.wait_ge(q["normT_ready"], g + 1)
                pe.wait_ge(q["h_saved"], g + 1)
                for m, bank in ((M_Z, 2), (M_G, 4)):
                    for k, (o, n) in enumerate(SPLIT):
                        last = pe.matmul(ps[:, bank + k, 0:n], mats[:, m, :], xT[:, o:o + n], start=True, stop=True)
                last.then_inc(q["zg_mm"], 1)

            def project_out(g):
                pe.wait_ge(q["state_ready"], GI * g + GI)
                after(pe, q["out_read"], g)
                after(pe, q["logit_ready"], g - 1)
                for t in range(T):
                    last = pe.matmul(out_tiles(t, t + 1)[:, 0], state[:, :, :].rearrange("p a s -> p (a s)")[:, t * TP:(t + 1) * TP],
                                     mats[:, M_OUT, :], start=True, stop=True)
                last.then_inc(q["out_mm"], 1)

            def turn_router(g):
                pe.wait_ge(q["xf_ready"], g + 1)
                pe.wait_ge(q["gate_ready"], up_to(g + 2))
                after(pe, q["xfT_ready"], g)
                for t in range(T):
                    last = pe.transpose(feat_tile(4, t), xf[:, t, :], ident[0:TP, 0:TP])
                last.then_inc(q["xf_turned"], 1)

            def router(g):
                pe.wait_ge(q["xfT_ready"], g + 1)
                after(pe, q["logit_ready"], g)
                pe.wait_ge(q["out_read"], up_to(g + 2))
                for t in range(T):
                    last = pe.matmul(ps[0:TP, 6, 256 + t * E:256 + (t + 1) * E], tT[:, t * TP:(t + 1) * TP], route_w[:, 0, :],
                                     start=True, stop=True)
                last.then_inc(q["logit_mm"], 1)

            def emit(i, par):
                use = i // 2 + 1 if isinstance(i, int) else None
                full = has(i, 0, G)

                def chunks(a, b):
                    for c in range(a, b):
                        rows_n = 128 if c < KF else KR
                        last = pe.matmul(ps[:, par, :], wp[0:rows_n, c, :], xs[0:rows_n, par, c, :],
                                         start=(c == 0), stop=(c == KF))
                    return last

                def loaded(k):
                    per = 32 if k == 2 else 16
                    if use is not None:
                        pe.wait_ge(x_in[par][k], per * use)
                    else:
                        pe.wait_ge(x_in[par][k], (i - par) * (per // 2) + per)

                if full:
                    after(pe, q["patch_read"], i - 1)
                    loaded(0)
                    chunks(0, 1)
                if isinstance(i, int) and i == 1:
                    pe.wait_ge(s_in, 16 * len(loads))
                if has(i, 1, G + 1):
                    turn_tokens(i - 1)
                if full:
                    chunks(1, 2)
                if has(i, 3, G + 3):
                    turn_router(i - 3)
                if full:
                    chunks(2, 5)
                if has(i, 3, G + 3):
                    router(i - 3)
                if full:
                    chunks(5, 6)
                    loaded(1)
                    chunks(6, 10)
                if has(i, 1, G + 1):
                    turn_norm(i - 1)
                if full:
                    chunks(10, 12)
                    loaded(2)
                if has(i, 1, G + 1):
                    project(i - 1)
                if full:
                    chunks(12, 19).then_inc(q["patch_mm"], 1)
                if has(i, 1, G + 1):
                    project_out(i - 1)

            steps(pe, emit, P1_FIRST, P1_INNER, P1_LAST)

        def p1_scalar(act):
            q = p1

            def emit(i, par):
                if has(i, 1, G + 1):
                    g = i - 1
                    act.wait_ge(q["tok_turned"], g + 1)
                    act.activation(h_tok[:, bass.ts(g, T), :], tok_psum(2), ACT.Copy).then_inc(q["h_saved"], 1)
                if has(i, 3, G + 3):
                    g = i - 3
                    act.wait_ge(q["xf_turned"], g + 1)
                    after(act, q["logit_mm"], g)
                    for k, (o, n) in enumerate(SPLIT):
                        last = act.activation(tT[:, o:o + n], ps[:, 4 + k, 0:n], ACT.Copy)
                    last.then_inc(q["xfT_ready"], 1)
                    last = act.activation(xf_all[:, bass.ts(g, T), :], xf[:, :, :], ACT.Copy)
                    last.then_inc(q["xfT_kept"], 1)
                if has(i, 1, G + 1):
                    g = i - 1
                    act.wait_ge(q["norm_turned"], g + 1)
                    after(act, q["zg_mm"], g)
                    for k, (o, n) in enumerate(SPLIT):
                        last = act.activation(xT[:, o:o + n], ps[:, 4 + k, 0:n], ACT.Copy)
                    last.then_inc(q["normT_ready"], 1)
                    act.wait_ge(q["zg_mm"], g + 1)
                    after(act, q["bz_ready"], g)
                    for k, (o, n) in enumerate(SPLIT):
                        last = act.activation(gate[:, o:o + n], ps[:, 4 + k, 0:n], ACT.Sigmoid,
                                              bias=cols[:, C_BG:C_BG + 1])
                    last.then_inc(q["gate_ready"], 1)

            steps(act, emit, P1_FIRST, P1_INNER, P1_LAST)

        def shrink(dve, g):
            q = p1
            n = SHRINK * g

            def then(ins, k):
                ins.then_inc(q["shrink_step"], 1)
                dve.wait_ge(q["shrink_step"], n + k)

            then(dve.tensor_reduce(largest[:, :], y[:, :, :], AX.X, ALU.max, apply_absolute_value=True), 1)
            then(dve.tensor_scalar(largest[:, :], largest[:, :], 1.0, None, ALU.max), 2)
            then(dve.reciprocal(shrunk[:, :], largest[:, :]), 3)
            dve.tensor_tensor(y[:, :, :], y[:, :, :], shrunk[:, :].unsqueeze(2).broadcast_to([TP, T, D]), ALU.mult)
            dve.tensor_scalar(limit[:, :], shrunk[:, :], 2.0 ** 64, 1e12, ALU.mult, ALU.min)
            then(dve.scalar_tensor_tensor(out=eps_shrunk[:, :], in0=shrunk[:, :], scalar=EPS, in1=shrunk[:, :],
                                          op0=ALU.mult, op1=ALU.mult), 4)
            dve.tensor_tensor(limit2[:, :], limit[:, :], limit[:, :], ALU.mult)
            then(dve.tensor_scalar(eps_shrunk2[:, :], eps_shrunk[:, :], 1e-30, None, ALU.max), 5)

        def judge(dve, g):
            q = p1
            mv, rstd = norm_tiles[1][1], norm_tiles[1][3]
            n = SHRINK * g
            dve.wait_ge(n_out["rstd_ready"], 2 * g + 1)
            dve.scalar_tensor_tensor(out=in_range[:, :], in0=mv[:, :, 1], scalar=float(D), in1=limit2[:, :],
                                     op0=ALU.mult, op1=ALU.is_lt).then_inc(q["shrink_step"], 1)
            dve.wait_ge(q["shrink_step"], n + 6)
            dve.tensor_tensor(kept[:, :], rstd[:, :], in_range[:, :], ALU.mult).then_inc(q["shrink_step"], 1)
            dve.wait_ge(q["shrink_step"], n + SHRINK)

        def p1_vector(dve):
            q = p1

            def emit(i, par):
                has1, has2, has3 = has(i, 1, G + 1), has(i, 2, G + 2), has(i, 3, G + 3)
                if has1:
                    g = i - 1
                    stand(dve, q["h_saved"], g + 1)
                    norm_stats(dve, n_in, h_tok[:, bass.ts(g, T), :], g + 1)
                if has2:
                    g = i - 2
                    dve.wait_ge(q["out_mm"], g + 1)
                    dve.wait_ge(q["xb_ready"], g + 1)
                    for a, b in ((0, 4), (4, 5)):
                        last = dve.tensor_tensor(y[:, a:b, :], out_tiles(a, b), xb[:, a:b, :], ALU.add)
                    last.then_inc(q["out_read"], 1)
                    dve.wait_ge(q["out_read"], g + 1)
                    shrink(dve, g)
                    norm_stats(dve, n_out, y, 2 * g + 1)
                if has1:
                    g = i - 1
                    after(dve, q["norm_turned"], g)
                    after(dve, q["xb_ready"], g)
                    norm_apply(dve, n_in, xn[:, 0], h_tok[:, bass.ts(g, T), :], g + 1).then_inc(q["norm_ready"], 1)
                if has2:
                    g = i - 2
                    judge(dve, g)
                    after(dve, q["xf_turned"], g)
                    after(dve, q["xfT_kept"], g)
                    norm_apply(dve, n_out, xf, y, 2 * g + 1, r=kept).then_inc(q["y_ready"], 1)
                    dve.wait_ge(q["y_ready"], g + 1)
                    dve.tensor_tensor(y[:, :, :], xf[:, :, :],
                                      rows[:, R_GAMMA:R_GAMMA + 1, :].broadcast_to([TP, T, D]), ALU.mult)\
                       .then_inc(q["scaled_ready"], 1)
                    dve.wait_ge(q["scaled_ready"], g + 1)
                    dve.wait_ge(q["hb_ready"], g + 1)
                    ht = h_tok[:, bass.ts(g, T), :]
                    dve.tensor_tensor(ht, y[:, :, :], hb[:, :, :], ALU.add).then_inc(q["h_ready"], 1)
                    stand(dve, q["h_ready"], g + 1)
                    norm_stats(dve, n_out, ht, 2 * g + 2)
                if has1:
                    g = i - 1
                    dve.wait_ge(q["zg_mm"], g + 1)
                    for k, (o, n) in enumerate(SPLIT):
                        dve.tensor_scalar(bz[:, o:o + n], ps[:, 2 + k, 0:n], cols[:, C_BZ:C_BZ + 1],
                                          cols[:, C_B:C_B + 1], ALU.add, ALU.mult)
                    dve.wait_ge(q["gate_ready"], g + 1)
                    dve.tensor_scalar(ga[:, :], gate[:, :], cols[:, C_A:C_A + 1], None, ALU.mult)\
                       .then_inc(q["bz_ready"], 1)
                    dve.wait_ge(q["bz_ready"], g + 1)
                    after(dve, q["out_mm"], g)
                    for b in range(GI):
                        prev = state[:, (b - 1) % GI, :]
                        if b:
                            dve.wait_ge(q["state_ready"], GI * g + b)
                        dve.tensor_tensor(carried[:, :], ga[:, b * S:(b + 1) * S], prev, ALU.mult)\
                           .then_inc(q["carry_ready"], 1)
                        dve.wait_ge(q["carry_ready"], GI * g + b + 1)
                        dve.tensor_tensor(state[:, b, :], carried[:, :], bz[:, b * S:(b + 1) * S], ALU.add)\
                           .then_inc(q["state_ready"], 1)
                if has2:
                    g = i - 2
                    norm_apply(dve, n_out, xf, h_tok[:, bass.ts(g, T), :], 2 * g + 2).then_inc(q["xf_ready"], 1)
                if has3:
                    g = i - 3
                    dve.wait_ge(q["logit_mm"], g + 1)
                    dve.tensor_tensor(logits[:, bass.ts(g, T), :],
                                      ps[0:TP, 6, 256:256 + T * E].rearrange("p (t e) -> p t e", e=E),
                                      route_b[:, 0:1, :].broadcast_to([TP, T, E]), ALU.add)\
                       .then_inc(q["logit_ready"], 1)
                if has(i, 0, G):
                    g = i
                    dve.wait_ge(q["patch_mm"], g + 1)
                    after(dve, q["tok_turned"], g)
                    dve.scalar_tensor_tensor(out=tokT[:, :, 1:S],
                                             in0=ps[:, par, :].rearrange("p (a s) -> p a s", s=NP),
                                             scalar=cols[:, C_TOKB:C_TOKB + 1],
                                             in1=posT[:, 1:S].unsqueeze(1).broadcast_to([D, GI, NP]),
                                             op0=ALU.add, op1=ALU.mult).then_inc(q["patch_read"], 1)

            dve.wait_ge(s_in, 16 * len(loads))
            dve.memset(state[:, :, :], 0.0)
            dve.tensor_copy(maskb[:, :], maskf[:, :])
            dve.tensor_tensor(tokT[:, 0, 0:1], cols[:, C_CLS:C_CLS + 1], posT[:, 0:1], ALU.mult).then_inc(s_const, 1)
            dve.wait_ge(s_const, 1)
            dve.tensor_copy(tokT[:, 1:GI, 0:1], tokT[:, 0:1, 0:1].broadcast_to([D, GI - 1, 1])).then_inc(s_const, 1)
            dve.wait_ge(s_const, 2)
            steps(dve, emit, P1_FIRST, P1_INNER, P1_LAST)

        def p1_gpsimd(pool):
            q = p1

            def emit(i, par):
                if has(i, 1, G + 1):
                    norm_spread(pool, n_in, i)
                if has(i, 2, G + 2):
                    norm_spread(pool, n_out, 2 * (i - 2) + 1, eps_shrunk2)
                if has(i, 1, G + 1):
                    g = i - 1
                    pool.wait_ge(q["norm_ready"], g + 1)
                    after(pool, q["out_read"], g)
                    pool.tensor_tensor(xb[:, :, :], xn[:, 0], rows[:, R_BOUT:R_BOUT + 1, :].broadcast_to([TP, T, D]),
                                       ALU.add).then_inc(q["xb_ready"], 1)
                if has(i, 2, G + 2):
                    norm_spread(pool, n_out, 2 * (i - 2) + 2)
                if has(i, 1, G + 1):
                    g = i - 1
                    after(pool, q["h_ready"], g)
                    pool.tensor_tensor(hb[:, :, :], h_tok[:, bass.ts(g, T), :],
                                       rows[:, R_BETA:R_BETA + 1, :].broadcast_to([TP, T, D]),
                                       ALU.add).then_inc(q["hb_ready"], 1)

            steps(pool, emit, P1_FIRST, P1_INNER, P1_LAST)

        rs = [{n: sem(f"route{k}_{n}") for n in ("step", "gap", "exp", "chosen", "counted", "slots_ready")} for k in range(2)]

        def route_vector(dve, layer):
            q = rs[layer]
            count = [0]

            def then(ins):
                count[0] += 1
                ins.then_inc(q["step"], 1)
                dve.wait_ge(q["step"], count[0])

            def wide(v):
                return v[:, :].unsqueeze(2).broadcast_to([TP, NT, E])

            idw = ids[:, :].unsqueeze(1).broadcast_to([TP, NT, E])
            BIG = 64.0

            def pick(of, top, out, first):
                then(dve.tensor_reduce(top[:, :], of[:, :, :], AX.X, ALU.max))
                then(dve.tensor_tensor(rt[0], of[:, :, :], wide(top), ALU.is_equal))
                then(dve.scalar_tensor_tensor(out=rt[1], in0=rt[0], scalar=-BIG, in1=idw, op0=ALU.mult, op1=ALU.add))
                then(dve.tensor_reduce(first[:, :], rt[1], AX.X, ALU.min))
                then(dve.tensor_tensor(out, rt[1], wide(first), ALU.is_equal))

            pick(logits, rv[0], rt[2], rv[1])
            if layer == 0:
                then(dve.scalar_tensor_tensor(out=rt[3], in0=rt[2], scalar=-3e38, in1=logits[:, :, :],
                                              op0=ALU.mult, op1=ALU.add))
                pick(rt[3], rv[2], rt[4], rv[3])
                dve.tensor_tensor(rv[4], rv[2], rv[0], ALU.subtract).then_inc(q["gap"], 1)
                then(dve.tensor_tensor(rt[5], rt[2], rt[4], ALU.add))
                dve.wait_ge(q["exp"], 1)
                then(dve.tensor_scalar(rv[6], rv[5], 1.0, None, ALU.add))
                then(dve.reciprocal(weight[:, 0, :], rv[6]))
                dve.tensor_tensor(weight[:, 1, :], rv[5], weight[:, 0, :], ALU.mult)
            else:
                dve.tensor_tensor(rt[3], logits[:, :, :], wide(rv[0]), ALU.subtract).then_inc(q["gap"], 1)
                dve.wait_ge(q["exp"], 1)
                then(dve.tensor_reduce(rv[6], rt[4], AX.X, ALU.add))
                dve.reciprocal(weight[:, 0, :], rv[6])
                then(dve.tensor_copy(rt[5], rt[2]))
            dve.sem_inc(q["chosen"], 1)

            dve.wait_ge(q["counted"], 1)
            then(dve.tensor_copy(et[0], ps[0:TP, 1, 0:NT * E].rearrange("p (t e) -> p e t", e=E)))
            for e in range(E):
                last = dve.tensor_tensor_scan(et[1][:, e, :], ones[:, 0:NT], et[0][:, e, :], 0.0, ALU.mult, ALU.add)
            then(last)
            then(dve.tensor_scalar(counted_i[:, 0, :], et[1][:, :, NT - 1], float(ET - 1), None, ALU.add))
            then(dve.tensor_single_scalar(counted_i[:, 1, :], counted_i[:, 0, :], ET.bit_length() - 1,
                                          ALU.arith_shift_right))
            then(dve.tensor_copy(re[0], counted_i[:, 1, :]))
            then(dve.tensor_tensor_scan(re[1], ones[:, 0:E], re[0], 0.0, ALU.mult, ALU.add))
            then(dve.tensor_tensor(re[2], re[1], re[0], ALU.subtract))
            then(dve.tensor_scalar(re[3], re[2], float(ET), None, ALU.mult))
            then(dve.tensor_tensor(et[2], et[1], et[0], ALU.subtract))
            then(dve.tensor_tensor(et[0], et[2], re[3].unsqueeze(2).broadcast_to([TP, E, NT]), ALU.add))
            then(dve.tensor_tensor(rt[6], ps[0:TP, 0, 0:NT * E].rearrange("p (t e) -> p t e", e=E),
                                   et[0].rearrange("p e t -> p t e"), ALU.add))
            for k in range(TOP[layer]):
                then(dve.tensor_tensor(rt[7], rt[6], rt[2 + 2 * k], ALU.mult))
                then(dve.tensor_reduce(rv[k], rt[7], AX.X, ALU.add))
                then(dve.tensor_copy(slot[:, k, :], rv[k]))
            N = NE[layer]
            then(dve.tensor_tensor(past[:, 0:N, :], re[1][0:1, :].unsqueeze(1).broadcast_to([1, N, E]),
                                   tile_no[:, 0:N].unsqueeze(2).broadcast_to([1, N, E]), ALU.is_le))
            then(dve.tensor_reduce(past_n[:, 0:N], past[:, 0:N, :], AX.X, ALU.add))
            dve.tensor_scalar(tile_expert[:, 0:N], past_n[:, 0:N], float(E - 1), None, ALU.min)\
               .then_inc(q["slots_ready"], 1)

        def route_tensor(pe, layer):
            q = rs[layer]
            pe.wait_ge(q["chosen"], 1)
            chosen = rt[5].rearrange("p t e -> p (t e)")
            pe.matmul(ps[0:TP, 0, 0:NT * E], later[:, :], chosen, start=True, stop=True)
            pe.matmul(ps[0:TP, 1, 0:NT * E], ones[:, :], chosen, start=True, stop=True).then_inc(q["counted"], 1)

        def route_gpsimd(pool, layer):
            q = rs[layer]
            pool.wait_ge(q["slots_ready"], 1)
            pool.wait_ge(s_clear, 16 * (NE[0] // 4))
            for t in range(NT):
                for k in range(TOP[layer]):
                    pool.indirect_dma_start(out=d["slots"],
                                            out_offset=bass.IndirectOffsetOnAxis(ap=slot[:, k, t:t + 1], axis=0),
                                            in_=xf_all[:, t, :], in_offset=None).then_inc(s_scattered, 16)
            pool.wait_ge(s_scattered, 16 * NT * sum(TOP[:layer + 1]))

        def route_scalar(act, layer):
            q = rs[layer]
            act.wait_ge(q["gap"], 1)
            if layer == 0:
                act.activation(rv[5], rv[4], ACT.Exp).then_inc(q["exp"], 1)
            else:
                act.activation(rt[4], rt[3], ACT.Exp).then_inc(q["exp"], 1)

        ex = {n: sem("ex_" + n) for n in ("rows_turned", "rowsT_ready", "up_mm", "silu_ready", "hid_ready", "down_mm",
                                          "out_ready")}
        tile_in = [sem(f"tile_in{r}") for r in range(RING)]
        pack_in = [sem(f"pack_in{r}") for r in range(RING // PACK)]
        pack_out = [sem(f"pack_out{r}") for r in range(RING // PACK)]
        got_in = [sem(f"got_in{g}") for g in range(G)]

        def tiles(eng, emit, layer, start):
            N = NE[layer]
            for t in range(start, RING):
                emit(t, t % RING)
            with eng.Fori(1, N // RING - 1) as k:
                for r in range(RING):
                    emit(RING * k + r, r)
            for t in range(N - RING, N):
                emit(t, t % RING)

        def within(t, layer):
            return not isinstance(t, int) or 0 <= t < NE[layer]

        def ring_count(t, r, base, per):
            if isinstance(t, int):
                return per * ((t + base) // RING + 1)
            return (t - r) * (per // RING) + (per * (base // RING) + per)

        def expert_of(eng, t):
            return eng.value_load(tile_expert[0:1, bass.ds(t, 1)], min_val=0, max_val=E - 1)

        def experts_sync(sp, layer):
            q = ex
            base = NE[0] * layer
            up = d[f"up{layer}"]

            def emit(t, r):
                e = expert_of(sp, t)
                after(sp, q["hid_ready"], t + (base - RING + 1))
                sp.dma_start(up_w[:, r, :], up[bass.ds(e, 1)].squeeze(0)).then_inc(tile_in[r], 16)

            for t in range(RING):
                emit(t, t)
            with sp.Fori(1, NE[layer] // RING) as k:
                for r in range(RING):
                    emit(RING * k + r, r)

        def experts_gpsimd(pool, layer):
            q = ex
            base = NE[0] * layer
            N = NE[layer]
            results = d[f"results{layer}"]

            def pack(array, t):
                return array[bass.ds(t * ET, PACK * ET), :].rearrange("(n p) d -> p n d", p=ET)

            def fetch(t, r):
                after(pool, q["rows_turned"], t + (base - RING + PACK))
                pool.dma_start(rows_in[:, r:r + PACK, :], pack(d["slots"], t)).then_inc(pack_in[r // PACK], 16)

            def store(t, r):
                pool.wait_ge(q["out_ready"], t + (base + PACK))
                pool.dma_start(pack(results, t), rows_out[:, r:r + PACK, :]).then_inc(pack_out[r // PACK], 16)

            for r in range(0, RING, PACK):
                fetch(r, r)
            with pool.Fori(0, N // RING - 1) as k:
                for r in range(0, RING, PACK):
                    fetch(RING * k + (RING + r), r)
                    store(RING * k + r, r)
            for r in range(0, RING, PACK):
                store(N - RING + r, r)

        def experts_tensor(pe, layer):
            q = ex
            base = NE[0] * layer
            U = UNITS[layer]

            def turn_rows(t, r):
                pe.wait_ge(pack_in[r // PACK], ring_count(t, r, base, 16))
                after(pe, q["rowsT_ready"], t + (base - 1))
                pe.transpose(ps[:, 6 + r % 2, 0:ET], rows_in[:, r, :], ident[:, :]).then_inc(q["rows_turned"], 1)

            def up(t, r):
                pe.wait_ge(tile_in[r], ring_count(t, r, base, 16))
                pe.wait_ge(q["rowsT_ready"], t + (base + 1))
                after(pe, q["hid_ready"], t + (base - 1))
                for f in range(4):
                    bank, at = (2 * (f // 2), f % 2) if layer == 0 else (0, f)
                    last = pe.matmul(ps[:, bank + r % 2, at * ET:(at + 1) * ET], up_w[:, r, f * D:(f + 1) * D],
                                     rowsT[:, r % 2, :], start=True, stop=True)
                last.then_inc(q["up_mm"], 1)

            def down(t, r, e):
                pe.wait_ge(q["hid_ready"], t + (base + 1))
                after(pe, q["out_ready"], t + (base - 1))
                for c in range(U):
                    last = pe.matmul(ps[:, 4 + r % 2, 0:D], hid[:, r % 2, c, :],
                                     down_w[:, bass.ds(e, 1), c, :].squeeze(1), start=(c == 0), stop=(c == U - 1))
                last.then_inc(q["down_mm"], 1)

            def emit(t, r):
                if within(t + 2, layer):
                    turn_rows(t + 2, (r + 2) % RING)
                if within(t + 1, layer):
                    up(t + 1, (r + 1) % RING)
                if within(t, layer):
                    down(t, r, expert_of(pe, t))

            tiles(pe, emit, layer, -2)

        def experts_scalar(act, layer):
            q = ex
            base = NE[0] * layer
            act.activation(warm[:, :], ident[0:1, 0:1], ACT.Silu if layer == 0 else ACT.Gelu_apprx_tanh)

            def emit(t, r):
                if layer == 0 and within(t + 2, layer):
                    n, p = t + 2, r % 2
                    act.wait_ge(q["rows_turned"], n + (base + 1))
                    act.activation(rowsT[:, p, :], ps[:, 6 + p, 0:ET], ACT.Copy).then_inc(q["rowsT_ready"], 1)
                if within(t + 1, layer):
                    n, r1 = t + 1, (r + 1) % RING
                    act.wait_ge(q["up_mm"], n + (base + 1))
                    if layer == 0:
                        for c in range(2):
                            last = act.activation(silu_h[:, r1 % 2, c * ET:(c + 1) * ET],
                                                  ps[:, r1 % 2, c * ET:(c + 1) * ET], ACT.Silu,
                                                  bias=up_w[:, r1, 4 * D + c:4 * D + c + 1])
                        last.then_inc(q["silu_ready"], 1)
                    else:
                        for c in range(4):
                            last = act.activation(hid[:, r1 % 2, c, :], ps[:, r1 % 2, c * ET:(c + 1) * ET],
                                                  ACT.Gelu_apprx_tanh, bias=up_w[:, r1, 4 * D + c:4 * D + c + 1])
                        last.then_inc(q["hid_ready"], 1)

            tiles(act, emit, layer, -2)

        def experts_vector(dve, layer):
            q = ex
            base = NE[0] * layer

            def emit(t, r):
                if layer == 1 and within(t + 2, layer):
                    n, p = t + 2, r % 2
                    dve.wait_ge(q["rows_turned"], n + (base + 1))
                    dve.tensor_copy(rowsT[:, p, :], ps[:, 6 + p, 0:ET]).then_inc(q["rowsT_ready"], 1)
                if layer == 0 and within(t + 1, layer):
                    n, r1 = t + 1, (r + 1) % RING
                    dve.wait_ge(q["silu_ready"], n + 1)
                    for c in range(2):
                        last = dve.scalar_tensor_tensor(
                            out=hid[:, r1 % 2, c, :], in0=ps[:, 2 + r1 % 2, c * ET:(c + 1) * ET],
                            scalar=up_w[:, r1, 4 * D + 2 + c:4 * D + 3 + c],
                            in1=silu_h[:, r1 % 2, c * ET:(c + 1) * ET], op0=ALU.add, op1=ALU.mult)
                    last.then_inc(q["hid_ready"], 1)
                if within(t, layer):
                    dve.wait_ge(q["down_mm"], t + (base + 1))
                    if not isinstance(t, int) or t + base >= RING:
                        dve.wait_ge(pack_out[r // PACK], ring_count(t, r, base - RING, 16))
                    dve.tensor_tensor(rows_out[:, r, :], ps[:, 4 + r % 2, 0:D],
                                      bias2[:, bass.ds(expert_of(dve, t), 1), :].squeeze(1), ALU.add).then_inc(q["out_ready"], 1)

            tiles(dve, emit, layer, -2)

        def all_results(pool, layer):
            for signal in pack_out:
                pool.wait_ge(signal, 16 * sum(NE[:layer + 1]) // RING)

        def gather(pool, layer, dst, index, signal):
            pool.indirect_dma_start(out=dst, out_offset=None, in_=d[f"results{layer}"],
                                    in_offset=bass.IndirectOffsetOnAxis(ap=index, axis=0)).then_inc(signal, 16)

        def last_gpsimd(pool):
            all_results(pool, 1)
            for g in range(G):
                for t in range(g * T, (g + 1) * T):
                    gather(pool, 1, got_all[:, t, :], slot[:, 0, t:t + 1], got_in[g])

        def last_count(g):
            return 16 * T * (1 + (2 * G // 2 if g < 2 else 0))

        def last_vector(dve):
            for g in range(G):
                dve.wait_ge(got_in[g], last_count(g))
                for t in range(g * T, (g + 1) * T):
                    last = dve.scalar_tensor_tensor(out=h_tok[:, t, :], in0=got_all[:, t, :],
                                                    scalar=weight[:, 0, t:t + 1], in1=h_tok[:, t, :],
                                                    op0=ALU.mult, op1=ALU.add)
                last.then_inc(s_last, 1)

        def last_sync(sp):
            for g in range(G):
                sp.wait_ge(s_last, g + 1)
                sp.dma_start(d["out"][:, g * T:(g + 1) * T, :], h_tok[:, g * T:(g + 1) * T, :]).then_inc(s_out, 16)
            sp.wait_ge(s_out, 16 * G)

        JOBS = ("f0", "f1", "g2", "t0", "t1", "k0", "k1", "q0", "q1", "v0", "v1", "g0", "g1")
        JOB_SLOT = {"f": 1, "g2": 2, "t": 3, "k": 4, "q": 5, "v": 6, "g": 7}

        KEYS = {5: ((0, 0, 5),), 6: ((0, 5, H), (1, 0, 2)), 7: ((1, 2, H),)}

        def job_slot(j):
            return JOB_SLOT[j if j == "g2" else j[0]]
        at_ = {n: sem("at_" + n) for n in
               ("stats_ready mean_ready spread_ready rstd_ready norm_ready keysM_ready scores_mm peak_ready "
                "diff_ready prob_ready turn_mm probT_ready av_mm rden_ready o_ready o_turned outT_ready "
                "last_turned last_kept combined index_ready pool_ready y_ready y2_ready ones_ready t_ready t_kept").split()}
        at_["full"] = {j: sem(f"full_{j}") for j in JOBS}
        at_["empty"] = {j: sem(f"empty_{j}") for j in JOBS}
        at_["tiles"] = norm_tiles[0]
        fin = {n: sem("fin_" + n) for n in ("stats_ready", "mean_ready", "spread_ready", "rstd_ready")}
        fin["tiles"] = norm_tiles[1]

        def job_group(i, j):
            return i + 1 if j[0] in "tkqv" else i - (2 if j == "g2" else 1)

        def job_list(i, layer):
            return [j for j in JOBS if (layer or j[0] != "g") and has(job_group(i, j), 0, G)]

        def job_bank(j):
            return 5 if j[1] == "1" else 7

        def job_before(i, j, layer):
            def same_bank(i):
                return [k for k in job_list(i, layer) if job_bank(k) == job_bank(j)]

            here = same_bank(i)
            at = here.index(j)
            if at:
                return here[at - 1], job_group(i, here[at - 1])
            if isinstance(i, int):
                if i < 0:
                    return None
                prev = same_bank(i - 1)
            else:
                prev = same_bank(i)
            return (prev[-1], job_group(i - 1, prev[-1])) if prev else None

        AT_FIRST, AT_INNER, AT_LAST = (-1, 2), 4, (G + 1, G + 2)

        def img(i, m, r):
            n = GI * i + (m + r)
            return (not isinstance(i, int) or 0 <= n < B), n

        def got_count(g, gp):
            per = 16 * 2 * T
            return per * (g // 2 + 1) if isinstance(g, int) else (g - gp) * (per // 2) + per

        def turned(h, n=1):
            return ps[0:S, 4, h * S:(h + n) * S] if h < H - 1 else ps[0:S, 6, 384:384 + S]

        def attention_tensor(pe, layer):
            q = at_
            L, N0 = G * layer, B * layer
            M = M_ATT + 4 * layer

            def take(i, j):
                before = job_before(i, j, layer)
                if before:
                    pe.wait_ge(q["empty"][before[0]], before[1] + (1 + (L if before[0][0] != "g" else 0)))

            def job(i, j, par):
                g = job_group(i, j)
                gp = 1 - par
                take(i, j)
                h = int(j[1])
                half = slice(h * HALF, (h + 1) * HALF)
                tiles = range(4) if h == 0 else range(4, 5)
                if j[0] == "f":
                    if h == 0:
                        pe.wait_ge(q["outT_ready"], GI * (g + (L + 1)))
                    for t in tiles:
                        last = pe.matmul(ps[0:TP, job_bank(j), t % 4 * D:(t % 4 + 1) * D], outT[:, gp, t * TP:(t + 1) * TP],
                                         mats[:, M + 3, :], start=True, stop=True)
                elif j[0] in "tg" and j != "g2":
                    if h == 0:
                        pe.wait_ge(*((q["norm_ready"], g + (L + 1)) if j[0] == "t" else (q["t_ready"], g + 1)))
                    src = xn[:, gp] if j[0] == "t" else xf[:, :, :]
                    for t in tiles:
                        last = pe.transpose(ps[:, job_bank(j), t % 4 * TP:(t % 4 + 1) * TP], src[:, t, :], ident[0:TP, 0:TP])
                elif j[0] in "kq":
                    if j == "k0":
                        pe.wait_ge(q["empty"]["t1"], g + (L + 1))
                    last = pe.matmul(ps[:, job_bank(j), 0:HALF], mats[:, M + (j[0] == "k"), :], xT[:, half], start=True, stop=True)
                elif j[0] == "v":
                    for a in range(GI // 2):
                        b = h * (GI // 2) + a
                        last = pe.matmul(ps[0:S, job_bank(j), a * D:(a + 1) * D], xT[:, b * S:(b + 1) * S], mats[:, M + 2, :],
                                         start=True, stop=True)
                else:
                    pe.wait_ge(q["empty"]["g1"], g + 1)
                    for t in range(T):
                        last = pe.matmul(ps[0:TP, job_bank(j), t * E:(t + 1) * E], tT[:, t * TP:(t + 1) * TP],
                                         route_w[:, 1, :], start=True, stop=True)
                last.then_inc(q["full"][j], 1)

            def emit(i, par):
                for m in range(GI):
                    ok, n = img(i, m, 1)
                    if ok:
                        p, b = (m + 1) % 2, (m + 1) % GI
                        gp = par if m + 1 < GI else 1 - par
                        g = i if m + 1 < GI else i + 1
                        if b in (0, GI // 2):
                            pe.wait_ge(q["keysM_ready"], 2 * g + (2 * L + (1 if b == 0 else 2)))
                            pe.wait_ge(q["empty"]["q1"], g + (L + 1))
                        after(pe, q["diff_ready"], n + (N0 - 1))
                        for k in range(2):
                            bank = ps[0:S, 2 * p + k, 0:HALF]
                            if layer == 0:
                                pe.matmul(bank, identb[0:S, 0:S], maskb[:, :], start=True, stop=False)
                            last = pe.matmul(bank, qT[:, gp, b * S:(b + 1) * S],
                                             keysM[:, gp, b, 4 * k:4 * k + 4, :].rearrange("p h s -> p (h s)"),
                                             start=(layer == 1), stop=True)
                        last.then_inc(q["scores_mm"], 1)
                    ok, n = img(i, m, -1)
                    if ok:
                        p, b = (m - 1) % 2, (m - 1) % GI
                        gp = par if m else 1 - par
                        pe.wait_ge(q["probT_ready"], n + (N0 + 1))
                        pe.wait_ge(q["last_kept"], n + (N0 + 1))
                        after(pe, q["outT_ready"], n + N0)
                        for h in range(H):
                            last = pe.matmul(ps[0:S, 6, h * HA:(h + 1) * HA], probT[:, p, h, :], vals[:, gp, b, h, :],
                                             start=True, stop=True)
                        last.then_inc(q["av_mm"], 1)
                    ok, n = img(i, m, 0)
                    if ok:
                        pe.wait_ge(q["prob_ready"], n + (N0 + 1))
                        after(pe, q["probT_ready"], n + N0)
                        for h in range(H - 1):
                            last = pe.transpose(turned(h), prob[:, m % 2, h, :], ident[0:S, 0:S])
                        last.then_inc(q["turn_mm"], 1)
                    for j in job_list(i, layer):
                        if job_slot(j) == m:
                            job(i, j, par)
                    ok, n = img(i, m, -1)
                    if ok:
                        pe.wait_ge(q["o_ready"], n + (N0 + 1))
                        pe.transpose(ps[:, 6, 256:256 + S], o_tok[:, (m - 1) % 2, :], ident[0:S, 0:S])\
                          .then_inc(q["o_turned"], 1)
                    ok, n = img(i, m, 0)
                    if ok:
                        pe.transpose(turned(H - 1), prob[:, m % 2, H - 1, :], ident[0:S, 0:S])\
                          .then_inc(q["last_turned"], 1)

            steps(pe, emit, AT_FIRST, AT_INNER, AT_LAST[layer])

        def attention_scalar(act, layer):
            q = at_
            L, N0 = G * layer, B * layer
            C = C_ATT + 3 * layer

            def job(i, j, par):
                g = job_group(i, j)
                gp = 1 - par
                h = int(j[1])
                half = slice(h * HALF, (h + 1) * HALF)
                tok = slice(0, 4 * TP) if h == 0 else slice(4 * TP, GT)
                nt = 4 if h == 0 else 1
                act.wait_ge(q["full"][j], g + (1 if j[0] == "g" else L + 1))
                if j[0] == "t":
                    last = act.activation(xT[:, tok], ps[:, job_bank(j), 0:nt * TP], ACT.Copy)
                elif j[0] == "k":
                    after(act, q["keysM_ready"], 2 * g + 2 * L)
                    last = act.activation(keysT[:, half], ps[:, job_bank(j), 0:HALF], ACT.Identity, bias=cols[:, C + 1:C + 2])
                elif j[0] == "q":
                    last = act.activation(qT[:, gp, half], ps[:, job_bank(j), 0:HALF], ACT.Identity, bias=cols[:, C:C + 1])
                elif j[0] == "v":
                    last = act.activation(vals[:, gp, 4 * h:4 * h + 4, :, 0:DK],
                                          ps[0:S, job_bank(j), :].rearrange("p (a h k) -> p a h k", a=4, h=H), ACT.Copy)
                else:
                    last = act.activation(tT[:, tok], ps[:, job_bank(j), 0:nt * TP], ACT.Copy)
                    if h:
                        act.activation(xf_all[:, bass.ts(g, T), :], xf[:, :, :], ACT.Copy).then_inc(q["t_kept"], 1)
                last.then_inc(q["empty"][j], 1)

            def emit(i, par):
                for m in range(GI):
                    ok, n = img(i, m, 0)
                    if ok:
                        act.wait_ge(q["turn_mm"], n + (N0 + 1))
                        act.activation(probT[:, m % 2, 0:H - 1, :].rearrange("p h s -> p (h s)"), turned(0, H - 1),
                                       ACT.Copy).then_inc(q["probT_ready"], 1)
                    ok, n = img(i, m, -1)
                    if ok:
                        gp = par if m else 1 - par
                        b = (m - 1) % GI
                        act.wait_ge(q["o_turned"], n + (N0 + 1))
                        if img(i, m, 0)[0]:
                            act.wait_ge(q["last_turned"], n + (N0 + 2))
                        act.activation(outT[:, gp, b * S:(b + 1) * S], ps[:, 6, 256:256 + S], ACT.Identity,
                                       bias=cols[:, C + 2:C + 3]).then_inc(q["outT_ready"], 1)
                    ok, n = img(i, m, 0)
                    if ok:
                        act.wait_ge(q["last_turned"], n + (N0 + 1))
                        act.activation(probT[:, m % 2, H - 1, :], turned(H - 1), ACT.Copy).then_inc(q["last_kept"], 1)
                    ok, n = img(i, m, 1)
                    if ok:
                        p = (m + 1) % 2
                        act.wait_ge(q["diff_ready"], n + (N0 + 1))
                        act.activation(prob[:, p, :, :], diff[:, p, :, :], ACT.Exp, scale=DK ** -0.5)\
                           .then_inc(q["prob_ready"], 1)
                    for j in job_list(i, layer):
                        if job_slot(j) == m and j[0] in "tkqvg" and j != "g2":
                            job(i, j, par)

            steps(act, emit, AT_FIRST, AT_INNER, AT_LAST[layer])

        def attention_vector(dve, layer):
            q = at_
            L, N0 = G * layer, B * layer

            def combine(g, gp, k):
                dve.wait_ge(got_in[gp], got_count(g, gp))
                after(dve, q["combined"], 2 * g + k)
                for t in range(T):
                    ht = h_tok[:, bass.ds(g * T + t, 1), :].squeeze(1)
                    last = dve.scalar_tensor_tensor(out=ht, in0=got[:, gp, k, t, :],
                                                    scalar=weight[:, k, bass.ds(g * T + t, 1)], in1=ht,
                                                    op0=ALU.mult, op1=ALU.add)
                last.then_inc(q["combined"], 1)

            def emit(i, par):
                nxt, prv = has(i + 1, 0, G), has(i - 1, 0, G)
                gp = 1 - par
                for m in range(GI):
                    ok, n = img(i, m, 1)
                    if ok:
                        p = (m + 1) % 2
                        banks = ps[0:S, 2 * p:2 * p + 2, 0:HALF].rearrange("p a (h s) -> p a h s", s=S)
                        dve.wait_ge(q["scores_mm"], n + (N0 + 1))
                        dve.tensor_reduce(peak[:, p, :].rearrange("p (a h) -> p a h", a=2), banks, AX.X, ALU.max)\
                           .then_inc(q["peak_ready"], 1)
                    ok, n = img(i, m, -1)
                    if ok:
                        av = ps[0:S, 6, 0:H * HA].rearrange("p (h a) -> p h a", a=HA)
                        dve.wait_ge(q["av_mm"], n + (N0 + 1))
                        dve.reciprocal(rden[:, :], av[:, :, DK]).then_inc(q["rden_ready"], 1)
                        dve.wait_ge(q["rden_ready"], n + (N0 + 1))
                        after(dve, q["o_turned"], n + (N0 - 1))
                        dve.tensor_tensor(o_tok[:, (m - 1) % 2, :].rearrange("p (h k) -> p h k", h=H), av[:, :, 0:DK],
                                          rden[:, :].unsqueeze(2).broadcast_to([S, H, DK]), ALU.mult)\
                           .then_inc(q["o_ready"], 1)
                    ok, n = img(i, m, 1)
                    if ok:
                        dve.wait_ge(q["peak_ready"], n + (N0 + 1))
                        after(dve, q["prob_ready"], n + (N0 - 1))
                        dve.tensor_tensor(diff[:, p, :, :].rearrange("p (a h) s -> p a h s", a=2), banks,
                                          peak[:, p, :].rearrange("p (a h) -> p a h", a=2).unsqueeze(3)
                                          .broadcast_to([S, 2, 4, S]), ALU.subtract).then_inc(q["diff_ready"], 1)
                    if m == 0 and nxt:
                        if layer == 0:
                            stand(dve, q["combined"], 2 * i + 4)
                        norm_sums(dve, q, h_tok[:, bass.ts(i + 1, T), :])
                    if m == 1 and nxt:
                        norm_means(dve, q, i + (L + 2))
                    if m == 2 and nxt:
                        g = i + 1
                        if layer == 1:
                            after(dve, q["pool_ready"], g + (L - 1))
                        after(dve, q["full"]["t1"], g + (L - 1))
                        norm_apply(dve, q, xn[:, gp], h_tok[:, bass.ts(g, T), :], g + (L + 1)).then_inc(q["norm_ready"], 1)
                    if m == 1 and prv:
                        g = i - 1
                        dve.wait_ge(q["pool_ready"], g + (L + 1))
                        if layer == 1:
                            after(dve, q["t_ready"], g)
                        for h, (a, b) in enumerate(((0, 4), (4, 5))):
                            dve.wait_ge(q["full"][f"f{h}"], g + (L + 1))
                            dst = h_tok[:, bass.ds(g * T + a, b - a), :] if layer == 0 else y[:, a:b, :]
                            bank = ps[0:TP, job_bank(f"f{h}"), 0:(b - a) * D].rearrange("p (t d) -> p t d", d=D)
                            dve.tensor_tensor(dst, bank, hb[:, a:b, :], ALU.add).then_inc(q["empty"][f"f{h}"], 1)
                    if m == 3 and prv and layer == 1:
                        g = i - 1
                        dve.wait_ge(q["empty"]["f1"], g + (L + 1))
                        norm_stats(dve, fin, y, g + 1)
                    if m == 4 and prv and layer == 1:
                        g = i - 1
                        after(dve, q["full"]["g1"], g)
                        after(dve, q["t_kept"], g)
                        norm_apply(dve, fin, xf, y, g + 1).then_inc(q["y_ready"], 1)
                    if nxt:
                        g = i + 1
                        for h, a, b in KEYS.get(m, ()):
                            if a == 0:
                                dve.wait_ge(q["empty"][f"k{h}"], g + (L + 1))
                                after(dve, q["scores_mm"], GI * (g + (L - 1)))
                            for hd in range(a, b):
                                last = dve.tensor_scalar(
                                    keysM[:, gp, 4 * h:4 * h + 4, hd, :],
                                    keysT[:, h * HALF:(h + 1) * HALF].rearrange("p (a s) -> p a s", s=S),
                                    cols[:, C_HEAD + hd:C_HEAD + hd + 1], None, ALU.mult)
                            if b == H:
                                last.then_inc(q["keysM_ready"], 1)
                    if m in (3, 4) and layer == 0 and has(i + 2, 0, G):
                        combine(i + 2, par, m - 3)
                    if m == 2 and has(i - 2, 0, G) and layer == 1:
                        g = i - 2
                        dve.wait_ge(q["full"]["g2"], g + 1)
                        dve.tensor_tensor(logits[:, bass.ts(g, T), :],
                                          ps[0:TP, 7, 0:T * E].rearrange("p (t e) -> p t e", e=E),
                                          route_b[:, 1:2, :].broadcast_to([TP, T, E]), ALU.add)\
                           .then_inc(q["empty"]["g2"], 1)

            if layer == 0:
                combine(0, 0, 0)
                combine(0, 0, 1)
            dve.memset(vals[:, :, :, :, DK:HA].rearrange("p a b h k -> p (a b h) k"), 1.0).then_inc(q["ones_ready"], 1)
            dve.wait_ge(q["ones_ready"], layer + 1)
            steps(dve, emit, AT_FIRST, AT_INNER, AT_LAST[layer])

        def attention_gpsimd(pool, layer):
            q = at_
            L, N0 = G * layer, B * layer

            def fetch_results(g, gp):
                after(pool, q["combined"], 2 * g - 2)
                pool.tensor_copy(slot_now[:, gp, :, :], slot[:, :, bass.ds(g * T, T)]).then_inc(q["index_ready"], 1)
                stand(pool, q["index_ready"], g + 1)
                for k in range(2):
                    for t in range(T):
                        gather(pool, 0, got[:, gp, k, t, :], slot_now[:, gp, k, t:t + 1], got_in[gp])

            def emit(i, par):
                if layer == 0 and has(i + 2, 0, G):
                    fetch_results(i + 2, par)
                if has(i - 1, 0, G):
                    g = i - 1
                    gp = 1 - par
                    after(pool, q["empty"]["f1"], g + L)
                    src = h_tok[:, bass.ts(g, T), :] if layer == 0 else xn[:, gp]
                    row = R_BO0 + layer
                    pool.tensor_tensor(hb[:, :, :], src, rows[:, row:row + 1, :].broadcast_to([TP, T, D]),
                                       ALU.add).then_inc(q["pool_ready"], 1)
                if has(i + 1, 0, G):
                    norm_spread(pool, q, i + (L + 2))
                if has(i - 1, 0, G) and layer == 1:
                    g = i - 1
                    norm_spread(pool, fin, i)
                    pool.wait_ge(q["y_ready"], g + 1)
                    pool.tensor_tensor(y[:, :, :], xf[:, :, :], rows[:, R_G1:R_G1 + 1, :].broadcast_to([TP, T, D]),
                                       ALU.mult).then_inc(q["y2_ready"], 1)
                    pool.wait_ge(q["y2_ready"], g + 1)
                    pool.tensor_tensor(xf[:, :, :], y[:, :, :], rows[:, R_B1:R_B1 + 1, :].broadcast_to([TP, T, D]),
                                       ALU.add).then_inc(q["t_ready"], 1)

            if layer == 0:
                all_results(pool, 0)
                fetch_results(0, 0)

            steps(pool, emit, AT_FIRST, AT_INNER, AT_LAST[layer])

        phases = [0]

        def barrier(eng, number):
            eng.drain().then_inc(phase_done, 1)
            eng.wait_ge(phase_done, 5 * number)

        block = ctx.enter_context(nc.Block())

        @block.sync
        def _(sp):
            p1_sync(sp)
            sp.wait_ge(s_zero, 1)
            cleared = d["slots"].rearrange("(p r) d -> p (r d)", p=128)
            for n in range(NE[0] // 4):
                sp.dma_start(cleared[:, n * 4 * D:(n + 1) * 4 * D], zeros[:, :]).then_inc(s_clear, 16)
            sp.dma_start(down_w[:, :, 0:UNITS[0], :], d["down0"]).then_inc(s_experts, 16)
            sp.dma_start(bias2[:, :, :], d["bias2_0"]).then_inc(s_experts, 16)
            barrier(sp, 1)
            barrier(sp, 2)
            experts_sync(sp, 0)
            barrier(sp, 3)
            sp.dma_start(down_w[:, :, :, :], d["down1"]).then_inc(s_experts, 16)
            sp.dma_start(bias2[:, :, :], d["bias2_1"]).then_inc(s_experts, 16)
            for n in (4, 5, 6):
                barrier(sp, n)
            experts_sync(sp, 1)
            last_sync(sp)

        @block.tensor
        def _(pe):
            pe.wait_ge(s_patch_w, 32)
            pe.wait_ge(s_made, 6)
            p1_tensor(pe)
            barrier(pe, 1)
            route_tensor(pe, 0)
            barrier(pe, 2)
            pe.wait_ge(s_experts, 32)
            experts_tensor(pe, 0)
            barrier(pe, 3)
            attention_tensor(pe, 0)
            barrier(pe, 4)
            attention_tensor(pe, 1)
            barrier(pe, 5)
            route_tensor(pe, 1)
            barrier(pe, 6)
            pe.wait_ge(s_experts, 64)
            experts_tensor(pe, 1)

        @block.scalar
        def _(act):
            act.dma_start(wp[:, 0:KF, :], d["wp"]).then_inc(s_patch_w, 16)
            act.dma_start(wp[0:KR, KF, :], d["wpr"]).then_inc(s_patch_w, 16)
            for dst, src in loads:
                act.dma_start(dst, src).then_inc(s_in, 16)
            act.wait_ge(s_in, 16 * len(loads))
            p1_scalar(act)
            barrier(act, 1)
            route_scalar(act, 0)
            barrier(act, 2)
            experts_scalar(act, 0)
            barrier(act, 3)
            attention_scalar(act, 0)
            barrier(act, 4)
            attention_scalar(act, 1)
            barrier(act, 5)
            route_scalar(act, 1)
            barrier(act, 6)
            experts_scalar(act, 1)

        @block.vector
        def _(dve):
            p1_vector(dve)
            barrier(dve, 1)
            route_vector(dve, 0)
            barrier(dve, 2)
            dve.wait_ge(s_experts, 32)
            experts_vector(dve, 0)
            barrier(dve, 3)
            attention_vector(dve, 0)
            barrier(dve, 4)
            attention_vector(dve, 1)
            barrier(dve, 5)
            route_vector(dve, 1)
            barrier(dve, 6)
            dve.wait_ge(s_experts, 64)
            experts_vector(dve, 1)
            last_vector(dve)

        @block.gpsimd
        def _(pool):
            pool.memset(zeros[:, :], 0.0).then_inc(s_zero, 1)
            pool.memset(ident[:, :], 0.0).then_inc(s_made, 1)
            pool.memset(ones[:, :], 1.0).then_inc(s_made, 1)
            pool.memset(halves[:, :], -0.5).then_inc(s_made, 1)
            pool.wait_ge(s_made, 3)
            pool.affine_select(out=ident[:, :], in_=ident[:, :], compare_op=ALU.not_equal, fill=1.0, base=0,
                               pattern=[[-1, 128]], channel_multiplier=1).then_inc(s_made, 1)
            pool.affine_select(out=later[:, :], in_=ones[:, :], compare_op=ALU.is_gt, fill=0.0, base=0,
                               pattern=[[1, TP]], channel_multiplier=-1).then_inc(s_made, 1)
            pool.wait_ge(s_made, 5)
            pool.tensor_copy(identb[:, :], ident[:, :]).then_inc(s_made, 1)
            pool.wait_ge(s_in, 16 * len(loads))
            p1_gpsimd(pool)
            barrier(pool, 1)
            route_gpsimd(pool, 0)
            barrier(pool, 2)
            experts_gpsimd(pool, 0)
            barrier(pool, 3)
            attention_gpsimd(pool, 0)
            barrier(pool, 4)
            attention_gpsimd(pool, 1)
            barrier(pool, 5)
            route_gpsimd(pool, 1)
            barrier(pool, 6)
            experts_gpsimd(pool, 1)
            last_gpsimd(pool)


def kernel(**inputs):
    import numpy as np
    import concourse.bacc as bacc
    from concourse.bass_utils import run_bass_kernel_spmd

    f = {k: np.asarray(v) for k, v in inputs.items()}
    P = f["x"].shape[2] // 8
    x = f["x"].reshape(G, GI, 3, 8, P, 8, P).transpose(0, 2, 4, 6, 1, 3, 5).reshape(G, KF * 128 + KR, GI * NP)
    w = f["L0_tok_W"].T

    def parts(a, n):
        return a.reshape(*a.shape[:-2], n, 128, a.shape[-1]).swapaxes(-3, -2)

    def with_bias(w, b):
        return np.concatenate([w, b.reshape(E, 4, 128).transpose(0, 2, 1)], 2)

    heads = np.zeros((D, H), np.float32)
    for h in range(H):
        heads[h * DK:(h + 1) * DK, h] = 1.0
    cols = np.concatenate([np.stack([
        f["L0_tok_b"], f["L0_tok_class_token"][0], f["L0_attn_b_in"][:D], f["L0_attn_b_in"][D:], f["L0_attn_B"],
        f["L0_attn_A"], f["L1_attn_b_Q"], f["L1_attn_b_K"], f["L1_attn_b_V"], f["L1_ffn_bq"], f["L1_ffn_bk"],
        f["L1_ffn_bv"]], 1), heads], 1)
    rows = np.stack([f["L0_attn_b_out"], f["L0_attn_gamma"], f["L0_attn_beta"], f["L1_attn_b_O"], f["L1_ffn_bo"],
                     f["L1_ffn_ln1_g"], f["L1_ffn_ln1_b"]])
    win = f["L0_attn_W_in"].T
    mats = np.stack([win[:, :D], win[:, D:], f["L0_attn_W_out"].T]
                    + [f["L1_attn_W_" + n] for n in "QKVO"] + [f["L1_ffn_W" + n] for n in "qkvo"], 1)
    i, j = np.arange(S)[:, None], np.arange(S)[None, :]
    gap = i - j
    seen = (gap == 0) | (gap >= 1) & (gap <= S // 2) | (gap > 0) & (gap & gap - 1 == 0)
    mask = np.tile(np.where(seen, 0.0, -1e30).astype(np.float32), (1, 4))
    arrays = {
        "xa": parts(x[:, :KF * 128], KF),
        "xr": x[:, KF * 128:],
        "wp": parts(w[:KF * 128], KF),
        "wpr": w[KF * 128:],
        "cols": cols,
        "posT": f["L0_tok_pos_embed"].T,
        "mats": mats,
        "rows": np.broadcast_to(rows, (TP, NROW, D)),
        "route_w": np.stack([f["L0_ffn_router_w"].T, f["L1_ffn_gate_W"]], 1),
        "route_b": np.broadcast_to(np.stack([f["L0_ffn_router_b"], f["L1_ffn_gate_b"]]), (TP, 2, E)),
        "bias2_0": np.broadcast_to(f["L0_ffn_fc2_b"], (128, E, D)),
        "bias2_1": np.broadcast_to(f["L1_ffn_b2"], (128, E, D)),
        "tile_no": np.arange(max(NE), dtype=np.float32)[None],
        "mask": mask,
        "ids": np.broadcast_to(np.arange(E, dtype=np.float32), (TP, E)),
        "up0": with_bias(f["L0_ffn_fc1_w"].transpose(0, 2, 1), f["L0_ffn_fc1_b"]),
        "up1": with_bias(f["L1_ffn_W1"], f["L1_ffn_b1"]),
        "down0": parts(f["L0_ffn_fc2_w"].transpose(0, 2, 1), 2).transpose(1, 0, 2, 3),
        "down1": parts(f["L1_ffn_W2"], 4).transpose(1, 0, 2, 3),
    }
    nc = bacc.Bacc("TRN2", target_bir_lowering=False, num_devices=1)
    d = {}
    for name, a in arrays.items():
        arrays[name] = a = np.ascontiguousarray(a)
        d[name] = nc.dram_tensor("in_" + name, a.shape, mybir.dt.from_np(a.dtype), kind="ExternalInput").ap()
    d["slots"] = nc.dram_tensor("slots", (NE[0] * ET, D), F32, kind="Internal").ap()
    for k in range(2):
        d[f"results{k}"] = nc.dram_tensor(f"results{k}", (NE[k] * ET, D), F32, kind="Internal").ap()
    d["out"] = nc.dram_tensor("stored_out", (B * S, D), F32, kind="ExternalOutput").ap().rearrange("(t p) d -> p t d", p=TP)
    build_program(nc, d)
    got = run_bass_kernel_spmd(nc, [{"in_" + k: a for k, a in arrays.items()}], core_ids=[0]).results[0]["stored_out"]
    return got.reshape(B, S, D)
```

```python
from contextlib import ExitStack

import concourse.bass as bass
from concourse import mybir

F32 = mybir.dt.float32
I32 = mybir.dt.int32
BF16 = mybir.dt.bfloat16
ALU = mybir.AluOpType
ACT = mybir.ActivationFunctionType
AX = mybir.AxisListType

D = 128
B = 64
S = 65
NP = S - 1
GI = 8
G = B // GI
GT = GI * S
TP = 104
T = GT // TP
NT = G * T
KF = 18
KR = 48
H = 8
DK = D // H
HA = DK + 1
E = 8
TOP = (2, 1)
ET = 128
NE = tuple(-(-((k * B * S + E * (ET - 1)) // ET) // 8) * 8 for k in TOP)
UNITS = (2, 4)
PACK = 2
RING = 4 * PACK
HALF = GI // 2 * S
CAP = B * S + ET
CHOOSE = (12, 6)
SETTLE = 5
EPS = 1e-5
SHRINK = 7
SPLIT = ((0, 3 * TP), (3 * TP, 2 * TP))
PARTS = ((0, 6), (6, 12), (12, 18))

C_TOKB, C_CLS, C_BZ, C_BG, C_B, C_A = range(6)
C_ATT = 6
C_HEAD = 12
NCOL = C_HEAD + H
R_BOUT, R_GAMMA, R_BETA, R_BO0, R_BO1, R_G1, R_B1 = range(7)
NROW = 7
M_Z, M_G, M_OUT, M_ATT = 0, 1, 2, 3
NMAT = 11


def after(eng, sem, value):
    if isinstance(value, int) and value <= 0:
        return
    eng.wait_ge(sem, value)


def build_program(nc, d):
    ctx = ExitStack()
    with ctx:
        def sb(name, shape, dt=F32):
            return ctx.enter_context(nc.sbuf_tensor(name, shape, dt))

        def sem(name):
            return ctx.enter_context(nc.semaphore(name))

        ps = ctx.enter_context(nc.psum_tensor("ps", [128, 8, 512], F32))

        h_tok = sb("h_tok", [TP, NT, D])
        xf_all = sb("xf_all", [TP, NT, D])
        mats = sb("mats", [D, NMAT, D])
        cols = sb("cols", [D, NCOL])
        rows = sb("rows", [TP, NROW, D])
        route_w = sb("route_w", [D, 2, E])
        route_b = sb("route_b", [TP, 2, E])
        bias2 = sb("bias2", [128, E, D])
        down_w = sb("down_w", [128, E, 4, D])
        ident = sb("ident", [128, 128])
        identb = sb("identb", [128, 128], BF16)
        halves = sb("halves", [TP, T])
        posT = sb("posT", [D, S])
        later = sb("later", [TP, TP])
        ones = sb("ones", [TP, TP])
        tile_no = sb("tile_no", [1, max(NE)])
        tile_expert = sb("tile_expert", [1, max(NE)], I32)
        weight = sb("weight", [TP, 2, NT])
        slot = sb("slot", [TP, 2, NT], I32)
        result_slot = sb("result_slot", [TP, 2, NT], I32)
        tile_row = sb("tile_row", [1, max(NE)], I32)
        tail_row = sb("tail_row", [1, E], I32)
        top = sb("top", [TP, 2, NT])
        chose = sb("chose", [TP, 2, NT, E])
        place = sb("place", [TP, 2, NT])
        largest_is, ranked_id, without, pos = (sb(n, [TP, T, E]) for n in ("largest_is", "ranked_id", "without", "pos"))
        lowest = sb("lowest", [TP, T])
        chosen = sb("chosen", [TP, T + 1, E])
        picked = sb("picked", [TP, 2, T, E])
        next_row = sb("next_row", [TP, E])
        slot_now = sb("slot_now", [TP, 2, 2, T], I32)
        zeros = sb("zeros", [ET, D])
        maskf = sb("maskf", [S, HALF])
        maskb = sb("maskb", [S, HALF], BF16)
        ids = sb("ids", [TP, E])
        regions = sb("regions", [TP, E])
        logits = sb("logits", [TP, NT, E])
        arena = sb("arena", [128, 2 * (KF + 1) * 512])
        xs = arena[:, :].rearrange("p (b c n) -> p b c n", b=2, c=KF + 1)
        wp = sb("wp", [128, KF + 1, D])

        def carve(start, parts, shape):
            n = 1
            for x in shape:
                n *= x
            ap = arena[0:parts, start:start + n]
            names = "abcd"[:len(shape)]
            if len(shape) > 1:
                ap = ap.rearrange(f"p ({' '.join(names)}) -> p {' '.join(names)}",
                                  **dict(zip(names, shape)))
            return ap, start + n

        at = 0
        keysM, at = carve(at, D, (2, GI, H, S))
        qT, at = carve(at, D, (2, GT))
        vals, at = carve(at, S, (2, GI, H, HA))
        outT, at = carve(at, D, (2, GT))
        keysT, at = carve(at, D, (GT,))
        diff, at = carve(at, S, (2, H, S))
        prob, at = carve(at, S, (2, H, S))
        probT, at = carve(at, S, (2, H, S))
        got, at = carve(at, TP, (2, 2, T, D))
        assert at <= 2 * (KF + 1) * 512
        at = 0
        up_w, at = carve(at, 128, (RING, 4 * D + 4))
        rows_in, at = carve(at, ET, (RING, D))
        rowsT, at = carve(at, D, (2, ET))
        silu_h, at = carve(at, 128, (2, 2 * ET))
        hid, at = carve(at, 128, (2, 4, ET))
        rows_out, at = carve(at, ET, (RING, D))
        got_all, at = carve(at, TP, (NT, D))
        rt = []
        for _ in range(9):
            r, at = carve(at, TP, (NT, E))
            rt.append(r)
        rv = []
        for _ in range(8):
            r, at = carve(at, TP, (NT,))
            rv.append(r)
        re = []
        for _ in range(5):
            r, at = carve(at, TP, (E,))
            re.append(r)
        counted_i = sb("counted_i", [TP, 2, E], I32)
        past, at = carve(at, 1, (max(NE), E))
        past2, at = carve(at, 1, (max(NE), E))
        past_n, at = carve(at, 1, (4, max(NE)))

        tokT = sb("tokT", [D, GI, S])
        xn = sb("xn", [TP, 2, T, D])
        xT = sb("xT", [D, GT])
        norm_tiles = [(sb(f"stats{k}", [TP, T, 6]), sb(f"mv{k}", [TP, T, 2]), sb(f"spread{k}", [TP, T]),
                       sb(f"rstd{k}", [TP, T])) for k in range(2)]
        gate = sb("gate", [D, GT])
        ga = sb("ga", [D, GT])
        bz = sb("bz", [D, GT])
        carried = sb("carried", [D, S])
        state = sb("state", [D, GI, S])
        xb = sb("xb", [TP, T, D])
        hb = sb("hb", [TP, T, D])
        y = sb("y", [TP, T, D])
        xf = sb("xf", [TP, T, D])
        tT = sb("tT", [D, GT])
        peak = sb("peak", [S, 2, H])
        rden = sb("rden", [S, H])
        o_tok = sb("o_tok", [S, 2, D])
        warm = sb("warm", [1, 1])
        largest, shrunk, limit, limit2, eps_shrunk, eps_shrunk2, in_range, kept = (
            sb(n, [TP, T]) for n in ("largest", "shrunk", "limit", "limit2", "eps_shrunk", "eps_shrunk2",
                                     "in_range", "kept"))

        def tok_psum(bank, n=T):
            return ps[0:TP, bank:bank + 2, :].rearrange("p a n -> p (a n)")[:, 0:n * D]\
                .rearrange("p (t d) -> p t d", d=D)

        def tok_tile(bank, t):
            return ps[0:TP, bank + t // 4, t % 4 * D:(t % 4 + 1) * D]

        def feat_tile(bank, t):
            k = t // 3
            return ps[:, bank + k, (t - 3 * k) * TP:(t - 3 * k + 1) * TP]

        s_patch_w = sem("patch_weights_loaded")
        s_in = sem("constants_loaded")
        s_const = sem("class_token_ready")
        s_made = sem("identity_made")
        s_stood = sem("stood")
        s_regions = sem("regions_empty_again")
        s_zero = sem("zeros_ready")
        s_tails = sem("tails_written")
        s_scattered = sem("rows_scattered")
        s_experts = sem("expert_constants_loaded")
        s_last = sem("sum_ready")
        s_out = sem("stored")
        phase_done = sem("phase_done")
        loads = []

        def load(dst, src):
            loads.append((dst, src))

        load(cols[:, :], d["cols"])
        load(posT[:, :], d["posT"])
        load(mats[:, :, :], d["mats"])
        load(rows[:, :, :], d["rows"])
        load(route_w[:, :, :], d["route_w"])
        load(route_b[:, :, :], d["route_b"])
        load(tile_no[:, :], d["tile_no"])
        load(maskf[:, :], d["mask"])
        load(ids[:, :], d["ids"])
        load(regions[:, :], d["regions"])

        x_in = [[sem(f"x_in{p}{k}") for k in range(len(PARTS))] for p in range(2)]
        names = ("patch_mm patch_read tok_turned h_saved norm_ready norm_turned normT_ready zg_mm gate_ready "
                 "bz_ready carry_ready state_ready out_mm xb_ready hb_ready out_read y_ready scaled_ready h_ready "
                 "xf_ready xf_turned xfT_ready xfT_kept logit_mm logit_ready shrink_step").split()
        p1 = {n: sem("p1_" + n) for n in names}
        norm_names = ("stats_ready", "mean_ready", "spread_ready", "rstd_ready")
        n_in = {n: sem("norm_in_" + n) for n in norm_names}
        n_in["tiles"] = norm_tiles[0]
        n_out = {n: sem("norm_out_" + n) for n in norm_names}
        n_out["tiles"] = norm_tiles[1]

        def stand(eng, sem_, value):
            eng.wait_ge(sem_, value)
            eng.sem_inc(s_stood, 1)

        def norm_sums(dve, q, src):
            stats = q["tiles"][0]
            for t in range(T):
                last = dve.bn_stats(stats[:, t, :], src[:, t, :])
            last.then_inc(q["stats_ready"], 1)

        def norm_means(dve, q, count):
            stats, mv = q["tiles"][0:2]
            stand(dve, q["stats_ready"], count)
            for t in range(T):
                last = dve.bn_aggr(mv[:, t, :], stats[:, t, :])
            last.then_inc(q["mean_ready"], 1)

        def norm_stats(dve, q, src, count):
            norm_sums(dve, q, src)
            norm_means(dve, q, count)

        def norm_spread(pool, q, count, eps=None):
            _, mv, spread, rstd = q["tiles"]
            stand(pool, q["mean_ready"], count)
            if eps is None:
                ins = pool.tensor_scalar(spread[:, :], mv[:, :, 1], EPS, None, ALU.add)
            else:
                ins = pool.tensor_tensor(spread[:, :], mv[:, :, 1], eps[:, :], ALU.add)
            ins.then_inc(q["spread_ready"], 1)
            pool.wait_ge(q["spread_ready"], count)
            pool.tensor_tensor(rstd[:, :], spread[:, :], halves[:, :], ALU.pow).then_inc(q["rstd_ready"], 1)

        def norm_apply(dve, q, dst, src, count, r=None):
            _, mv, _, rstd = q["tiles"]
            if r is None:
                dve.wait_ge(q["rstd_ready"], count)
            else:
                rstd = r
            for t in range(T):
                last = dve.tensor_scalar(dst[:, t, :], src[:, t, :], mv[:, t, 0:1], rstd[:, t:t + 1],
                                         ALU.subtract, ALU.mult)
            return last

        rs = [{n: sem(f"route{k}_{n}") for n in ("step", "chose", "ranked", "settled")} for k in range(2)]
        s_gap = sem("logit_gaps_ready")
        s_exp = sem("exponentials_ready")
        s_tiles = sem("expert_tiles_ready")

        def steps(eng, emit, first, inner, last):
            for i in range(first[0], first[1]):
                emit(i, i % 2)
            a = first[1]
            with eng.Fori(0, inner // 2) as k:
                for j in range(2):
                    emit(2 * k + (a + j), (a + j) % 2)
            for i in range(a + inner, last):
                emit(i, i % 2)

        def has(i, lo, hi):
            return not isinstance(i, int) or lo <= i < hi

        P1_FIRST, P1_INNER, P1_LAST = (0, 4), 4, G + 4

        def p1_sync(sp):
            def emit(g):
                par = g % 2
                if g >= 2:
                    sp.wait_ge(p1["patch_mm"], g - 1)
                for k, (a, b) in enumerate(PARTS):
                    sp.dma_start(xs[:, par, a:b, :], d["xa"][g, :, a:b, :]).then_inc(x_in[par][k], 16)
                sp.dma_start(xs[0:KR, par, KF, :], d["xr"][g]).then_inc(x_in[par][2], 16)
            emit(0)
            emit(1)
            with sp.Fori(0, 3) as k:
                for par in range(2):
                    g = 2 * k + (2 + par)
                    sp.wait_ge(p1["patch_mm"], g - 1)
                    for n, (a, b) in enumerate(PARTS):
                        sp.dma_start(xs[:, par, a:b, :], d["xa"][g, :, a:b, :]).then_inc(x_in[par][n], 16)
                    sp.dma_start(xs[0:KR, par, KF, :], d["xr"][g]).then_inc(x_in[par][2], 16)

        def up_to(g):
            return min(g, G) if isinstance(g, int) else g

        def out_tiles(a, b):
            bank, first = (7, 0) if a < 4 else (6, 4)
            return ps[0:TP, bank, (a - first) * D:(b - first) * D].rearrange("p (t d) -> p t d", d=D)

        def p1_tensor(pe):
            q = p1

            def turn_tokens(g):
                pe.wait_ge(q["patch_read"], g + 1)
                after(pe, q["bz_ready"], g)
                for t in range(T):
                    last = pe.transpose(tok_tile(2, t), tokT[:, :, :].rearrange("p a s -> p (a s)")[:, t * TP:(t + 1) * TP],
                                        ident[:, :])
                last.then_inc(q["tok_turned"], 1)

            def turn_norm(g):
                pe.wait_ge(q["norm_ready"], g + 1)
                after(pe, q["xfT_ready"], g - 1)
                for t in range(T):
                    last = pe.transpose(feat_tile(4, t), xn[:, 0, t, :], ident[0:TP, 0:TP])
                last.then_inc(q["norm_turned"], 1)

            def project(g):
                pe.wait_ge(q["normT_ready"], g + 1)
                pe.wait_ge(q["h_saved"], g + 1)
                for m, bank in ((M_Z, 2), (M_G, 4)):
                    for k, (o, n) in enumerate(SPLIT):
                        last = pe.matmul(ps[:, bank + k, 0:n], mats[:, m, :], xT[:, o:o + n], start=True, stop=True)
                last.then_inc(q["zg_mm"], 1)

            def project_out(g):
                pe.wait_ge(q["state_ready"], GI * g + GI)
                after(pe, q["out_read"], g)
                after(pe, q["logit_ready"], g - 1)
                for t in range(T):
                    last = pe.matmul(out_tiles(t, t + 1)[:, 0], state[:, :, :].rearrange("p a s -> p (a s)")[:, t * TP:(t + 1) * TP],
                                     mats[:, M_OUT, :], start=True, stop=True)
                last.then_inc(q["out_mm"], 1)

            def turn_router(g):
                pe.wait_ge(q["xf_ready"], g + 1)
                pe.wait_ge(q["gate_ready"], up_to(g + 2))
                after(pe, q["xfT_ready"], g)
                after(pe, rs[0]["settled"], SETTLE * (g - 1) + 2 if not isinstance(g, int) or g else 0)
                for t in range(T):
                    last = pe.transpose(feat_tile(4, t), xf[:, t, :], ident[0:TP, 0:TP])
                last.then_inc(q["xf_turned"], 1)

            def router(g):
                pe.wait_ge(q["xfT_ready"], g + 1)
                after(pe, q["logit_ready"], g)
                pe.wait_ge(q["out_read"], up_to(g + 2))
                for t in range(T):
                    last = pe.matmul(ps[0:TP, 6, 256 + t * E:256 + (t + 1) * E], tT[:, t * TP:(t + 1) * TP], route_w[:, 0, :],
                                     start=True, stop=True)
                last.then_inc(q["logit_mm"], 1)

            def emit(i, par):
                use = i // 2 + 1 if isinstance(i, int) else None
                full = has(i, 0, G)

                def chunks(a, b):
                    for c in range(a, b):
                        rows_n = 128 if c < KF else KR
                        last = pe.matmul(ps[:, par, :], wp[0:rows_n, c, :], xs[0:rows_n, par, c, :],
                                         start=(c == 0), stop=(c == KF))
                    return last

                def loaded(k):
                    per = 32 if k == 2 else 16
                    if use is not None:
                        pe.wait_ge(x_in[par][k], per * use)
                    else:
                        pe.wait_ge(x_in[par][k], (i - par) * (per // 2) + per)

                if full:
                    after(pe, q["patch_read"], i - 1)
                    loaded(0)
                    chunks(0, 3)
                if has(i, 3, G + 3):
                    turn_router(i - 3)
                if full:
                    chunks(3, 5)
                if has(i, 3, G + 3):
                    router(i - 3)
                if full:
                    chunks(5, 6)
                    loaded(1)
                    chunks(6, 10)
                if has(i, 1, G + 1):
                    turn_norm(i - 1)
                if full:
                    chunks(10, 12)
                    loaded(2)
                if has(i, 1, G + 1):
                    project(i - 1)
                if full:
                    chunks(12, 19).then_inc(q["patch_mm"], 1)
                    if isinstance(i, int) and i == 0:
                        pe.wait_ge(s_in, 16 * len(loads))
                    turn_tokens(i)
                if has(i, 1, G + 1):
                    project_out(i - 1)
                if has(i, 3, G + 3):
                    pe.wait_ge(q["gate_ready"], up_to(i))
                    rank(pe, 0, i - 3, 5)

            steps(pe, emit, P1_FIRST, P1_INNER, P1_LAST)

        def p1_scalar(act):
            q = p1

            def emit(i, par):
                if has(i, 1, G + 1):
                    g = i - 1
                    act.wait_ge(q["tok_turned"], g + 1)
                    act.activation(h_tok[:, bass.ts(g, T), :], tok_psum(2), ACT.Copy).then_inc(q["h_saved"], 1)
                if has(i, 3, G + 3):
                    g = i - 3
                    act.wait_ge(q["xf_turned"], g + 1)
                    after(act, q["logit_mm"], g)
                    for k, (o, n) in enumerate(SPLIT):
                        last = act.activation(tT[:, o:o + n], ps[:, 4 + k, 0:n], ACT.Copy)
                    last.then_inc(q["xfT_ready"], 1)
                    last = act.activation(xf_all[:, bass.ts(g, T), :], xf[:, :, :], ACT.Copy)
                    last.then_inc(q["xfT_kept"], 1)
                if has(i, 1, G + 1):
                    g = i - 1
                    act.wait_ge(q["norm_turned"], g + 1)
                    after(act, q["zg_mm"], g)
                    for k, (o, n) in enumerate(SPLIT):
                        last = act.activation(xT[:, o:o + n], ps[:, 4 + k, 0:n], ACT.Copy)
                    last.then_inc(q["normT_ready"], 1)
                    act.wait_ge(q["zg_mm"], g + 1)
                    after(act, q["bz_ready"], g)
                    for k, (o, n) in enumerate(SPLIT):
                        last = act.activation(gate[:, o:o + n], ps[:, 4 + k, 0:n], ACT.Sigmoid,
                                              bias=cols[:, C_BG:C_BG + 1])
                    last.then_inc(q["gate_ready"], 1)

            steps(act, emit, P1_FIRST, P1_INNER, P1_LAST)

        def shrink(dve, g):
            q = p1
            n = SHRINK * g

            def then(ins, k):
                ins.then_inc(q["shrink_step"], 1)
                dve.wait_ge(q["shrink_step"], n + k)

            then(dve.tensor_reduce(largest[:, :], y[:, :, :], AX.X, ALU.max, apply_absolute_value=True), 1)
            then(dve.tensor_scalar(largest[:, :], largest[:, :], 1.0, None, ALU.max), 2)
            then(dve.reciprocal(shrunk[:, :], largest[:, :]), 3)
            dve.tensor_tensor(y[:, :, :], y[:, :, :], shrunk[:, :].unsqueeze(2).broadcast_to([TP, T, D]), ALU.mult)
            dve.tensor_scalar(limit[:, :], shrunk[:, :], 2.0 ** 64, 1e12, ALU.mult, ALU.min)
            then(dve.scalar_tensor_tensor(out=eps_shrunk[:, :], in0=shrunk[:, :], scalar=EPS, in1=shrunk[:, :],
                                          op0=ALU.mult, op1=ALU.mult), 4)
            dve.tensor_tensor(limit2[:, :], limit[:, :], limit[:, :], ALU.mult)
            then(dve.tensor_scalar(eps_shrunk2[:, :], eps_shrunk[:, :], 1e-30, None, ALU.max), 5)

        def judge(dve, g):
            q = p1
            mv, rstd = norm_tiles[1][1], norm_tiles[1][3]
            n = SHRINK * g
            dve.wait_ge(n_out["rstd_ready"], 2 * g + 1)
            dve.scalar_tensor_tensor(out=in_range[:, :], in0=mv[:, :, 1], scalar=float(D), in1=limit2[:, :],
                                     op0=ALU.mult, op1=ALU.is_lt).then_inc(q["shrink_step"], 1)
            dve.wait_ge(q["shrink_step"], n + 6)
            dve.tensor_tensor(kept[:, :], rstd[:, :], in_range[:, :], ALU.mult).then_inc(q["shrink_step"], 1)
            dve.wait_ge(q["shrink_step"], n + SHRINK)

        READ_AT = 7

        def p1_vector(dve):
            q = p1

            def read_patches(g, par):
                dve.wait_ge(q["patch_mm"], g + 1)
                after(dve, q["tok_turned"], g)
                dve.scalar_tensor_tensor(out=tokT[:, :, 1:S],
                                         in0=ps[:, par, :].rearrange("p (a s) -> p a s", s=NP),
                                         scalar=cols[:, C_TOKB:C_TOKB + 1],
                                         in1=posT[:, 1:S].unsqueeze(1).broadcast_to([D, GI, NP]),
                                         op0=ALU.add, op1=ALU.mult).then_inc(q["patch_read"], 1)

            def emit(i, par):
                has1, has2, has3 = has(i, 1, G + 1), has(i, 2, G + 2), has(i, 3, G + 3)
                if has1:
                    g = i - 1
                    stand(dve, q["h_saved"], g + 1)
                    norm_stats(dve, n_in, h_tok[:, bass.ts(g, T), :], g + 1)
                if has(i, 4, G + 4):
                    for k in range(SETTLE):
                        settle(dve, 0, i - 4, 5, k)
                if has2:
                    g = i - 2
                    dve.wait_ge(q["out_mm"], g + 1)
                    dve.wait_ge(q["xb_ready"], g + 1)
                    for a, b in ((0, 4), (4, 5)):
                        last = dve.tensor_tensor(y[:, a:b, :], out_tiles(a, b), xb[:, a:b, :], ALU.add)
                    last.then_inc(q["out_read"], 1)
                    dve.wait_ge(q["out_read"], g + 1)
                    shrink(dve, g)
                    norm_stats(dve, n_out, y, 2 * g + 1)
                if has1:
                    g = i - 1
                    after(dve, q["norm_turned"], g)
                    after(dve, q["xb_ready"], g)
                    norm_apply(dve, n_in, xn[:, 0], h_tok[:, bass.ts(g, T), :], g + 1).then_inc(q["norm_ready"], 1)
                if has3:
                    g = i - 3
                    dve.wait_ge(q["logit_mm"], g + 1)
                    dve.tensor_tensor(logits[:, bass.ts(g, T), :],
                                      ps[0:TP, 6, 256:256 + T * E].rearrange("p (t e) -> p t e", e=E),
                                      route_b[:, 0:1, :].broadcast_to([TP, T, E]), ALU.add)\
                       .then_inc(q["logit_ready"], 1)
                if has2:
                    g = i - 2
                    judge(dve, g)
                    after(dve, q["xf_turned"], g)
                    after(dve, q["xfT_kept"], g)
                    norm_apply(dve, n_out, xf, y, 2 * g + 1, r=kept).then_inc(q["y_ready"], 1)
                    dve.wait_ge(q["y_ready"], g + 1)
                    dve.tensor_tensor(y[:, :, :], xf[:, :, :],
                                      rows[:, R_GAMMA:R_GAMMA + 1, :].broadcast_to([TP, T, D]), ALU.mult)\
                       .then_inc(q["scaled_ready"], 1)
                    dve.wait_ge(q["scaled_ready"], g + 1)
                    dve.wait_ge(q["hb_ready"], g + 1)
                    ht = h_tok[:, bass.ts(g, T), :]
                    dve.tensor_tensor(ht, y[:, :, :], hb[:, :, :], ALU.add).then_inc(q["h_ready"], 1)
                    stand(dve, q["h_ready"], g + 1)
                    norm_stats(dve, n_out, ht, 2 * g + 2)
                if has3:
                    stand(dve, q["logit_ready"], i - 2)
                if has1:
                    g = i - 1
                    dve.wait_ge(q["zg_mm"], g + 1)
                    for k, (o, n) in enumerate(SPLIT):
                        dve.tensor_scalar(bz[:, o:o + n], ps[:, 2 + k, 0:n], cols[:, C_BZ:C_BZ + 1],
                                          cols[:, C_B:C_B + 1], ALU.add, ALU.mult)
                    dve.wait_ge(q["gate_ready"], g + 1)
                    dve.tensor_scalar(ga[:, :], gate[:, :], cols[:, C_A:C_A + 1], None, ALU.mult)\
                       .then_inc(q["bz_ready"], 1)
                    dve.wait_ge(q["bz_ready"], g + 1)
                    after(dve, q["out_mm"], g)
                    for b in range(GI):
                        if b == READ_AT and has(i, 0, G):
                            read_patches(i, par)
                        prev = state[:, (b - 1) % GI, :]
                        if b:
                            dve.wait_ge(q["state_ready"], GI * g + b)
                        dve.tensor_tensor(carried[:, :], ga[:, b * S:(b + 1) * S], prev, ALU.mult)\
                           .then_inc(q["carry_ready"], 1)
                        if has3 and 2 * b < CHOOSE[0]:
                            choose(dve, 0, i - 3, 2 * b)
                        dve.wait_ge(q["carry_ready"], GI * g + b + 1)
                        dve.tensor_tensor(state[:, b, :], carried[:, :], bz[:, b * S:(b + 1) * S], ALU.add)\
                           .then_inc(q["state_ready"], 1)
                        if has3 and 2 * b < CHOOSE[0]:
                            choose(dve, 0, i - 3, 2 * b + 1)
                elif has(i, 0, G):
                    read_patches(i, par)
                elif has3:
                    for k in range(CHOOSE[0]):
                        choose(dve, 0, i - 3, k)
                if has2:
                    g = i - 2
                    norm_apply(dve, n_out, xf, h_tok[:, bass.ts(g, T), :], 2 * g + 2).then_inc(q["xf_ready"], 1)

            dve.wait_ge(s_in, 16 * len(loads))
            dve.memset(state[:, :, :], 0.0)
            dve.memset(chosen[:, T, :], 0.0)
            dve.tensor_copy(next_row[:, :], regions[:, :])
            dve.tensor_copy(maskb[:, :], maskf[:, :])
            dve.tensor_tensor(tokT[:, 0, 0:1], cols[:, C_CLS:C_CLS + 1], posT[:, 0:1], ALU.mult).then_inc(s_const, 1)
            dve.wait_ge(s_const, 1)
            dve.tensor_copy(tokT[:, 1:GI, 0:1], tokT[:, 0:1, 0:1].broadcast_to([D, GI - 1, 1])).then_inc(s_const, 1)
            dve.wait_ge(s_const, 2)
            steps(dve, emit, P1_FIRST, P1_INNER, P1_LAST)

        def p1_gpsimd(pool):
            q = p1

            def emit(i, par):
                if has(i, 1, G + 1):
                    norm_spread(pool, n_in, i)
                if has(i, 4, G + 4):
                    pool.wait_ge(q["xfT_kept"], i - 3)
                    scatter(pool, 0, i - 4, 0)
                if has(i, 2, G + 2):
                    norm_spread(pool, n_out, 2 * (i - 2) + 1, eps_shrunk2)
                if has(i, 1, G + 1):
                    g = i - 1
                    pool.wait_ge(q["norm_ready"], g + 1)
                    after(pool, q["out_read"], g)
                    pool.tensor_tensor(xb[:, :, :], xn[:, 0], rows[:, R_BOUT:R_BOUT + 1, :].broadcast_to([TP, T, D]),
                                       ALU.add).then_inc(q["xb_ready"], 1)
                if has(i, 2, G + 2):
                    norm_spread(pool, n_out, 2 * (i - 2) + 2)
                if has(i, 1, G + 1):
                    g = i - 1
                    after(pool, q["h_ready"], g)
                    pool.tensor_tensor(hb[:, :, :], h_tok[:, bass.ts(g, T), :],
                                       rows[:, R_BETA:R_BETA + 1, :].broadcast_to([TP, T, D]),
                                       ALU.add).then_inc(q["hb_ready"], 1)

                if has(i, 4, G + 4):
                    scatter(pool, 0, i - 4, 1)

            for i in range(G + 4):
                emit(i, i % 2)

        def wide(v, n):
            return v.unsqueeze(2).broadcast_to([TP, n, E])

        def choose(dve, layer, g, k):
            q = rs[layer]
            ts = bass.ts(g, T)
            lg = logits[:, ts, :]
            if k:
                (stand if layer == 1 and k == 5 else after)(dve, q["chose"], CHOOSE[layer] * g + k)
            n, of = (0, lg) if k < 5 else (1, without[:, :, :])
            step = k if k < 5 else k - 6
            if k == CHOOSE[layer] - 1:
                both = chose[:, 0, ts, :], chose[:, 1, ts, :]
                if layer == 0:
                    ins = dve.tensor_tensor(chosen[:, 0:T, :], *both, ALU.add)
                else:
                    ins = dve.tensor_copy(chosen[:, 0:T, :], both[0])
            elif k == 5:
                ins = dve.scalar_tensor_tensor(out=without[:, :, :], in0=chose[:, 0, ts, :], scalar=-3e38, in1=lg,
                                               op0=ALU.mult, op1=ALU.add)
            elif step == 0:
                ins = dve.tensor_reduce(top[:, n, ts], of, AX.X, ALU.max)
            elif step == 1:
                ins = dve.tensor_tensor(largest_is[:, :, :], of, wide(top[:, n, ts], T), ALU.is_equal)
            elif step == 2:
                ins = dve.scalar_tensor_tensor(out=ranked_id[:, :, :], in0=largest_is[:, :, :], scalar=-64.0,
                                               in1=ids[:, :].unsqueeze(1).broadcast_to([TP, T, E]),
                                               op0=ALU.mult, op1=ALU.add)
            elif step == 3:
                ins = dve.tensor_reduce(lowest[:, :], ranked_id[:, :, :], AX.X, ALU.min)
            else:
                ins = dve.tensor_tensor(chose[:, n, ts, :], ranked_id[:, :, :], wide(lowest[:, :], T), ALU.is_equal)
            ins.then_inc(q["chose"], 1)

        def rank(pe, layer, g, bank):
            q = rs[layer]
            pe.wait_ge(q["chose"], CHOOSE[layer] * (g + 1))
            pe.matmul(ps[0:TP, bank, 0:(T + 1) * E], later[:, :], chosen[:, :, :].rearrange("p t e -> p (t e)"),
                      start=True, stop=False)
            for t in range(T):
                last = pe.matmul(ps[0:TP, bank, (t + 1) * E:(T + 1) * E], ones[:, :],
                                 chosen[:, t:t + 1, :].broadcast_to([TP, T - t, E]), start=False, stop=(t == T - 1))
            last.then_inc(q["ranked"], 1)

        def settle(dve, layer, g, bank, k):
            q = rs[layer]
            K, ts = TOP[layer], bass.ts(g, T)
            if k == 0:
                dve.wait_ge(q["ranked"], g + 1)
                ins = dve.tensor_tensor(pos[:, :, :], ps[0:TP, bank, 0:T * E].rearrange("p (t e) -> p t e", e=E),
                                        next_row[:, :].unsqueeze(1).broadcast_to([TP, T, E]), ALU.add)
            elif k == 1:
                dve.wait_ge(q["settled"], SETTLE * g + k)
                ins = dve.tensor_tensor(next_row[:, :], next_row[:, :], ps[0:TP, bank, T * E:(T + 1) * E], ALU.add)
            else:
                (stand if k == 4 else after)(dve, q["settled"], SETTLE * g + k)
                if k == 2:
                    for n in range(K):
                        ins = dve.tensor_tensor(picked[:, n, :, :], pos[:, :, :], chose[:, n, ts, :], ALU.mult)
                elif k == 3:
                    ins = dve.tensor_reduce(place[:, 0:K, ts], picked[:, 0:K, :, :], AX.X, ALU.add)
                else:
                    ins = dve.tensor_copy(slot[:, 0:K, ts], place[:, 0:K, ts])
            ins.then_inc(q["settled"], 1)

        def scatter(pool, layer, g, k):
            pool.wait_ge(rs[layer]["settled"], SETTLE * (g + 1))
            for t in range(g * T, (g + 1) * T):
                pool.indirect_dma_start(out=d["slots"],
                                        out_offset=bass.IndirectOffsetOnAxis(ap=slot[:, k, t:t + 1], axis=0),
                                        in_=xf_all[:, t, :], in_offset=None).then_inc(s_scattered, 16)

        def route_vector(dve, layer):
            q = rs[layer]
            K, N = TOP[layer], NE[layer]
            count = [0]

            def then(ins):
                count[0] += 1
                ins.then_inc(q["step"], 1)
                dve.wait_ge(q["step"], count[0])

            dve.wait_ge(q["settled"], SETTLE * G)
            if layer == 0:
                dve.tensor_tensor(rv[4], top[:, 1, :], top[:, 0, :], ALU.subtract).then_inc(s_gap, 1)
            else:
                dve.tensor_tensor(rt[3], logits[:, :, :], wide(top[:, 0, :], NT), ALU.subtract).then_inc(s_gap, 1)
            dve.tensor_copy(tail_row[:, :], next_row[0:1, :])
            then(dve.tensor_tensor(re[4], next_row[:, :], regions[:, :], ALU.subtract))
            then(dve.tensor_scalar(counted_i[:, 0, :], re[4], float(ET - 1), None, ALU.add))
            then(dve.tensor_single_scalar(counted_i[:, 1, :], counted_i[:, 0, :], ET.bit_length() - 1,
                                          ALU.arith_shift_right))
            then(dve.tensor_copy(re[0], counted_i[:, 1, :]))
            then(dve.tensor_tensor_scan(re[1], ones[:, 0:E], re[0], 0.0, ALU.mult, ALU.add))
            ends = re[1][0:1, 0:E - 1].unsqueeze(1).broadcast_to([1, N, E - 1])
            then(dve.tensor_tensor(past[:, 0:N, 0:E - 1], ends,
                                   tile_no[:, 0:N].unsqueeze(2).broadcast_to([1, N, E - 1]), ALU.is_le))
            dve.tensor_tensor(past2[:, 0:N, 0:E - 1], past[:, 0:N, 0:E - 1],
                              re[0][0:1, 0:E - 1].unsqueeze(1).broadcast_to([1, N, E - 1]), ALU.mult)
            then(dve.tensor_reduce(past_n[:, 0, 0:N], past[:, 0:N, 0:E - 1], AX.X, ALU.add))
            dve.tensor_copy(tile_expert[:, 0:N], past_n[:, 0, 0:N])
            then(dve.tensor_reduce(past_n[:, 1, 0:N], past2[:, 0:N, 0:E - 1], AX.X, ALU.add))
            then(dve.tensor_tensor(past_n[:, 2, 0:N], tile_no[:, 0:N], past_n[:, 1, 0:N], ALU.subtract))
            then(dve.tensor_scalar(past_n[:, 3, 0:N], past_n[:, 2, 0:N], float(ET), None, ALU.mult))
            then(dve.scalar_tensor_tensor(out=past_n[:, 1, 0:N], in0=past_n[:, 0, 0:N], scalar=float(CAP),
                                          in1=past_n[:, 3, 0:N], op0=ALU.mult, op1=ALU.add))
            dve.tensor_tensor(tile_row[:, 0:N], past_n[:, 1, 0:N],
                              next_row[0:1, E - 1:E].broadcast_to([1, N]), ALU.min).then_inc(s_tiles, 1)
            then(dve.tensor_tensor(re[2], re[1], re[0], ALU.subtract))
            then(dve.scalar_tensor_tensor(out=re[3], in0=re[2], scalar=float(ET), in1=regions[:, :],
                                          op0=ALU.mult, op1=ALU.subtract))
            for k in range(K):
                then(dve.tensor_tensor(rt[0], chose[:, k, :, :], re[3].unsqueeze(1).broadcast_to([TP, NT, E]), ALU.mult))
                then(dve.tensor_reduce(rv[k], rt[0], AX.X, ALU.add))
                then(dve.tensor_tensor(result_slot[:, k, :], place[:, k, :], rv[k], ALU.add))
            dve.wait_ge(s_exp, layer + 1)
            if layer == 0:
                then(dve.tensor_scalar(rv[6], rv[5], 1.0, None, ALU.add))
                then(dve.reciprocal(weight[:, 0, :], rv[6]))
                then(dve.tensor_tensor(weight[:, 1, :], rv[5], weight[:, 0, :], ALU.mult))
            else:
                then(dve.tensor_reduce(rv[6], rt[4], AX.X, ALU.add))
                then(dve.reciprocal(weight[:, 0, :], rv[6]))

        def route_scalar(act, layer):
            act.wait_ge(s_gap, layer + 1)
            if layer == 0:
                act.activation(rv[5], rv[4], ACT.Exp).then_inc(s_exp, 1)
            else:
                act.activation(rt[4], rt[3], ACT.Exp).then_inc(s_exp, 1)

        def write_tails(act, layer):
            act.wait_ge(s_tiles, layer + 1)
            act.wait_ge(s_zero, 1)
            for e in range(E):
                row = act.value_load(tail_row[0:1, e:e + 1], min_val=e * CAP, max_val=e * CAP + B * S)
                act.dma_start(d["slots"][bass.ds(row, ET), :], zeros[:, :]).then_inc(s_tails, 16)

        ex = {n: sem("ex_" + n) for n in ("rows_turned", "rowsT_ready", "up_mm", "silu_ready", "hid_ready", "down_mm",
                                          "out_ready")}
        tile_in = [sem(f"tile_in{r}") for r in range(RING)]
        pack_out = [sem(f"pack_out{r}") for r in range(RING // PACK)]
        rows_at = [sem(f"rows_in{r}") for r in range(RING)]
        got_in = [sem(f"got_in{p}") for p in range(2)]

        def tiles(eng, emit, layer, start):
            N = NE[layer]
            for t in range(start, RING):
                emit(t, t % RING)
            with eng.Fori(1, N // RING - 1) as k:
                for r in range(RING):
                    emit(RING * k + r, r)
            for t in range(N - RING, N):
                emit(t, t % RING)

        def within(t, layer):
            return not isinstance(t, int) or 0 <= t < NE[layer]

        def ring_count(t, r, base, per):
            if isinstance(t, int):
                return per * ((t + base) // RING + 1)
            return (t - r) * (per // RING) + (per * (base // RING) + per)

        def expert_of(eng, t):
            return eng.value_load(tile_expert[0:1, bass.ds(t, 1)], min_val=0, max_val=E - 1)

        def experts_sync(sp, layer):
            q = ex
            base = NE[0] * layer
            N = NE[layer]
            up = d[f"up{layer}"]
            results = d[f"results{layer}"]

            def fetch(t, r):
                e = expert_of(sp, t)
                after(sp, q["hid_ready"], t + (base - RING + 1))
                sp.dma_start(up_w[:, r, :], up[bass.ds(e, 1)].squeeze(0)).then_inc(tile_in[r], 16)

            def store(t, r):
                sp.wait_ge(q["out_ready"], t + (base + PACK))
                sp.dma_start(results[bass.ds(t * ET, PACK * ET), :].rearrange("(n p) d -> p n d", p=ET),
                             rows_out[:, r:r + PACK, :]).then_inc(pack_out[r // PACK], 16)

            def emit(t, r):
                if within(t + RING, layer):
                    fetch(t + RING, r)
                if r % PACK == 1 and within(t - (PACK + 1), layer):
                    store(t - (PACK + 1), (r - (PACK + 1)) % RING)

            sp.wait_ge(s_tiles, layer + 1)
            for t in range(RING):
                fetch(t, t)
            for t in range(RING):
                emit(t, t)
            with sp.Fori(1, N // RING - 1) as k:
                for r in range(RING):
                    emit(RING * k + r, r)
            for t in range(N - RING, N):
                emit(t, t % RING)
            store(N - PACK, RING - PACK)

        def experts_gpsimd(pool, layer):
            base = NE[0] * layer

            def fetch(t, r):
                row = pool.value_load(tile_row[0:1, bass.ds(t, 1)], min_val=0, max_val=E * CAP - ET)
                after(pool, ex["rows_turned"], t + (base - RING + 1))
                pool.dma_start(rows_in[:, r, :], d["slots"][bass.ds(row, ET), :]).then_inc(rows_at[r], 16)

            pool.wait_ge(s_tiles, layer + 1)
            pool.wait_ge(s_scattered, 16 * NT * sum(TOP[:layer + 1]))
            pool.wait_ge(s_tails, 16 * E * (layer + 1))
            for t in range(RING):
                fetch(t, t)
            with pool.Fori(1, NE[layer] // RING) as k:
                for r in range(RING):
                    fetch(RING * k + r, r)

        def experts_tensor(pe, layer):
            q = ex
            base = NE[0] * layer
            U = UNITS[layer]

            def turn_rows(t, r):
                pe.wait_ge(rows_at[r], ring_count(t, r, base, 16))
                after(pe, q["rowsT_ready"], t + (base - 1))
                pe.transpose(ps[:, 6 + r % 2, 0:ET], rows_in[:, r, :], ident[:, :]).then_inc(q["rows_turned"], 1)

            def up(t, r):
                pe.wait_ge(tile_in[r], ring_count(t, r, base, 16))
                pe.wait_ge(q["rowsT_ready"], t + (base + 1))
                after(pe, q["hid_ready"], t + (base - 1))
                for f in range(4):
                    bank, at = (2 * (f // 2), f % 2) if layer == 0 else (0, f)
                    last = pe.matmul(ps[:, bank + r % 2, at * ET:(at + 1) * ET], up_w[:, r, f * D:(f + 1) * D],
                                     rowsT[:, r % 2, :], start=True, stop=True)
                last.then_inc(q["up_mm"], 1)

            def down(t, r, e):
                pe.wait_ge(q["hid_ready"], t + (base + 1))
                after(pe, q["out_ready"], t + (base - 1))
                for c in range(U):
                    last = pe.matmul(ps[:, 4 + r % 2, 0:D], hid[:, r % 2, c, :],
                                     down_w[:, bass.ds(e, 1), c, :].squeeze(1), start=(c == 0), stop=(c == U - 1))
                last.then_inc(q["down_mm"], 1)

            def emit(t, r):
                if within(t + 2, layer):
                    turn_rows(t + 2, (r + 2) % RING)
                if within(t + 1, layer):
                    up(t + 1, (r + 1) % RING)
                if within(t, layer):
                    down(t, r, expert_of(pe, t))

            tiles(pe, emit, layer, -2)

        def experts_scalar(act, layer):
            q = ex
            base = NE[0] * layer
            act.activation(warm[:, :], ident[0:1, 0:1], ACT.Silu if layer == 0 else ACT.Gelu_apprx_tanh)

            def emit(t, r):
                if layer == 0 and within(t + 2, layer):
                    n, p = t + 2, r % 2
                    act.wait_ge(q["rows_turned"], n + (base + 1))
                    act.activation(rowsT[:, p, :], ps[:, 6 + p, 0:ET], ACT.Copy).then_inc(q["rowsT_ready"], 1)
                if within(t + 1, layer):
                    n, r1 = t + 1, (r + 1) % RING
                    act.wait_ge(q["up_mm"], n + (base + 1))
                    if layer == 0:
                        for c in range(2):
                            last = act.activation(silu_h[:, r1 % 2, c * ET:(c + 1) * ET],
                                                  ps[:, r1 % 2, c * ET:(c + 1) * ET], ACT.Silu,
                                                  bias=up_w[:, r1, 4 * D + c:4 * D + c + 1])
                        last.then_inc(q["silu_ready"], 1)
                    else:
                        for c in range(4):
                            last = act.activation(hid[:, r1 % 2, c, :], ps[:, r1 % 2, c * ET:(c + 1) * ET],
                                                  ACT.Gelu_apprx_tanh, bias=up_w[:, r1, 4 * D + c:4 * D + c + 1])
                        last.then_inc(q["hid_ready"], 1)

            tiles(act, emit, layer, -2)

        def experts_vector(dve, layer):
            q = ex
            base = NE[0] * layer

            def emit(t, r):
                if layer == 1 and within(t + 2, layer):
                    n, p = t + 2, r % 2
                    dve.wait_ge(q["rows_turned"], n + (base + 1))
                    dve.tensor_copy(rowsT[:, p, :], ps[:, 6 + p, 0:ET]).then_inc(q["rowsT_ready"], 1)
                if layer == 0 and within(t + 1, layer):
                    n, r1 = t + 1, (r + 1) % RING
                    dve.wait_ge(q["silu_ready"], n + 1)
                    for c in range(2):
                        last = dve.scalar_tensor_tensor(
                            out=hid[:, r1 % 2, c, :], in0=ps[:, 2 + r1 % 2, c * ET:(c + 1) * ET],
                            scalar=up_w[:, r1, 4 * D + 2 + c:4 * D + 3 + c],
                            in1=silu_h[:, r1 % 2, c * ET:(c + 1) * ET], op0=ALU.add, op1=ALU.mult)
                    last.then_inc(q["hid_ready"], 1)
                if within(t, layer):
                    dve.wait_ge(q["down_mm"], t + (base + 1))
                    if not isinstance(t, int) or t + base >= RING:
                        dve.wait_ge(pack_out[r // PACK], ring_count(t, r, base - RING, 16))
                    dve.tensor_tensor(rows_out[:, r, :], ps[:, 4 + r % 2, 0:D],
                                      bias2[:, bass.ds(expert_of(dve, t), 1), :].squeeze(1), ALU.add).then_inc(q["out_ready"], 1)

            tiles(dve, emit, layer, -2)

        def all_results(pool, layer):
            for signal in pack_out:
                pool.wait_ge(signal, 16 * sum(NE[:layer + 1]) // RING)

        def gather(pool, layer, dst, index, signal):
            pool.indirect_dma_start(out=dst, out_offset=None, in_=d[f"results{layer}"],
                                    in_offset=bass.IndirectOffsetOnAxis(ap=index, axis=0)).then_inc(signal, 16)

        def last_gpsimd(pool):
            all_results(pool, 1)
            for g in range(G):
                for t in range(g * T, (g + 1) * T):
                    gather(pool, 1, got_all[:, t, :], result_slot[:, 0, t:t + 1], rows_at[g])

        def last_vector(dve):
            for g in range(G):
                dve.wait_ge(rows_at[g], 16 * (sum(NE) // RING + T))
                for t in range(g * T, (g + 1) * T):
                    last = dve.scalar_tensor_tensor(out=h_tok[:, t, :], in0=got_all[:, t, :],
                                                    scalar=weight[:, 0, t:t + 1], in1=h_tok[:, t, :],
                                                    op0=ALU.mult, op1=ALU.add)
                last.then_inc(s_last, 1)

        def last_sync(sp):
            for g in range(G):
                sp.wait_ge(s_last, g + 1)
                sp.dma_start(d["out"][:, g * T:(g + 1) * T, :], h_tok[:, g * T:(g + 1) * T, :]).then_inc(s_out, 16)
            sp.wait_ge(s_out, 16 * G)

        JOBS = ("gr", "f0", "f1", "g2", "t0", "t1", "k0", "k1", "q0", "q1", "v0", "v1", "g0", "g1")
        JOB_SLOT = {"f": 1, "g2": 2, "t": 3, "k": 4, "gr": 0, "q": 5, "v": 6, "g": 7}

        KEYS = {5: ((0, 0, 5),), 6: ((0, 5, H), (1, 0, 2)), 7: ((1, 2, H),)}

        SETTLE_AT = {1: (0, 1), 2: (2,), 3: (3,), 4: (4,)}

        def job_slot(j):
            return JOB_SLOT[j if j in ("g2", "gr") else j[0]]
        at_ = {n: sem("at_" + n) for n in
               ("stats_ready mean_ready spread_ready rstd_ready norm_ready keysM_ready scores_mm peak_ready "
                "diff_ready prob_ready turn_mm probT_ready av_mm rden_ready o_ready o_turned outT_ready "
                "last_turned last_kept combined index_ready pool_ready y_ready y2_ready ones_ready t_ready t_kept").split()}
        at_["full"] = {j: sem(f"full_{j}") for j in JOBS if j != "gr"}
        at_["empty"] = {j: sem(f"empty_{j}") for j in JOBS if j != "gr"}
        at_["tiles"] = norm_tiles[0]
        fin = {n: sem("fin_" + n) for n in ("stats_ready", "mean_ready", "spread_ready", "rstd_ready")}
        fin["tiles"] = norm_tiles[1]

        def job_group(i, j):
            return i + 1 if j[0] in "tkqv" else i - {"g2": 2, "gr": 3}.get(j, 1)

        def job_list(i, layer):
            return [j for j in JOBS if (layer or j[0] != "g") and has(job_group(i, j), 0, G)]

        def job_bank(j):
            return 5 if j[1] == "1" else 7

        def job_before(i, j, layer):
            def same_bank(i):
                return [k for k in job_list(i, layer) if job_bank(k) == job_bank(j)]

            here = same_bank(i)
            at = here.index(j)
            if at:
                return here[at - 1], job_group(i, here[at - 1])
            if isinstance(i, int):
                if i < 0:
                    return None
                prev = same_bank(i - 1)
            else:
                prev = same_bank(i)
            return (prev[-1], job_group(i - 1, prev[-1])) if prev else None

        AT_FIRST, AT_INNER, AT_LAST = ((-1, 2), (-1, 3)), 4, (G + 1, G + 3)

        def img(i, m, r):
            n = GI * i + (m + r)
            return (not isinstance(i, int) or 0 <= n < B), n

        def got_count(g, gp):
            per = 16 * 2 * T
            return per * (g // 2 + 1) if isinstance(g, int) else (g - gp) * (per // 2) + per

        def turned(h, n=1):
            return ps[0:S, 4, h * S:(h + n) * S] if h < H - 1 else ps[0:S, 6, 384:384 + S]

        def attention_tensor(pe, layer):
            q = at_
            L, N0 = G * layer, B * layer
            M = M_ATT + 4 * layer

            def take(i, j):
                before = job_before(i, j, layer)
                if before and before[0] == "gr":
                    pe.wait_ge(rs[1]["settled"], SETTLE * before[1] + 2)
                elif before:
                    pe.wait_ge(q["empty"][before[0]], before[1] + (1 + (L if before[0][0] != "g" else 0)))

            def job(i, j, par):
                g = job_group(i, j)
                gp = 1 - par
                take(i, j)
                if j == "gr":
                    rank(pe, 1, g, job_bank(j))
                    return
                h = int(j[1])
                half = slice(h * HALF, (h + 1) * HALF)
                tiles = range(4) if h == 0 else range(4, 5)
                if j[0] == "f":
                    if h == 0:
                        pe.wait_ge(q["outT_ready"], GI * (g + (L + 1)))
                    for t in tiles:
                        last = pe.matmul(ps[0:TP, job_bank(j), t % 4 * D:(t % 4 + 1) * D], outT[:, gp, t * TP:(t + 1) * TP],
                                         mats[:, M + 3, :], start=True, stop=True)
                elif j[0] in "tg" and j != "g2":
                    if h == 0:
                        pe.wait_ge(*((q["norm_ready"], g + (L + 1)) if j[0] == "t" else (q["t_ready"], g + 1)))
                    src = xn[:, gp] if j[0] == "t" else xf[:, :, :]
                    for t in tiles:
                        last = pe.transpose(ps[:, job_bank(j), t % 4 * TP:(t % 4 + 1) * TP], src[:, t, :], ident[0:TP, 0:TP])
                elif j[0] in "kq":
                    if j == "k0":
                        pe.wait_ge(q["empty"]["t1"], g + (L + 1))
                    last = pe.matmul(ps[:, job_bank(j), 0:HALF], mats[:, M + (j[0] == "k"), :], xT[:, half], start=True, stop=True)
                elif j[0] == "v":
                    for a in range(GI // 2):
                        b = h * (GI // 2) + a
                        last = pe.matmul(ps[0:S, job_bank(j), a * D:(a + 1) * D], xT[:, b * S:(b + 1) * S], mats[:, M + 2, :],
                                         start=True, stop=True)
                else:
                    pe.wait_ge(q["empty"]["g1"], g + 1)
                    for t in range(T):
                        last = pe.matmul(ps[0:TP, job_bank(j), t * E:(t + 1) * E], tT[:, t * TP:(t + 1) * TP],
                                         route_w[:, 1, :], start=True, stop=True)
                last.then_inc(q["full"][j], 1)

            def emit(i, par):
                for m in range(GI):
                    ok, n = img(i, m, 1)
                    if ok:
                        p, b = (m + 1) % 2, (m + 1) % GI
                        gp = par if m + 1 < GI else 1 - par
                        g = i if m + 1 < GI else i + 1
                        if b in (0, GI // 2):
                            pe.wait_ge(q["keysM_ready"], 2 * g + (2 * L + (1 if b == 0 else 2)))
                            pe.wait_ge(q["empty"]["q1"], g + (L + 1))
                        after(pe, q["diff_ready"], n + (N0 - 1))
                        for k in range(2):
                            bank = ps[0:S, 2 * p + k, 0:HALF]
                            if layer == 0:
                                pe.matmul(bank, identb[0:S, 0:S], maskb[:, :], start=True, stop=False)
                            last = pe.matmul(bank, qT[:, gp, b * S:(b + 1) * S],
                                             keysM[:, gp, b, 4 * k:4 * k + 4, :].rearrange("p h s -> p (h s)"),
                                             start=(layer == 1), stop=True)
                        last.then_inc(q["scores_mm"], 1)
                    ok, n = img(i, m, -1)
                    if ok:
                        p, b = (m - 1) % 2, (m - 1) % GI
                        gp = par if m else 1 - par
                        pe.wait_ge(q["probT_ready"], n + (N0 + 1))
                        pe.wait_ge(q["last_kept"], n + (N0 + 1))
                        after(pe, q["outT_ready"], n + N0)
                        for h in range(H):
                            last = pe.matmul(ps[0:S, 6, h * HA:(h + 1) * HA], probT[:, p, h, :], vals[:, gp, b, h, :],
                                             start=True, stop=True)
                        last.then_inc(q["av_mm"], 1)
                    ok, n = img(i, m, 0)
                    if ok:
                        pe.wait_ge(q["prob_ready"], n + (N0 + 1))
                        after(pe, q["probT_ready"], n + N0)
                        for h in range(H - 1):
                            last = pe.transpose(turned(h), prob[:, m % 2, h, :], ident[0:S, 0:S])
                        last.then_inc(q["turn_mm"], 1)
                    for j in job_list(i, layer):
                        if job_slot(j) == m:
                            job(i, j, par)
                    ok, n = img(i, m, -1)
                    if ok:
                        pe.wait_ge(q["o_ready"], n + (N0 + 1))
                        pe.transpose(ps[:, 6, 256:256 + S], o_tok[:, (m - 1) % 2, :], ident[0:S, 0:S])\
                          .then_inc(q["o_turned"], 1)
                    ok, n = img(i, m, 0)
                    if ok:
                        pe.transpose(turned(H - 1), prob[:, m % 2, H - 1, :], ident[0:S, 0:S])\
                          .then_inc(q["last_turned"], 1)

            steps(pe, emit, AT_FIRST[layer], AT_INNER, AT_LAST[layer])

        def attention_scalar(act, layer):
            q = at_
            L, N0 = G * layer, B * layer
            C = C_ATT + 3 * layer

            def job(i, j, par):
                g = job_group(i, j)
                gp = 1 - par
                h = int(j[1])
                half = slice(h * HALF, (h + 1) * HALF)
                tok = slice(0, 4 * TP) if h == 0 else slice(4 * TP, GT)
                nt = 4 if h == 0 else 1
                act.wait_ge(q["full"][j], g + (1 if j[0] == "g" else L + 1))
                if j[0] == "t":
                    last = act.activation(xT[:, tok], ps[:, job_bank(j), 0:nt * TP], ACT.Copy)
                elif j[0] == "k":
                    after(act, q["keysM_ready"], 2 * g + 2 * L)
                    last = act.activation(keysT[:, half], ps[:, job_bank(j), 0:HALF], ACT.Identity, bias=cols[:, C + 1:C + 2])
                elif j[0] == "q":
                    last = act.activation(qT[:, gp, half], ps[:, job_bank(j), 0:HALF], ACT.Identity, bias=cols[:, C:C + 1])
                elif j[0] == "v":
                    last = act.activation(vals[:, gp, 4 * h:4 * h + 4, :, 0:DK],
                                          ps[0:S, job_bank(j), :].rearrange("p (a h k) -> p a h k", a=4, h=H), ACT.Copy)
                else:
                    last = act.activation(tT[:, tok], ps[:, job_bank(j), 0:nt * TP], ACT.Copy)
                    if h:
                        act.activation(xf_all[:, bass.ts(g, T), :], xf[:, :, :], ACT.Copy).then_inc(q["t_kept"], 1)
                last.then_inc(q["empty"][j], 1)

            def emit(i, par):
                for m in range(GI):
                    ok, n = img(i, m, 0)
                    if ok:
                        act.wait_ge(q["turn_mm"], n + (N0 + 1))
                        act.activation(probT[:, m % 2, 0:H - 1, :].rearrange("p h s -> p (h s)"), turned(0, H - 1),
                                       ACT.Copy).then_inc(q["probT_ready"], 1)
                    ok, n = img(i, m, -1)
                    if ok:
                        gp = par if m else 1 - par
                        b = (m - 1) % GI
                        act.wait_ge(q["o_turned"], n + (N0 + 1))
                        if img(i, m, 0)[0]:
                            act.wait_ge(q["last_turned"], n + (N0 + 2))
                        act.activation(outT[:, gp, b * S:(b + 1) * S], ps[:, 6, 256:256 + S], ACT.Identity,
                                       bias=cols[:, C + 2:C + 3]).then_inc(q["outT_ready"], 1)
                    ok, n = img(i, m, 0)
                    if ok:
                        act.wait_ge(q["last_turned"], n + (N0 + 1))
                        act.activation(probT[:, m % 2, H - 1, :], turned(H - 1), ACT.Copy).then_inc(q["last_kept"], 1)
                    ok, n = img(i, m, 1)
                    if ok:
                        p = (m + 1) % 2
                        act.wait_ge(q["diff_ready"], n + (N0 + 1))
                        act.activation(prob[:, p, :, :], diff[:, p, :, :], ACT.Exp, scale=DK ** -0.5)\
                           .then_inc(q["prob_ready"], 1)
                    for j in job_list(i, layer):
                        if job_slot(j) == m and j[0] in "tkqvg" and j not in ("g2", "gr"):
                            job(i, j, par)

            steps(act, emit, AT_FIRST[layer], AT_INNER, AT_LAST[layer])

        def attention_vector(dve, layer):
            q = at_
            L, N0 = G * layer, B * layer

            def combine(g, gp, k):
                dve.wait_ge(got_in[gp], got_count(g, gp))
                after(dve, q["combined"], 2 * g + k)
                for t in range(T):
                    ht = h_tok[:, bass.ds(g * T + t, 1), :].squeeze(1)
                    last = dve.scalar_tensor_tensor(out=ht, in0=got[:, gp, k, t, :],
                                                    scalar=weight[:, k, bass.ds(g * T + t, 1)], in1=ht,
                                                    op0=ALU.mult, op1=ALU.add)
                last.then_inc(q["combined"], 1)

            def route_between(i, m):
                if m == 3 and has(i - 2, 0, G):
                    stand(dve, q["empty"]["g2"], i - 1)
                if m >= 3 and has(i - 2, 0, G):
                    choose(dve, 1, i - 2, m - 3)
                if m == 0 and has(i - 3, 0, G):
                    choose(dve, 1, i - 3, GI - 3)
                if m in SETTLE_AT and has(i - 3, 0, G):
                    for k in SETTLE_AT[m]:
                        settle(dve, 1, i - 3, job_bank("gr"), k)

            def emit(i, par):
                nxt, prv = has(i + 1, 0, G), has(i - 1, 0, G)
                gp = 1 - par
                for m in range(GI):
                    ok, n = img(i, m, 1)
                    if ok:
                        p = (m + 1) % 2
                        banks = ps[0:S, 2 * p:2 * p + 2, 0:HALF].rearrange("p a (h s) -> p a h s", s=S)
                        dve.wait_ge(q["scores_mm"], n + (N0 + 1))
                        dve.tensor_reduce(peak[:, p, :].rearrange("p (a h) -> p a h", a=2), banks, AX.X, ALU.max)\
                           .then_inc(q["peak_ready"], 1)
                    ok, n = img(i, m, -1)
                    if ok:
                        av = ps[0:S, 6, 0:H * HA].rearrange("p (h a) -> p h a", a=HA)
                        dve.wait_ge(q["av_mm"], n + (N0 + 1))
                        dve.reciprocal(rden[:, :], av[:, :, DK]).then_inc(q["rden_ready"], 1)
                    if layer == 1:
                        route_between(i, m)
                    if ok:
                        dve.wait_ge(q["rden_ready"], n + (N0 + 1))
                        after(dve, q["o_turned"], n + (N0 - 1))
                        dve.tensor_tensor(o_tok[:, (m - 1) % 2, :].rearrange("p (h k) -> p h k", h=H), av[:, :, 0:DK],
                                          rden[:, :].unsqueeze(2).broadcast_to([S, H, DK]), ALU.mult)\
                           .then_inc(q["o_ready"], 1)
                    ok, n = img(i, m, 1)
                    if ok:
                        dve.wait_ge(q["peak_ready"], n + (N0 + 1))
                        after(dve, q["prob_ready"], n + (N0 - 1))
                        dve.tensor_tensor(diff[:, p, :, :].rearrange("p (a h) s -> p a h s", a=2), banks,
                                          peak[:, p, :].rearrange("p (a h) -> p a h", a=2).unsqueeze(3)
                                          .broadcast_to([S, 2, 4, S]), ALU.subtract).then_inc(q["diff_ready"], 1)
                    if m == 0 and nxt:
                        if layer == 0:
                            stand(dve, q["combined"], 2 * i + 4)
                        norm_sums(dve, q, h_tok[:, bass.ts(i + 1, T), :])
                    if m == 1 and nxt:
                        norm_means(dve, q, i + (L + 2))
                    if m == 2 and nxt:
                        g = i + 1
                        if layer == 1:
                            after(dve, q["pool_ready"], g + (L - 1))
                        after(dve, q["full"]["t1"], g + (L - 1))
                        norm_apply(dve, q, xn[:, gp], h_tok[:, bass.ts(g, T), :], g + (L + 1)).then_inc(q["norm_ready"], 1)
                    if m == 1 and prv:
                        g = i - 1
                        dve.wait_ge(q["pool_ready"], g + (L + 1))
                        if layer == 1:
                            after(dve, q["t_ready"], g)
                        for h, (a, b) in enumerate(((0, 4), (4, 5))):
                            dve.wait_ge(q["full"][f"f{h}"], g + (L + 1))
                            dst = h_tok[:, bass.ds(g * T + a, b - a), :] if layer == 0 else y[:, a:b, :]
                            bank = ps[0:TP, job_bank(f"f{h}"), 0:(b - a) * D].rearrange("p (t d) -> p t d", d=D)
                            dve.tensor_tensor(dst, bank, hb[:, a:b, :], ALU.add).then_inc(q["empty"][f"f{h}"], 1)
                    if m == 3 and prv and layer == 1:
                        g = i - 1
                        dve.wait_ge(q["empty"]["f1"], g + (L + 1))
                        norm_stats(dve, fin, y, g + 1)
                    if m == 4 and prv and layer == 1:
                        g = i - 1
                        after(dve, q["full"]["g1"], g)
                        after(dve, q["t_kept"], g)
                        norm_apply(dve, fin, xf, y, g + 1).then_inc(q["y_ready"], 1)
                    if nxt:
                        g = i + 1
                        for h, a, b in KEYS.get(m, ()):
                            if a == 0:
                                dve.wait_ge(q["empty"][f"k{h}"], g + (L + 1))
                                after(dve, q["scores_mm"], GI * (g + (L - 1)))
                            for hd in range(a, b):
                                last = dve.tensor_scalar(
                                    keysM[:, gp, 4 * h:4 * h + 4, hd, :],
                                    keysT[:, h * HALF:(h + 1) * HALF].rearrange("p (a s) -> p a s", s=S),
                                    cols[:, C_HEAD + hd:C_HEAD + hd + 1], None, ALU.mult)
                            if b == H:
                                last.then_inc(q["keysM_ready"], 1)
                    if m in (3, 4) and layer == 0 and has(i + 2, 0, G):
                        combine(i + 2, par, m - 3)
                    if m == 2 and has(i - 2, 0, G) and layer == 1:
                        g = i - 2
                        dve.wait_ge(q["full"]["g2"], g + 1)
                        dve.tensor_tensor(logits[:, bass.ts(g, T), :],
                                          ps[0:TP, 7, 0:T * E].rearrange("p (t e) -> p t e", e=E),
                                          route_b[:, 1:2, :].broadcast_to([TP, T, E]), ALU.add)\
                           .then_inc(q["empty"]["g2"], 1)

            if layer == 0:
                combine(0, 0, 0)
                combine(0, 0, 1)
            dve.memset(vals[:, :, :, :, DK:HA].rearrange("p a b h k -> p (a b h) k"), 1.0).then_inc(q["ones_ready"], 1)
            dve.wait_ge(q["ones_ready"], layer + 1)
            steps(dve, emit, AT_FIRST[layer], AT_INNER, AT_LAST[layer])

        def attention_gpsimd(pool, layer):
            q = at_
            L, N0 = G * layer, B * layer

            def fetch_results(g, gp):
                after(pool, q["combined"], 2 * g - 2)
                pool.tensor_copy(slot_now[:, gp, :, :], result_slot[:, :, bass.ds(g * T, T)]).then_inc(q["index_ready"], 1)
                stand(pool, q["index_ready"], g + 1)
                for k in range(2):
                    for t in range(T):
                        gather(pool, 0, got[:, gp, k, t, :], slot_now[:, gp, k, t:t + 1], got_in[gp])

            def emit(i, par):
                if layer == 0 and has(i + 2, 0, G):
                    fetch_results(i + 2, par)
                if has(i - 1, 0, G):
                    g = i - 1
                    gp = 1 - par
                    after(pool, q["empty"]["f1"], g + L)
                    src = h_tok[:, bass.ts(g, T), :] if layer == 0 else xn[:, gp]
                    row = R_BO0 + layer
                    pool.tensor_tensor(hb[:, :, :], src, rows[:, row:row + 1, :].broadcast_to([TP, T, D]),
                                       ALU.add).then_inc(q["pool_ready"], 1)
                if has(i + 1, 0, G):
                    norm_spread(pool, q, i + (L + 2))
                if has(i - 1, 0, G) and layer == 1:
                    g = i - 1
                    norm_spread(pool, fin, i)
                    pool.wait_ge(q["y_ready"], g + 1)
                    pool.tensor_tensor(y[:, :, :], xf[:, :, :], rows[:, R_G1:R_G1 + 1, :].broadcast_to([TP, T, D]),
                                       ALU.mult).then_inc(q["y2_ready"], 1)
                    pool.wait_ge(q["y2_ready"], g + 1)
                    pool.tensor_tensor(xf[:, :, :], y[:, :, :], rows[:, R_B1:R_B1 + 1, :].broadcast_to([TP, T, D]),
                                       ALU.add).then_inc(q["t_ready"], 1)

            if layer == 0:
                all_results(pool, 0)
                fetch_results(0, 0)

            if layer == 0:
                steps(pool, emit, AT_FIRST[layer], AT_INNER, AT_LAST[layer])
            else:
                for i in range(-1, G + 3):
                    emit(i, i % 2)
                    if has(i - 3, 0, G):
                        pool.wait_ge(q["t_kept"], i - 2)
                        scatter(pool, 1, i - 3, 0)

        def barrier(eng, number):
            eng.drain().then_inc(phase_done, 1)
            eng.wait_ge(phase_done, 5 * number)

        block = ctx.enter_context(nc.Block())

        @block.sync
        def _(sp):
            p1_sync(sp)
            sp.dma_start(down_w[:, :, 0:UNITS[0], :], d["down0"]).then_inc(s_experts, 16)
            sp.dma_start(bias2[:, :, :], d["bias2_0"]).then_inc(s_experts, 16)
            barrier(sp, 1)
            experts_sync(sp, 0)
            barrier(sp, 2)
            sp.dma_start(down_w[:, :, :, :], d["down1"]).then_inc(s_experts, 16)
            sp.dma_start(bias2[:, :, :], d["bias2_1"]).then_inc(s_experts, 16)
            barrier(sp, 3)
            barrier(sp, 4)
            experts_sync(sp, 1)
            last_sync(sp)

        @block.tensor
        def _(pe):
            pe.wait_ge(s_patch_w, 32)
            pe.wait_ge(s_made, 6)
            p1_tensor(pe)
            barrier(pe, 1)
            pe.wait_ge(s_tiles, 1)
            pe.wait_ge(s_experts, 32)
            experts_tensor(pe, 0)
            barrier(pe, 2)
            attention_tensor(pe, 0)
            barrier(pe, 3)
            attention_tensor(pe, 1)
            barrier(pe, 4)
            pe.wait_ge(s_tiles, 2)
            pe.wait_ge(s_experts, 64)
            experts_tensor(pe, 1)

        @block.scalar
        def _(act):
            act.dma_start(wp[:, 0:KF, :], d["wp"]).then_inc(s_patch_w, 16)
            act.dma_start(wp[0:KR, KF, :], d["wpr"]).then_inc(s_patch_w, 16)
            for dst, src in loads:
                act.dma_start(dst, src).then_inc(s_in, 16)
            act.wait_ge(s_in, 16 * len(loads))
            p1_scalar(act)
            route_scalar(act, 0)
            write_tails(act, 0)
            barrier(act, 1)
            experts_scalar(act, 0)
            barrier(act, 2)
            attention_scalar(act, 0)
            barrier(act, 3)
            attention_scalar(act, 1)
            route_scalar(act, 1)
            write_tails(act, 1)
            barrier(act, 4)
            experts_scalar(act, 1)

        @block.vector
        def _(dve):
            p1_vector(dve)
            route_vector(dve, 0)
            barrier(dve, 1)
            dve.wait_ge(s_experts, 32)
            experts_vector(dve, 0)
            barrier(dve, 2)
            attention_vector(dve, 0)
            barrier(dve, 3)
            dve.tensor_copy(next_row[:, :], regions[:, :]).then_inc(s_regions, 1)
            dve.wait_ge(s_regions, 1)
            attention_vector(dve, 1)
            route_vector(dve, 1)
            barrier(dve, 4)
            dve.wait_ge(s_experts, 64)
            experts_vector(dve, 1)
            last_vector(dve)

        @block.gpsimd
        def _(pool):
            pool.memset(zeros[:, :], 0.0).then_inc(s_zero, 1)
            pool.memset(ident[:, :], 0.0).then_inc(s_made, 1)
            pool.memset(ones[:, :], 1.0).then_inc(s_made, 1)
            pool.memset(halves[:, :], -0.5).then_inc(s_made, 1)
            pool.wait_ge(s_made, 3)
            pool.affine_select(out=ident[:, :], in_=ident[:, :], compare_op=ALU.not_equal, fill=1.0, base=0,
                               pattern=[[-1, 128]], channel_multiplier=1).then_inc(s_made, 1)
            pool.affine_select(out=later[:, :], in_=ones[:, :], compare_op=ALU.is_gt, fill=0.0, base=0,
                               pattern=[[1, TP]], channel_multiplier=-1).then_inc(s_made, 1)
            pool.wait_ge(s_made, 5)
            pool.tensor_copy(identb[:, :], ident[:, :]).then_inc(s_made, 1)
            pool.wait_ge(s_in, 16 * len(loads))
            p1_gpsimd(pool)
            barrier(pool, 1)
            experts_gpsimd(pool, 0)
            barrier(pool, 2)
            attention_gpsimd(pool, 0)
            barrier(pool, 3)
            attention_gpsimd(pool, 1)
            barrier(pool, 4)
            experts_gpsimd(pool, 1)
            last_gpsimd(pool)


def kernel(**inputs):
    import numpy as np
    import concourse.bacc as bacc
    from concourse.bass_utils import run_bass_kernel_spmd

    f = {k: np.asarray(v) for k, v in inputs.items()}
    P = f["x"].shape[2] // 8
    x = f["x"].reshape(G, GI, 3, 8, P, 8, P).transpose(0, 2, 4, 6, 1, 3, 5).reshape(G, KF * 128 + KR, GI * NP)
    w = f["L0_tok_W"].T

    def parts(a, n):
        return a.reshape(*a.shape[:-2], n, 128, a.shape[-1]).swapaxes(-3, -2)

    def with_bias(w, b):
        return np.concatenate([w, b.reshape(E, 4, 128).transpose(0, 2, 1)], 2)

    heads = np.zeros((D, H), np.float32)
    for h in range(H):
        heads[h * DK:(h + 1) * DK, h] = 1.0
    cols = np.concatenate([np.stack([
        f["L0_tok_b"], f["L0_tok_class_token"][0], f["L0_attn_b_in"][:D], f["L0_attn_b_in"][D:], f["L0_attn_B"],
        f["L0_attn_A"], f["L1_attn_b_Q"], f["L1_attn_b_K"], f["L1_attn_b_V"], f["L1_ffn_bq"], f["L1_ffn_bk"],
        f["L1_ffn_bv"]], 1), heads], 1)
    rows = np.stack([f["L0_attn_b_out"], f["L0_attn_gamma"], f["L0_attn_beta"], f["L1_attn_b_O"], f["L1_ffn_bo"],
                     f["L1_ffn_ln1_g"], f["L1_ffn_ln1_b"]])
    win = f["L0_attn_W_in"].T
    mats = np.stack([win[:, :D], win[:, D:], f["L0_attn_W_out"].T]
                    + [f["L1_attn_W_" + n] for n in "QKVO"] + [f["L1_ffn_W" + n] for n in "qkvo"], 1)
    i, j = np.arange(S)[:, None], np.arange(S)[None, :]
    gap = i - j
    seen = (gap == 0) | (gap >= 1) & (gap <= S // 2) | (gap > 0) & (gap & gap - 1 == 0)
    mask = np.tile(np.where(seen, 0.0, -1e30).astype(np.float32), (1, 4))
    arrays = {
        "xa": parts(x[:, :KF * 128], KF),
        "xr": x[:, KF * 128:],
        "wp": parts(w[:KF * 128], KF),
        "wpr": w[KF * 128:],
        "cols": cols,
        "posT": f["L0_tok_pos_embed"].T,
        "mats": mats,
        "rows": np.broadcast_to(rows, (TP, NROW, D)),
        "route_w": np.stack([f["L0_ffn_router_w"].T, f["L1_ffn_gate_W"]], 1),
        "route_b": np.broadcast_to(np.stack([f["L0_ffn_router_b"], f["L1_ffn_gate_b"]]), (TP, 2, E)),
        "bias2_0": np.broadcast_to(f["L0_ffn_fc2_b"], (128, E, D)),
        "bias2_1": np.broadcast_to(f["L1_ffn_b2"], (128, E, D)),
        "tile_no": np.arange(max(NE), dtype=np.float32)[None],
        "mask": mask,
        "regions": np.broadcast_to(CAP * np.arange(E, dtype=np.float32), (TP, E)),
        "ids": np.broadcast_to(np.arange(E, dtype=np.float32), (TP, E)),
        "up0": with_bias(f["L0_ffn_fc1_w"].transpose(0, 2, 1), f["L0_ffn_fc1_b"]),
        "up1": with_bias(f["L1_ffn_W1"], f["L1_ffn_b1"]),
        "down0": parts(f["L0_ffn_fc2_w"].transpose(0, 2, 1), 2).transpose(1, 0, 2, 3),
        "down1": parts(f["L1_ffn_W2"], 4).transpose(1, 0, 2, 3),
    }
    nc = bacc.Bacc("TRN2", target_bir_lowering=False, num_devices=1)
    d = {}
    for name, a in arrays.items():
        arrays[name] = a = np.ascontiguousarray(a)
        d[name] = nc.dram_tensor("in_" + name, a.shape, mybir.dt.from_np(a.dtype), kind="ExternalInput").ap()
    d["slots"] = nc.dram_tensor("slots", (E * CAP, D), F32, kind="Internal").ap()
    for k in range(2):
        d[f"results{k}"] = nc.dram_tensor(f"results{k}", (NE[k] * ET, D), F32, kind="Internal").ap()
    d["out"] = nc.dram_tensor("stored_out", (B * S, D), F32, kind="ExternalOutput").ap().rearrange("(t p) d -> p t d", p=TP)
    build_program(nc, d)
    got = run_bass_kernel_spmd(nc, [{"in_" + k: a for k, a in arrays.items()}], core_ids=[0]).results[0]["stored_out"]
    return got.reshape(B, S, D)
```
